# Optimizing a Trainium2 kernel written in Bass

```python
import numpy as np
import jax
import jax.numpy as jnp

def _softmax(x, axis=-1):
    return jax.nn.softmax(x, axis=axis)

def _gelu(x):
    return jax.nn.gelu(x, approximate=True)

def _silu(x):
    return jax.nn.silu(x)

def _sigmoid(x):
    return jax.nn.sigmoid(x)

def _layernorm(x, axis=-1, eps=1e-05):
    m = jnp.mean(x, axis=axis, keepdims=True)
    v = jnp.var(x, axis=axis, keepdims=True)
    return (x - m) / jnp.sqrt(v + eps)

def _scatter_add(tgt, idx, src, axis=0):
    return tgt.at[idx].add(src)

def _segment_sum(src, seg, n):
    return jax.ops.segment_sum(src, seg, n)
kernel_name = 'mk_gnn_preln_d4_gnn_r8_97339c'

def setup_inputs(seed: int=0):
    np.random.seed(seed)
    _w = jnp.asarray

    def _rec_inputs():
        import jax
        import jax.numpy as jnp
        _gk = jax.random.key(seed)
        x = -0.000202 + 1 * jax.random.normal(jax.random.fold_in(_gk, 1), (6250, 128), jnp.float32)
        _s = jax.random.randint(jax.random.fold_in(_gk, 2), (50000,), 0, 6250, jnp.int32)
        _d = jax.random.randint(jax.random.fold_in(_gk, 3), (50000,), 0, 6250, jnp.int32)
        _loop = jnp.arange(6250, dtype=jnp.int32)
        src = jnp.concatenate([_s, _d, _loop])
        dst = jnp.concatenate([_d, _s, _loop])
        _o = jnp.argsort(dst, stable=True)
        src = src[_o]
        dst = dst[_o]
        edge_attr_4 = 0.000735704 + 1.0001 * jax.random.normal(jax.random.fold_in(_gk, 11), (106250, 4), jnp.float32)
        return (x, src, dst, edge_attr_4)
    x, src, dst, edge_attr_4 = _rec_inputs()

    def _L0_gnn_setup():
        import jax, jax.numpy as jnp
        import numpy as np
        N_NODES = 6250
        N_EDGES = 62500
        D_FEAT = 128
        key = jax.random.key(seed)
        k1, k2 = jax.random.split(key)
        x = jax.random.normal(k1, (N_NODES, D_FEAT), dtype=jnp.float32)
        edge_index = jax.random.randint(k2, (2, N_EDGES), 0, N_NODES, dtype=jnp.int64)
        return {'x': x, 'edge_index': edge_index}
    _L0_gnn_all = _L0_gnn_setup()
    _L0_gnn_in = {k: v for k, v in _L0_gnn_all.items() if k in ()}
    del _L0_gnn_all

    def _L1_gnn_setup():
        import jax, jax.numpy as jnp
        import numpy as np
        N = 5000
        E = 80000
        IN_DIM = 128
        HID_DIM = 128
        OUT_DIM = 128
        HEADS = 8
        DH1 = HID_DIM // HEADS
        DH2 = OUT_DIM // HEADS
        NEG_SLOPE = 0.2
        LN_EPS = 1e-05

        def gatv2_layer(x, Wl, Wr, att, bias, src, dst, heads, dh):
            n = x.shape[0]
            xl = (x @ Wl).reshape(n, heads, dh)
            xr = (x @ Wr).reshape(n, heads, dh)
            m = xl[src] + xr[dst]
            e = jnp.einsum('ehd,hd->eh', jax.nn.leaky_relu(m, NEG_SLOPE), att)
            emax = jax.ops.segment_max(e, dst, num_segments=n)
            ex = jnp.exp(e - emax[dst])
            denom = jax.ops.segment_sum(ex, dst, num_segments=n)
            alpha = ex / denom[dst]
            out = jax.ops.segment_sum(alpha[..., None] * xl[src], dst, num_segments=n)
            return out.reshape(n, heads * dh) + bias

        def layer_norm(x, g, b):
            mu = jnp.mean(x, axis=-1, keepdims=True)
            var = jnp.mean((x - mu) ** 2, axis=-1, keepdims=True)
            return (x - mu) * jax.lax.rsqrt(var + LN_EPS) * g + b
        key = jax.random.key(seed)
        ks = jax.random.split(key, 12)
        s1 = 1.0 / np.sqrt(IN_DIM)
        s2 = 1.0 / np.sqrt(HID_DIM)
        return {'x': jax.random.normal(ks[0], (N, IN_DIM), jnp.float32), 'edge_idx': jax.random.randint(ks[1], (2, E), 0, N), 'Wl1': jax.random.normal(ks[2], (IN_DIM, HEADS * DH1), jnp.float32) * s1, 'Wr1': jax.random.normal(ks[3], (IN_DIM, HEADS * DH1), jnp.float32) * s1, 'att1': jax.random.normal(ks[4], (HEADS, DH1), jnp.float32) * s2, 'b1': jnp.zeros((HEADS * DH1,), jnp.float32), 'g1': jnp.ones((HID_DIM,), jnp.float32), 'be1': jnp.zeros((HID_DIM,), jnp.float32), 'Wl2': jax.random.normal(ks[5], (HID_DIM, HEADS * DH2), jnp.float32) * s2, 'Wr2': jax.random.normal(ks[6], (HID_DIM, HEADS * DH2), jnp.float32) * s2, 'att2': jax.random.normal(ks[7], (HEADS, DH2), jnp.float32) * s2, 'b2': jnp.zeros((HEADS * DH2,), jnp.float32), 'g2': jnp.ones((OUT_DIM,), jnp.float32), 'be2': jnp.zeros((OUT_DIM,), jnp.float32)}
    _L1_gnn_all = _L1_gnn_setup()
    _L1_gnn_in = {k: v for k, v in _L1_gnn_all.items() if k in ('Wl1', 'Wr1', 'att1', 'b1', 'g1', 'be1', 'Wl2', 'Wr2', 'att2', 'b2', 'g2', 'be2')}
    del _L1_gnn_all

    def _L2_gnn_setup():
        import jax, jax.numpy as jnp
        import numpy as np
        N, E, DIN, DOUT = (6250, 78125, 128, 128)

        def gcn_conv(x, W, b, src, dst, n):
            loops = jnp.arange(n, dtype=src.dtype)
            src2 = jnp.concatenate([src, loops])
            dst2 = jnp.concatenate([dst, loops])
            ones = jnp.ones(src2.shape[0], dtype=x.dtype)
            deg = jax.ops.segment_sum(ones, dst2, num_segments=n)
            dinv = jnp.where(deg > 0, jax.lax.rsqrt(deg), 0.0)
            norm = dinv[src2] * dinv[dst2]
            h = x @ W
            msgs = h[src2] * norm[:, None]
            out = jax.ops.segment_sum(msgs, dst2, num_segments=n)
            return out + b
        key = jax.random.key(seed)
        k = jax.random.split(key, 4)
        x = jax.random.normal(k[0], (N, DIN), dtype=jnp.float32)
        edge_index = jax.random.randint(k[1], (2, E), 0, N, dtype=jnp.int32)
        s = 1.0 / np.sqrt(DIN)
        W_fwd = jax.random.uniform(k[2], (DIN, DOUT), jnp.float32, -s, s)
        W_bwd = jax.random.uniform(k[3], (DIN, DOUT), jnp.float32, -s, s)
        b_fwd = jnp.zeros((DOUT,), jnp.float32)
        b_bwd = jnp.zeros((DOUT,), jnp.float32)
        return {'x': x, 'edge_index': edge_index, 'W_fwd': W_fwd, 'b_fwd': b_fwd, 'W_bwd': W_bwd, 'b_bwd': b_bwd}
    _L2_gnn_all = _L2_gnn_setup()
    _L2_gnn_in = {k: v for k, v in _L2_gnn_all.items() if k in ('W_fwd', 'b_fwd', 'W_bwd', 'b_bwd')}
    del _L2_gnn_all

    def _L3_gnn_setup():
        import jax, jax.numpy as jnp
        import numpy as np
        N_NODES = 12500
        N_EDGES = 80000
        IN_DIM = 128
        OUT_DIM = 128
        EDGE_DIM = 4
        N_GROUPS = 8
        EPS = 1e-05

        def group_norm(h, gamma, beta):
            E, C = h.shape
            hg = h.reshape(E, N_GROUPS, C // N_GROUPS)
            mean = jnp.mean(hg, axis=-1, keepdims=True)
            var = jnp.mean(jnp.square(hg - mean), axis=-1, keepdims=True)
            hg = (hg - mean) * jax.lax.rsqrt(var + EPS)
            return hg.reshape(E, C) * gamma + beta
        key = jax.random.key(seed)
        ks = jax.random.split(key, 9)
        x = jax.random.normal(ks[0], (N_NODES, IN_DIM), dtype=jnp.float32)
        edge_index = jax.random.randint(ks[1], (2, N_EDGES), 0, N_NODES, dtype=jnp.int64)
        edge_attr = jax.random.normal(ks[2], (N_EDGES, EDGE_DIM), dtype=jnp.float32)
        d_in = 2 * IN_DIM + EDGE_DIM
        W1 = jax.random.uniform(ks[3], (d_in, OUT_DIM), jnp.float32, -1, 1) / np.sqrt(d_in)
        b1 = jax.random.uniform(ks[4], (OUT_DIM,), jnp.float32, -1, 1) / np.sqrt(d_in)
        W2 = jax.random.uniform(ks[5], (OUT_DIM, OUT_DIM), jnp.float32, -1, 1) / np.sqrt(OUT_DIM)
        b2 = jax.random.uniform(ks[6], (OUT_DIM,), jnp.float32, -1, 1) / np.sqrt(OUT_DIM)
        gn_gamma = jnp.ones((OUT_DIM,), jnp.float32)
        gn_beta = jnp.zeros((OUT_DIM,), jnp.float32)
        return {'x': x, 'edge_index': edge_index, 'edge_attr': edge_attr, 'W1': W1, 'b1': b1, 'gn_gamma': gn_gamma, 'gn_beta': gn_beta, 'W2': W2, 'b2': b2}
    _L3_gnn_all = _L3_gnn_setup()
    _L3_gnn_in = {k: v for k, v in _L3_gnn_all.items() if k in ('W1', 'b1', 'gn_gamma', 'gn_beta', 'W2', 'b2')}
    del _L3_gnn_all
    return {'x': x, 'src': src, 'dst': dst, 'edge_attr_4': edge_attr_4, 'L1_gnn_Wl1': _L1_gnn_in['Wl1'], 'L1_gnn_Wr1': _L1_gnn_in['Wr1'], 'L1_gnn_att1': _L1_gnn_in['att1'], 'L1_gnn_b1': _L1_gnn_in['b1'], 'L1_gnn_g1': _L1_gnn_in['g1'], 'L1_gnn_be1': _L1_gnn_in['be1'], 'L1_gnn_Wl2': _L1_gnn_in['Wl2'], 'L1_gnn_Wr2': _L1_gnn_in['Wr2'], 'L1_gnn_att2': _L1_gnn_in['att2'], 'L1_gnn_b2': _L1_gnn_in['b2'], 'L1_gnn_g2': _L1_gnn_in['g2'], 'L1_gnn_be2': _L1_gnn_in['be2'], 'L2_gnn_W_fwd': _L2_gnn_in['W_fwd'], 'L2_gnn_b_fwd': _L2_gnn_in['b_fwd'], 'L2_gnn_W_bwd': _L2_gnn_in['W_bwd'], 'L2_gnn_b_bwd': _L2_gnn_in['b_bwd'], 'L3_gnn_W1': _L3_gnn_in['W1'], 'L3_gnn_b1': _L3_gnn_in['b1'], 'L3_gnn_gn_gamma': _L3_gnn_in['gn_gamma'], 'L3_gnn_gn_beta': _L3_gnn_in['gn_beta'], 'L3_gnn_W2': _L3_gnn_in['W2'], 'L3_gnn_b2': _L3_gnn_in['b2']}

def reference(x, src, dst, edge_attr_4, L1_gnn_Wl1, L1_gnn_Wr1, L1_gnn_att1, L1_gnn_b1, L1_gnn_g1, L1_gnn_be1, L1_gnn_Wl2, L1_gnn_Wr2, L1_gnn_att2, L1_gnn_b2, L1_gnn_g2, L1_gnn_be2, L2_gnn_W_fwd, L2_gnn_b_fwd, L2_gnn_W_bwd, L2_gnn_b_bwd, L3_gnn_W1, L3_gnn_b1, L3_gnn_gn_gamma, L3_gnn_gn_beta, L3_gnn_W2, L3_gnn_b2):
    import jax
    import jax.numpy as jnp

    def _L0_gnn_ref(x, edge_index):
        import jax, jax.numpy as jnp
        import numpy as np
        N_NODES = 6250
        N_EDGES = 62500
        D_FEAT = 128
        row, col = (edge_index[0], edge_index[1])
        messages = jnp.take(x, row, axis=0)
        out = jax.ops.segment_sum(messages, col, num_segments=x.shape[0])
        return out

    def _L1_gnn_ref(x, edge_idx, Wl1, Wr1, att1, b1, g1, be1, Wl2, Wr2, att2, b2, g2, be2):
        import jax, jax.numpy as jnp
        import numpy as np
        N = 5000
        E = 80000
        IN_DIM = 128
        HID_DIM = 128
        OUT_DIM = 128
        HEADS = 8
        DH1 = HID_DIM // HEADS
        DH2 = OUT_DIM // HEADS
        NEG_SLOPE = 0.2
        LN_EPS = 1e-05

        def gatv2_layer(x, Wl, Wr, att, bias, src, dst, heads, dh):
            n = x.shape[0]
            xl = (x @ Wl).reshape(n, heads, dh)
            xr = (x @ Wr).reshape(n, heads, dh)
            m = xl[src] + xr[dst]
            e = jnp.einsum('ehd,hd->eh', jax.nn.leaky_relu(m, NEG_SLOPE), att)
            emax = jax.ops.segment_max(e, dst, num_segments=n)
            ex = jnp.exp(e - emax[dst])
            denom = jax.ops.segment_sum(ex, dst, num_segments=n)
            alpha = ex / denom[dst]
            out = jax.ops.segment_sum(alpha[..., None] * xl[src], dst, num_segments=n)
            return out.reshape(n, heads * dh) + bias

        def layer_norm(x, g, b):
            mu = jnp.mean(x, axis=-1, keepdims=True)
            var = jnp.mean((x - mu) ** 2, axis=-1, keepdims=True)
            return (x - mu) * jax.lax.rsqrt(var + LN_EPS) * g + b
        src, dst = (edge_idx[0], edge_idx[1])
        h = gatv2_layer(x, Wl1, Wr1, att1, b1, src, dst, HEADS, DH1)
        h = layer_norm(jax.nn.relu(h), g1, be1)
        h = gatv2_layer(h, Wl2, Wr2, att2, b2, src, dst, HEADS, DH2)
        h = layer_norm(jax.nn.relu(h), g2, be2)
        return h

    def _L2_gnn_ref(x, edge_index, W_fwd, b_fwd, W_bwd, b_bwd):
        import jax, jax.numpy as jnp
        import numpy as np
        N, E, DIN, DOUT = (6250, 78125, 128, 128)

        def gcn_conv(x, W, b, src, dst, n):
            loops = jnp.arange(n, dtype=src.dtype)
            src2 = jnp.concatenate([src, loops])
            dst2 = jnp.concatenate([dst, loops])
            ones = jnp.ones(src2.shape[0], dtype=x.dtype)
            deg = jax.ops.segment_sum(ones, dst2, num_segments=n)
            dinv = jnp.where(deg > 0, jax.lax.rsqrt(deg), 0.0)
            norm = dinv[src2] * dinv[dst2]
            h = x @ W
            msgs = h[src2] * norm[:, None]
            out = jax.ops.segment_sum(msgs, dst2, num_segments=n)
            return out + b
        src, dst = (edge_index[0], edge_index[1])
        n = x.shape[0]
        x_forward = gcn_conv(x, W_fwd, b_fwd, src, dst, n)
        x_backward = gcn_conv(x, W_bwd, b_bwd, dst, src, n)
        return jax.nn.relu(x_forward + x_backward)

    def _L3_gnn_ref(x, edge_index, edge_attr, W1, b1, gn_gamma, gn_beta, W2, b2):
        import jax, jax.numpy as jnp
        import numpy as np
        N_NODES = 12500
        N_EDGES = 80000
        IN_DIM = 128
        OUT_DIM = 128
        EDGE_DIM = 4
        N_GROUPS = 8
        EPS = 1e-05

        def group_norm(h, gamma, beta):
            E, C = h.shape
            hg = h.reshape(E, N_GROUPS, C // N_GROUPS)
            mean = jnp.mean(hg, axis=-1, keepdims=True)
            var = jnp.mean(jnp.square(hg - mean), axis=-1, keepdims=True)
            hg = (hg - mean) * jax.lax.rsqrt(var + EPS)
            return hg.reshape(E, C) * gamma + beta
        src, dst = (edge_index[0], edge_index[1])
        feat = jnp.concatenate([x[dst], x[src], edge_attr], axis=-1)
        h = feat @ W1 + b1
        h = group_norm(h, gn_gamma, gn_beta)
        h = jax.nn.silu(h)
        messages = h @ W2 + b2
        out = jax.ops.segment_sum(messages, dst, num_segments=x.shape[0])
        count = jax.ops.segment_sum(jnp.ones((messages.shape[0], 1), x.dtype), dst, num_segments=x.shape[0])
        return out / jnp.maximum(count, 1.0)
    edge_index = jnp.stack([src, dst])
    h = jnp.maximum(_layernorm(x, axis=-1), 0.0)
    x = x + _L0_gnn_ref(h, edge_index)
    h = jnp.maximum(_layernorm(x, axis=-1), 0.0)
    x = x + _L1_gnn_ref(h, edge_index, L1_gnn_Wl1, L1_gnn_Wr1, L1_gnn_att1, L1_gnn_b1, L1_gnn_g1, L1_gnn_be1, L1_gnn_Wl2, L1_gnn_Wr2, L1_gnn_att2, L1_gnn_b2, L1_gnn_g2, L1_gnn_be2)
    h = jnp.maximum(_layernorm(x, axis=-1), 0.0)
    x = x + _L2_gnn_ref(h, edge_index, L2_gnn_W_fwd, L2_gnn_b_fwd, L2_gnn_W_bwd, L2_gnn_b_bwd)
    h = jnp.maximum(_layernorm(x, axis=-1), 0.0)
    x = x + _L3_gnn_ref(h, edge_index, edge_attr_4, L3_gnn_W1, L3_gnn_b1, L3_gnn_gn_gamma, L3_gnn_gn_beta, L3_gnn_W2, L3_gnn_b2)
    return x

_drawn_inputs = setup_inputs


def setup_inputs(seed=0):
    import zlib

    import numpy as np

    out = dict(_drawn_inputs(seed))
    spreads = {'L1_gnn_b1': (0.0, 0.1),
     'L1_gnn_g1': (1.0, 0.572),
     'L1_gnn_be1': (0.0, 0.462),
     'L1_gnn_b2': (0.0, 0.4),
     'L1_gnn_g2': (1.0, 0.566),
     'L1_gnn_be2': (0.0, 0.606),
     'L2_gnn_b_fwd': (0.0, 0.8),
     'L2_gnn_b_bwd': (0.0, 0.8),
     'L3_gnn_gn_gamma': (1.0, 0.6),
     'L3_gnn_gn_beta': (0.0, 0.8)}
    factors = {'edge_attr_4': 8.0,
     'L1_gnn_Wr1': 8.0,
     'L1_gnn_att1': 5.011,
     'L1_gnn_Wr2': 8.0,
     'L1_gnn_att2': 8.0,
     'L3_gnn_b1': 8.0,
     'L3_gnn_b2': 8.0}
    for name, (base, spread) in spreads.items():
        noise = np.random.default_rng([zlib.crc32(name.encode()), seed]).standard_normal(out[name].shape)
        drawn = base * np.exp(spread * noise) if base else spread * noise
        out[name] = jnp.asarray(drawn.astype(out[name].dtype))
    for name, factor in factors.items():
        out[name] = (out[name] * factor).astype(out[name].dtype)
    return out
```

```python
from contextlib import ExitStack

import concourse.bass as bass
from concourse import mybir

F32 = mybir.dt.float32
I32 = mybir.dt.int32
BF16 = mybir.dt.bfloat16
ALU = mybir.AluOpType
ACT = mybir.ActivationFunctionType
AX = mybir.AxisListType.X

P = 128
N = 6250
F = 128
E = 106250
NBLK = -(-N // P)
NPAD = NBLK * P
G = 4
GE = G * P
NG = (E + NBLK * (GE - 1)) // GE
U = 4
NCOL = 832
LASTP = E // NCOL
LASTC = E - LASTP * NCOL
NBUK = NBLK + 1
EPAD = P * NCOL + P * 5
PADT = 8191
H = 8
D = F // H
HD = D + 1
EPS = 1e-5
SLOPE = 0.2
BIG = 1e30
STEPB = float(2 ** 96)


HC = NCOL // (NG // U)
PADR = 5
VECS = ("L1_gnn_att1 L1_gnn_b1 L1_gnn_g1 L1_gnn_be1 L1_gnn_att2 L1_gnn_b2 L1_gnn_g2 L1_gnn_be2 "
        "L2_gnn_b_fwd L2_gnn_b_bwd L3_gnn_b1 L3_gnn_gn_gamma L3_gnn_gn_beta L3_gnn_b2").split()
NVEC = len(VECS)
NWEIGHT = 9 + G + NVEC
NORM_STEPS = 16
NU = NG // U
STOP = 3


class At:

    def __init__(self, turn, slot):
        self.turn, self.slot, self.g = turn, slot, turn * U + slot

    def back(self, lag):
        return At(self.turn + (self.slot - lag) // U, (self.slot - lag) % U)

    def within(self, n):
        return not isinstance(self.g, int) or 0 <= self.g < n


def ticks(eng, n, lag, tick):
    for t in range(U):
        tick(At(0, t))
    with eng.Fori(1, n // U) as turn:
        for u in range(U):
            tick(At(turn, u))
    for t in range(n // U * U, n + lag):
        tick(At(t // U, t % U))


def wait(eng, sem, value):
    if not isinstance(value, int) or value > 0:
        eng.wait_ge(sem, value)


class Chain:

    def __init__(self, eng, sem):
        self.eng, self.sem, self.done, self.turns = eng, sem, 0, None

    def __call__(self, ins):
        ins.then_inc(self.sem, 1)
        self.done += 1
        self.eng.wait_ge(self.sem, self.done if self.turns is None else self.turns + self.done)

    def enter(self, i, per):
        self.turns = i * per

    def leave(self, n, per):
        self.turns = None
        self.done += (n - 1) * per


def build(nc, a, out):
    with ExitStack() as ctx:
        def sb(name, shape, dt=F32):
            return ctx.enter_context(nc.sbuf_tensor(name, shape, dt))

        def ps(name, shape, dt=F32):
            return ctx.enter_context(nc.psum_tensor(name, shape, dt))

        def sem(name):
            return ctx.enter_context(nc.semaphore(name))

        def dram(name, shape, dt=F32):
            return nc.dram_tensor(name, shape, dt, kind="Internal").ap()

        edges_by = [dram("edges_by_dst", (EPAD, 2), I32),
                    dram("edges_by_src", (EPAD, 2), I32)]
        attr_by_dst = dram("attr_by_dst", (EPAD, 4))
        table = [dram(f"table{q}", (NPAD, F)) for q in range(6)]

        x = sb("x", [P, NBLK, F])
        h = sb("h", [P, NBLK, F])
        tab = sb("tab", [P, NBLK, F])
        xr = sb("xr", [P, NBLK, F])
        acc = sb("acc", [P, NBLK, H * HD])
        nmax = sb("nmax", [P, NBLK, H])
        rden = sb("rden", [P, NBLK, H])
        stat = sb("stat", [P, 3, NBLK])
        deg_in = sb("deg_in", [P, NBLK])
        deg_out = sb("deg_out", [P, NBLK])
        dinv = sb("dinv", [P, 2, NBLK])
        ident = sb("ident", [P, P])
        tri = sb("tri", [P, P])
        ones = sb("ones", [P, P])
        iota_n = sb("iota_n", [P, P])
        iota_g = sb("iota_g", [P, NG])
        w_pair = sb("w_pair", [P, 4, 2 * F])
        w_attr = sb("w_attr", [P, G, F])
        w_out = sb("w_out", [P, F])
        vecs = sb("vecs", [P, NVEC, F])
        edge_in = sb("edge_in", [P, NCOL, 2], I32)
        rank = sb("rank", [P, NCOL])
        spare = xr[:, :, :].rearrange("p b f -> p (b f)")
        key_i, key, lo, hot, pos, onecol = [spare[:, i * NCOL:(i + 1) * NCOL] for i in range(6)]
        key_i = key_i.bitcast(I32)
        pos_win = sb("pos_win", [P, HC], I32)
        rec_win = sb("rec_win", [P, HC, 2], I32)
        mean = sb("mean", [P, 2, G * H])
        var = sb("var", [P, 2, G * H])
        inv = sb("inv", [P, 2, G * H])
        trial = sb("trial", [P, 2, G * H])
        rcount = sb("rcount", [P, NBLK])
        cnt = sb("cnt", [P, NBUK])
        btot = sb("btot", [P, NBUK])
        bincl = sb("bincl", [P, NBUK])
        bbase = sb("bbase", [P, NG // U])
        bgrp_i = sb("bgrp_i", [P, NBUK], I32)
        bgrp = sb("bgrp", [P, NBUK])
        bend = sb("bend", [P, NBUK])
        bdelta = sb("bdelta", [P, NBUK])
        gtmp = sb("gtmp", [P, NG])
        gblk = sb("gblk", [P, NG])
        gstart = sb("gstart", [P, NG])
        gbase = [sb(f"gbase{k}", [P, NG]) for k in range(2)]
        gblk_i = [sb(f"gblk_i{k}", [P, NG], I32) for k in range(2)]
        gstart_i = [sb(f"gstart_i{k}", [P, NG], I32) for k in range(2)]
        hist_lo = sb("hist_lo", [P, HC, P], BF16)
        hist_hi = sb("hist_hi", [P, HC, NBLK], BF16)
        pad_rows = sb("pad_rows", [P, 2, PADR, 2], I32)
        pad_attr = sb("pad_attr", [P, PADR, 4])
        rec = sb("rec", [P, U, G, 2], I32)
        rows = sb("rows", [P, U, G, F + 1])
        tloc = sb("tloc", [P, U, G])
        onehot = sb("onehot", [P, U, G, P])

        hs = sb("hs", [P, U, F])
        hs_t = sb("hs_t", [P, U, F])
        gmax = sb("gmax", [P, 2, H])
        gseen = sb("gseen", [P, 2, G])
        gtile = sb("gtile", [P, 2, G, H])
        newmax = sb("newmax", [P, 2, H])
        drop = sb("drop", [P, 2, H])
        factor = sb("factor", [P, 2, H])
        shifted = sb("shifted", [P, 2, G, H])
        bank = [ps(f"bank{k}", [P, 512]) for k in range(8)]

        (consts_pool, weights_in, x_in, edges_in, edges_set, dst_copied, pads_set, pads_out, v, counts_ready,
         prefix_ready, prefix_used, groups_ready, rank_done, hist_hot, hist_mm, pos_ready, unused_sem, scattered,
         table_set, table_out, hs_ready, turned, turned_sb, mult, mult_used, tick_mark, onehot_ready, tloc_ready, agg_ready,
         acc_ready, var_ready, sqrt_ready, final_set, stored) = [sem(n) for n in (
             "consts_pool weights_in x_in edges_in edges_set dst_copied pads_set pads_out v counts_ready "
             "prefix_ready prefix_used groups_ready rank_done hist_hot hist_mm pos_ready unused_sem scattered "
             "table_set table_out hs_ready turned turned_sb mult mult_used tick_mark onehot_ready tloc_ready agg_ready "
             "acc_ready var_ready sqrt_ready final_set stored").split()]
        (keys_ready, turned_hot, turned_hot_sb, spread, sum_used, scored, score_step, score_turned, score_sb,
         seg_step, seg_turned, seg_sb, max_ready, max_step, max_spread, shift_step, factor_ready, weight_ready,
         weighted_ready, acc_step) = [sem(n) for n in (
             "keys_ready turned_hot turned_hot_sb spread sum_used scored score_step score_turned score_sb "
             "seg_step seg_turned seg_sb max_ready max_step max_spread shift_step factor_ready weight_ready "
             "weighted_ready acc_step").split()]
        (win_free, attr_set, edge_step, squared, norm_step, activated, attr_free, out_step) = [sem(n) for n in (
             "win_free attr_set edge_step squared norm_step activated attr_free out_step").split()]
        attr_in = [sem(f"attr_in{u}") for u in range(U)]
        rec_in = [sem(f"rec_in{u}") for u in range(U)]
        rows_in = [sem(f"rows_in{u}") for u in range(U)]

        block = ctx.enter_context(nc.Block())

        flat = tab[:, :, :].rearrange("p b f -> p (b f)")
        area = [0]

        def ring(*shape):
            size = 1
            for n in shape:
                size *= n
            part = flat[:, area[0]:area[0] + size]
            area[0] += size
            return part.rearrange("p (u n) -> p u n", u=shape[0])

        hot_t = ring(2, GE)
        both = ring(2, GE)
        acted = ring(2, GE)
        weighted = ring(2, G * H * HD)
        score = ring(2, G * 32)
        steps = ring(2, G * 32)
        turned_rows = ring(2, 2 * P)
        fence = ring(2, P + 2)
        running = ring(2, P)
        at_last = ring(2, P)
        last_t = ring(2, G * 32)
        assert area[0] <= NBLK * F
        area[0] = 0
        hot_t = ring(2, GE)
        centered = ring(2, GE)
        square = ring(2, GE)
        silu = ring(2, GE)
        attr = ring(U, G * 32)
        attr_t = ring(2, P)
        assert area[0] <= NBLK * F
        counts_ps, prefix_ps, hist_ps = bank[0][:, 0:NBUK], bank[1][:, 0:NBUK], bank[6][:, 0:NBLK]
        agg = bank[7][:, 0:H * HD]

        def vec(name):
            return vecs[:, VECS.index(name), :]

        def per_block(row):
            return row.unsqueeze(1).broadcast_to([P, NBLK, F])

        def per_feature(col):
            return col.unsqueeze(2).broadcast_to([P, NBLK, F])

        @block.sync
        def _(sp):
            weights = [(w_pair[:, 0, 0:F], a["L1_gnn_Wl1"]), (w_pair[:, 0, F:2 * F], a["L1_gnn_Wr1"]),
                       (w_pair[:, 1, 0:F], a["L1_gnn_Wl2"]), (w_pair[:, 1, F:2 * F], a["L1_gnn_Wr2"]),
                       (w_pair[:, 2, 0:F], a["L2_gnn_W_fwd"]), (w_pair[:, 2, F:2 * F], a["L2_gnn_W_bwd"]),
                       (w_pair[:, 3, 0:F], a["L3_gnn_W1"][F:2 * F, :]), (w_pair[:, 3, F:2 * F], a["L3_gnn_W1"][0:F, :]),
                       (w_out[:, :], a["L3_gnn_W2"])]
            weights += [(w_attr[32 * t:32 * t + 4, t, :], a["L3_gnn_W1"][2 * F:2 * F + 4, :]) for t in range(G)]
            weights += [(vecs[:, i, :], (a[name].rearrange("h d -> (h d)") if "att" in name else a[name])
                         .unsqueeze(0).broadcast_to([P, F])) for i, name in enumerate(VECS)]
            assert len(weights) == NWEIGHT
            sp.wait_ge(pads_set, 1)
            sp.dma_start(edge_in[0:LASTP, :, :], a["edges"][0:LASTP * NCOL, :].rearrange("(p c) k -> p c k", c=NCOL)
                         ).then_inc(edges_in, 16)
            sp.dma_start(edge_in[LASTP:LASTP + 1, 0:LASTC, :],
                         a["edges"][LASTP * NCOL:E, :].unsqueeze(0)).then_inc(edges_in, 16)
            sp.dma_start(x[:, 0:NBLK - 1, :], a["x"][0:(NBLK - 1) * P, :].rearrange("(b p) f -> p b f", p=P)
                         ).then_inc(x_in, 16)
            sp.dma_start(x[0:N - (NBLK - 1) * P, NBLK - 1, :], a["x"][(NBLK - 1) * P:N, :]).then_inc(x_in, 16)
            sp.dma_start(edges_by[0][0:E, :], a["edges"]).then_inc(dst_copied, 16)
            sp.dma_start(attr_by_dst[0:E, :], a["edge_attr_4"]).then_inc(dst_copied, 16)
            sp.dma_start(edges_by[0][E:E + P * PADR, :].rearrange("(p r) k -> p r k", p=P),
                         pad_rows[:, 0, :, :]).then_inc(pads_out, 16)
            sp.dma_start(edges_by[1][P * NCOL:EPAD, :].rearrange("(p r) k -> p r k", p=P),
                         pad_rows[:, 1, :, :]).then_inc(pads_out, 16)
            sp.dma_start(attr_by_dst[E:E + P * PADR, :].rearrange("(p r) k -> p r k", p=P),
                         pad_attr[:, :, :]).then_inc(pads_out, 16)
            for to, of in weights:
                sp.dma_start(to, of).then_inc(weights_in, 16)
            sp.wait_ge(dst_copied, 32)
            sp.wait_ge(pads_out, 48)

            def store_table(q, staged):
                sp.wait_ge(table_set, q + 1)
                sp.dma_start(table[q].rearrange("(b p) f -> p b f", p=P), staged).then_inc(table_out, 16)

            def edge_records(q, k, with_attr=False):
                sp.wait_ge(groups_ready, k + 1)

                def tick(at):
                    wait(sp, agg_ready, q * NG + at.g - U + 1)
                    first = sp.value_load(gstart_i[k][0:1, bass.ds(at.g, 1)], min_val=0, max_val=E)
                    sp.dma_start(rec[:, at.slot, :, :],
                                 edges_by[k][bass.ds(first, GE), :].rearrange("(p t) k -> p t k", t=G)
                                 ).then_inc(rec_in[at.slot], 16)
                    if with_attr:
                        wait(sp, attr_free, at.g - U + 1)
                        sp.dma_start(attr[:, at.slot, :].rearrange("p (t c) -> p t c", t=G)[:, :, 0:4],
                                     attr_by_dst[bass.ds(first, GE), :].rearrange("(p t) k -> p t k", t=G)
                                     ).then_inc(attr_in[at.slot], 16)
                ticks(sp, NG, 0, tick)

            store_table(0, tab[:, :, :])
            edge_records(0, 0)
            if STOP >= 1:
                for q in (1, 2):
                    store_table(q, tab[:, :, :])
                    edge_records(q, 0)
            if STOP >= 2:
                store_table(3, tab[:, :, :])
                store_table(4, xr[:, :, :])
                edge_records(3, 0)
                sp.wait_ge(scattered, 16 * NCOL)
                edge_records(4, 1)
            if STOP >= 3:
                store_table(5, tab[:, :, :])
                sp.wait_ge(attr_set, 1)
                edge_records(5, 0, True)
            if True:
                sp.wait_ge(final_set, 1)
                sp.dma_start(out[0:(NBLK - 1) * P, :].rearrange("(b p) f -> p b f", p=P), x[:, 0:NBLK - 1, :]
                             ).then_inc(stored, 16)
                sp.dma_start(out[(NBLK - 1) * P:N, :], x[0:N - (NBLK - 1) * P, NBLK - 1, :]).then_inc(stored, 16)
                sp.wait_ge(stored, 32)

        @block.gpsimd
        def _(pool):
            nc.gpsimd.iota(iota_n[:, :], [[1, P]], base=0, channel_multiplier=0,
                           allow_small_or_imprecise_dtypes=True).then_inc(consts_pool, 1)
            nc.gpsimd.iota(iota_g[:, :], [[1, NG]], base=0, channel_multiplier=0,
                           allow_small_or_imprecise_dtypes=True).then_inc(consts_pool, 1)
            nc.gpsimd.memset(ones[:, :], 1.0).then_inc(consts_pool, 1)
            pool.wait_ge(consts_pool, 3)
            nc.gpsimd.affine_select(out=ident[:, :], in_=ones[:, :], compare_op=ALU.is_equal, fill=0.0, base=0,
                                    pattern=[[-1, P]], channel_multiplier=1).then_inc(consts_pool, 1)
            nc.gpsimd.affine_select(out=tri[:, :], in_=ones[:, :], compare_op=ALU.is_gt, fill=0.0, base=0,
                                    pattern=[[1, P]], channel_multiplier=-1).then_inc(consts_pool, 1)

            def scatter_columns(at):
                if at.slot == 0:
                    wait(pool, scattered, 16 * HC * at.turn)
                    if isinstance(at.turn, int):
                        pool.wait_ge(rank_done, 4 * NU)
                    pool.sem_inc(tick_mark, 1)
                    cols = bass.ds(at.turn * HC, HC)
                    nc.gpsimd.tensor_copy(pos_win[:, :], rank[:, cols]).then_inc(win_free, 1)
                    nc.gpsimd.tensor_copy(rec_win[:, :, :], edge_in[:, cols, :]).then_inc(win_free, 1)
                    pool.wait_ge(win_free, 2 * at.turn + 2)
                    pool.sem_inc(tick_mark, 1)
                for c in range(at.slot * HC // U, (at.slot + 1) * HC // U):
                    pool.indirect_dma_start(edges_by[1], bass.IndirectOffsetOnAxis(pos_win[:, c:c + 1], 0),
                                            rec_win[:, c, :], None).then_inc(scattered, 16)

            def gathers(q, gathered_end, beside=None):
                pool.wait_ge(table_out, 16 * (q + 1))

                def tick(at):
                    turn = q * (NG // U) + at.turn
                    wait(pool, agg_ready, q * NG + at.g - U + 1)
                    pool.wait_ge(rec_in[at.slot], 16 * (turn + 1))
                    pool.sem_inc(tick_mark, 1)
                    for t in range(G):
                        pool.indirect_dma_start(
                            rows[:, at.slot, t, 0:F], None, table[q],
                            bass.IndirectOffsetOnAxis(rec[:, at.slot, t, gathered_end:gathered_end + 1], 0)
                        ).then_inc(rows_in[at.slot], 16)
                    if beside is not None:
                        beside(at)
                ticks(pool, NG, 0, tick)

            gathers(0, 0)
            if STOP >= 1:
                gathers(1, 0, scatter_columns)
                gathers(2, 0)
            if STOP >= 2:
                gathers(3, 0)
                gathers(4, 1)
            if STOP >= 3:
                gathers(5, 0)

        @block.vector
        def _(dve):
            chain = Chain(dve, v)
            chain(dve.memset(edge_in[96:P, :, 0], PADT))
            chain(dve.memset(edge_in[96:P, :, 1], 0))
            chain(dve.memset(pad_rows[:, :, :, :], 0))
            chain(dve.memset(pad_rows[:, 0, :, 1], PADT))
            chain(dve.memset(pad_rows[:, 1, :, 0], PADT))
            chain(dve.memset(pad_attr[:, :, :], 0.0))
            chain(dve.memset(w_attr[:, :, :], 0.0))
            chain(dve.memset(x[0:P, NBLK - 1, :], 0.0))
            dve.sem_inc(pads_set, 1)
            chain(dve.memset(rows[:, :, :, F:F + 1], 1.0))
            chain(dve.memset(onecol[:, :], 1.0))
            chain(dve.memset(bbase[:, :], 0.0))

            def count_buckets(end):
                chain(dve.tensor_scalar(key_i[:, :], edge_in[:, :, end], 7, None, ALU.arith_shift_right))
                chain(dve.tensor_copy(key[:, :], key_i[:, :]))
                chain(dve.tensor_scalar(key[:, :], key[:, :], float(NBLK), None, ALU.min))
                with dve.Fori(0, NBUK) as b:
                    chain.enter(b, 1)
                    chain(dve.tensor_scalar(hot[:, :], key[:, :], iota_n[:, bass.ds(b, 1)], 0.0,
                                            ALU.is_equal, ALU.add, accum_out=cnt[:, bass.ds(b, 1)]))
                chain.leave(NBUK, 1)
                dve.sem_inc(counts_ready, 1)

            def group_table(k):
                dve.wait_ge(prefix_ready, k + 1)
                chain(dve.tensor_copy(btot[:, :], counts_ps))
                if k == 0:
                    chain(dve.tensor_scalar(btot[:, 0:1], btot[:, 0:1], -float(P * NCOL - E), None, ALU.add))
                if k == 1:
                    chain(dve.tensor_tensor_scan(bincl[:, :], onecol[:, 0:NBUK], btot[:, :], 0.0, ALU.mult, ALU.add))
                    chain(dve.tensor_tensor(bincl[:, :], bincl[:, :], btot[:, :], ALU.subtract))
                    chain(dve.scalar_tensor_tensor(out=bbase[:, 0:NBUK], in0=bincl[:, :], scalar=-1.0, in1=prefix_ps,
                                                   op0=ALU.add, op1=ALU.add))
                dve.sem_inc(prefix_used, 1)
                chain(dve.tensor_scalar(bgrp_i[:, :], btot[:, :], float(GE - 1), None, ALU.add))
                chain(dve.tensor_scalar(bgrp_i[:, :], bgrp_i[:, :], GE.bit_length() - 1, None, ALU.arith_shift_right))
                chain(dve.tensor_copy(bgrp[:, :], bgrp_i[:, :]))
                chain(dve.tensor_tensor_scan(bend[:, :], onecol[:, 0:NBUK], bgrp[:, :], 0.0, ALU.mult, ALU.add))
                chain(dve.scalar_tensor_tensor(out=bdelta[:, :], in0=bgrp[:, :], scalar=-float(GE), in1=btot[:, :],
                                               op0=ALU.mult, op1=ALU.add))
                chain(dve.memset(gblk[:, :], 0.0))
                chain(dve.tensor_scalar(gstart[:, :], iota_g[:, :], float(GE), None, ALU.mult))
                with dve.Fori(0, NBLK) as b:
                    chain.enter(b, 3)
                    end_b, delta_b = bend[:, bass.ds(b, 1)], bdelta[:, bass.ds(b, 1)]
                    chain(dve.scalar_tensor_tensor(out=gblk[:, :], in0=iota_g[:, :], scalar=end_b, in1=gblk[:, :],
                                                   op0=ALU.is_ge, op1=ALU.add))
                    chain(dve.tensor_scalar(gtmp[:, :], iota_g[:, :], end_b, delta_b, ALU.is_ge, ALU.mult))
                    chain(dve.tensor_tensor(gstart[:, :], gstart[:, :], gtmp[:, :], ALU.add))
                chain.leave(NBLK, 3)
                chain(dve.tensor_scalar(gblk_i[k][:, :], gblk[:, :], float(NBLK - 1), None, ALU.min))
                chain(dve.tensor_scalar(gbase[k][:, :], gblk[:, :], float(NBLK - 1), float(P), ALU.min, ALU.mult))
                chain(dve.tensor_scalar(gstart_i[k][:, :], gstart[:, :], float(E), None, ALU.min))
                dve.sem_inc(groups_ready, 1)

            centered_count = [0]

            def center_rows(src):
                chain(dve.tensor_reduce(stat[:, 0, :], src, AX, ALU.add))
                chain(dve.tensor_scalar(stat[:, 1, :], stat[:, 0, :], 1.0 / F, None, ALU.mult))
                chain(dve.tensor_tensor(h[:, :, :], src, per_feature(stat[:, 1, :]), ALU.subtract))
                chain(dve.tensor_tensor(tab[:, :, :], h[:, :, :], h[:, :, :], ALU.mult))
                chain(dve.tensor_reduce(stat[:, 0, :], tab[:, :, :], AX, ALU.add))
                chain(dve.tensor_scalar(stat[:, 1, :], stat[:, 0, :], 1.0 / F, EPS, ALU.mult, ALU.add))
                dve.sem_inc(var_ready, 1)
                centered_count[0] += 1
                dve.wait_ge(sqrt_ready, centered_count[0])
                chain(dve.reciprocal(stat[:, 2, :], stat[:, 0, :]))

            def one_hot(q, k, at, end):
                turn = q * (NG // U) + at.turn
                dve.wait_ge(rec_in[at.slot], 16 * (turn + 1))
                wait(dve, agg_ready, q * NG + at.g - U + 1)
                dve.tensor_scalar(tloc[:, at.slot, :], rec[:, at.slot, :, end], gbase[k][:, bass.ds(at.g, 1)], None,
                                  ALU.subtract).then_inc(tloc_ready, 1)
                dve.wait_ge(tloc_ready, q * NG + at.g + 1)
                dve.tensor_tensor(onehot[:, at.slot, :, :], iota_n[:, :].unsqueeze(1).broadcast_to([P, G, P]),
                                  tloc[:, at.slot, :].unsqueeze(2).broadcast_to([P, G, P]), ALU.is_equal
                                  ).then_inc(onehot_ready, 1)

            def add_sums(q, k, at, width):
                blk = dve.value_load(gblk_i[k][0:1, bass.ds(at.g, 1)], min_val=0, max_val=NBLK - 1)
                dve.wait_ge(agg_ready, q * NG + at.g + 1)
                wait(dve, acc_ready, q * NG + at.g)
                dve.tensor_tensor(acc[:, bass.ds(blk, 1), 0:width], acc[:, bass.ds(blk, 1), 0:width],
                                  agg[:, 0:width].unsqueeze(1), ALU.add).then_inc(acc_ready, 1)

            def sum_pass(q, k, end, extra=None):
                width = F + 1

                def tick(at):
                    if at.within(NG):
                        one_hot(q, k, at, end)
                        if extra is not None and at.slot == 0:
                            extra(at.turn)
                    if at.back(1).within(NG):
                        add_sums(q, k, at.back(1), width)
                ticks(dve, NG, 1, tick)

            dve.wait_ge(consts_pool, 5)
            dve.wait_ge(edges_in, 32)
            count_buckets(1)
            dve.wait_ge(x_in, 32)
            center_rows(x[:, :, :])
            chain(dve.scalar_tensor_tensor(out=tab[:, :, :], in0=h[:, :, :], scalar=0.0,
                                           in1=per_feature(stat[:, 2, :]), op0=ALU.max, op1=ALU.mult))
            dve.sem_inc(table_set, 1)
            group_table(0)
            count_buckets(0)
            group_table(1)
            chain(dve.memset(rank[:, :], 0.0))
            chain(dve.memset(acc[:, :, :], 0.0))
            chain(dve.tensor_scalar(key_i[:, :], edge_in[:, :, 0], P - 1, None, ALU.bitwise_and))
            chain(dve.tensor_copy(lo[:, :], key_i[:, :]))

            def sort_turn(turn):
                bucket = iota_n[:, bass.ds(turn, 1)]
                if isinstance(turn, int) and turn >= NG // U:
                    return
                done = 4 * turn
                dve.tensor_scalar(hot[:, :], key[:, :], bucket, None, ALU.is_equal).then_inc(rank_done, 1)
                dve.wait_ge(rank_done, done + 1)
                dve.tensor_tensor_scan(pos[:, :], onecol[:, :], hot[:, :], bbase[:, bass.ds(turn, 1)],
                                       ALU.mult, ALU.add).then_inc(rank_done, 1)
                dve.wait_ge(rank_done, done + 2)
                dve.tensor_tensor(hot[:, :], hot[:, :], pos[:, :], ALU.mult).then_inc(rank_done, 1)
                dve.wait_ge(rank_done, done + 3)
                dve.tensor_tensor(rank[:, :], rank[:, :], hot[:, :], ALU.add).then_inc(rank_done, 1)
                dve.wait_ge(rank_done, done + 4)
                wait(dve, hist_mm, turn)
                cols = bass.ds(turn * HC, HC)
                dve.tensor_tensor(hist_lo[:, :, :], iota_n[:, :].unsqueeze(1).broadcast_to([P, HC, P]),
                                  lo[:, cols].unsqueeze(2).broadcast_to([P, HC, P]), ALU.is_equal
                                  ).then_inc(hist_hot, 1)
                dve.tensor_tensor(hist_hi[:, :, :], iota_n[:, 0:NBLK].unsqueeze(1).broadcast_to([P, HC, NBLK]),
                                  key[:, cols].unsqueeze(2).broadcast_to([P, HC, NBLK]), ALU.is_equal
                                  ).then_inc(hist_hot, 1)

            sum_pass(0, 0, 1, sort_turn)
            dve.wait_ge(acc_ready, NG)
            chain(dve.tensor_copy(deg_in[:, :], acc[:, :, F]))
            chain(dve.tensor_tensor(x[:, :, :], x[:, :, :], acc[:, :, 0:F], ALU.add))
            dve.wait_ge(hist_mm, NG // U)
            chain(dve.tensor_copy(deg_out[:, :], hist_ps))

            def project(j, prepare, finish):
                def tick(at):
                    if at.within(NBLK):
                        wait(dve, turned, j * NBLK + at.g - U + 1)
                        prepare(hs[:, at.slot, :], bass.ds(at.g, 1)).then_inc(hs_ready, 1)
                    b = at.back(2)
                    if b.within(NBLK):
                        dve.wait_ge(mult, j * NBLK + b.g + 1)
                        finish(bank[2 + b.slot % 2], bass.ds(b.g, 1)).then_inc(mult_used, 1)
                ticks(dve, NBLK, 2, tick)
                dve.wait_ge(mult_used, (j + 1) * NBLK)

            def relu_scaled(to, b):
                return dve.tensor_scalar(to, h[:, b, :], 0.0, stat[:, 2, b], ALU.max, ALU.mult)

            def as_is(to, b):
                return dve.tensor_scalar(to, h[:, b, :], 1.0, None, ALU.mult)

            def both_sides(psum, b):
                dve.tensor_scalar(tab[:, b, :], psum[:, 0:F], 1.0, None, ALU.mult)
                return dve.tensor_scalar(xr[:, b, :], psum[:, F:2 * F], 1.0, None, ALU.mult)

            def attention_pass(q, layer):
                a0 = (q - 1) * NG
                att = vec(f"L1_gnn_att{layer}")
                dve.wait_ge(table_out, 16 * (q + 1))
                chain(dve.memset(acc[:, :, :], 0.0))
                chain(dve.memset(nmax[:, :, :], -BIG))
                chain(dve.memset(score, 0.0))
                chain(dve.memset(score.rearrange("p u (t c) -> p (u t) c", c=32)[:, :, H:H + 1], 1.0))
                chain(dve.memset(steps, 0.0))
                chain(dve.memset(fence, 0.0))
                chain(dve.memset(fence[:, :, P:P + 1], -1.0))

                def tiles(part):
                    return part.rearrange("p (t c) -> p t c", t=G)

                def hots(at):
                    one_hot(q, 0, at, 1)
                    wait(dve, score_turned, a0 + at.g - 1)
                    dve.tensor_scalar(tiles(steps[:, at.slot % 2, :])[:, :, 0:H + 1],
                                      tloc[:, at.slot, :].unsqueeze(2).broadcast_to([P, G, H + 1]), STEPB, None,
                                      ALU.mult).then_inc(keys_ready, 1)

                def new_maximum(at, blk):
                    o, c = at.slot % 2, 6 * (a0 + at.g)
                    tile_max = bank[5][:, P:P + 16 * G].rearrange("p (t c) -> p t c", t=G)
                    dve.wait_ge(max_ready, a0 + at.g + 1)
                    dve.tensor_scalar(gseen[:, o, :], tile_max[:, :, H], -1.0, BIG, ALU.add, ALU.mult
                                      ).then_inc(max_step, 1)
                    dve.wait_ge(max_step, c + 1)
                    dve.tensor_tensor(gtile[:, o, :, :], tile_max[:, :, 0:H],
                                      gseen[:, o, :].unsqueeze(2).broadcast_to([P, G, H]), ALU.add
                                      ).then_inc(max_step, 1)
                    dve.wait_ge(max_step, c + 2)
                    dve.tensor_reduce(gmax[:, o, :], gtile[:, o, :, :].rearrange("p t h -> p h t"), AX, ALU.max
                                      ).then_inc(max_step, 1)
                    dve.wait_ge(max_step, c + 3)
                    wait(dve, max_spread, a0 + at.g - 1)
                    old = nmax[:, bass.ds(blk, 1), :]
                    dve.tensor_tensor(newmax[:, o:o + 1, :], old, gmax[:, o:o + 1, :], ALU.max).then_inc(max_step, 1)
                    dve.wait_ge(max_step, c + 4)
                    wait(dve, factor_ready, a0 + at.g - 1)
                    dve.tensor_tensor(drop[:, o:o + 1, :], old, newmax[:, o:o + 1, :], ALU.subtract
                                      ).then_inc(max_step, 1)
                    dve.wait_ge(max_step, c + 5)
                    dve.tensor_scalar(old, newmax[:, o:o + 1, :], 1.0, None, ALU.mult).then_inc(max_step, 1)
                    dve.wait_ge(max_step, c + 6)

                def activate(at):
                    o, c = at.slot % 2, 3 * (a0 + at.g)
                    dve.wait_ge(rows_in[at.slot], 16 * G * (q * NU + at.turn + 1))
                    dve.wait_ge(spread, a0 + at.g + 1)
                    dve.tensor_tensor(tiles(both[:, o, :]), tiles(bank[2 + o][:, :]), rows[:, at.slot, :, 0:F],
                                      ALU.add).then_inc(sum_used, 1)
                    dve.wait_ge(sum_used, a0 + at.g + 1)
                    dve.scalar_tensor_tensor(out=acted[:, o, :], in0=both[:, o, :], scalar=SLOPE, in1=both[:, o, :],
                                             op0=ALU.mult, op1=ALU.max).then_inc(score_step, 1)

                def scores(at):
                    o, c = at.slot % 2, 3 * (a0 + at.g)
                    dve.wait_ge(score_step, c + 1)
                    dve.tensor_tensor(tiles(acted[:, o, :]), tiles(acted[:, o, :]),
                                      att.unsqueeze(1).broadcast_to([P, G, F]), ALU.mult).then_inc(score_step, 1)
                    dve.wait_ge(score_step, c + 2)
                    dve.tensor_reduce(tiles(score[:, o, :])[:, :, 0:H],
                                      acted[:, o, :].rearrange("p (t h d) -> p t h d", t=G, h=H), AX, ALU.add
                                      ).then_inc(score_step, 1)

                def segment_maximum(at):
                    o, c = at.slot % 2, 3 * (a0 + at.g)
                    dve.wait_ge(score_sb, a0 + at.g + 1)
                    turned_steps, turned_score = turned_rows[:, o, 0:P], turned_rows[:, o, P:2 * P]
                    dve.tensor_tensor(fence[:, o, 1:P], turned_steps[:, 0:P - 1], turned_steps[:, 1:P],
                                      ALU.subtract).then_inc(seg_step, 1)
                    dve.wait_ge(seg_step, c + 1)
                    dve.tensor_tensor_scan(running[:, o, :], fence[:, o, 0:P], turned_score, -BIG, ALU.add, ALU.max
                                           ).then_inc(seg_step, 1)
                    dve.wait_ge(seg_step, c + 2)
                    wait(dve, seg_turned, a0 + at.g - 1)
                    dve.scalar_tensor_tensor(out=at_last[:, o, :], in0=fence[:, o, 1:P + 1], scalar=0.0,
                                             in1=running[:, o, :], op0=ALU.not_equal, op1=ALU.mult
                                             ).then_inc(seg_step, 1)

                def shift(at):
                    o, c = at.slot % 2, 2 * (a0 + at.g)
                    dve.wait_ge(max_spread, a0 + at.g + 1)
                    wait(dve, weight_ready, a0 + at.g - 1)
                    dve.tensor_tensor(shifted[:, o, :, :], tiles(score[:, o, :])[:, :, 0:H],
                                      bank[6][:, 0:G * H].rearrange("p (t h) -> p t h", t=G), ALU.subtract
                                      ).then_inc(shift_step, 1)
                    dve.wait_ge(shift_step, c + 1)
                    dve.tensor_scalar(shifted[:, o, :, :], shifted[:, o, :, :], 0.0, None, ALU.min
                                      ).then_inc(shift_step, 1)

                def weigh(at):
                    o = at.slot % 2
                    dve.wait_ge(weight_ready, a0 + at.g + 1)
                    w = weighted[:, o, :].rearrange("p (t h d) -> p t h d", t=G, h=H)
                    dve.tensor_tensor(w[:, :, :, 0:D],
                                      rows[:, at.slot, :, 0:F].rearrange("p t (h d) -> p t h d", h=H),
                                      w[:, :, :, D:HD].broadcast_to([P, G, H, D]), ALU.mult
                                      ).then_inc(weighted_ready, 1)

                def accumulate(at, blk):
                    o = at.slot % 2
                    dve.wait_ge(factor_ready, a0 + at.g + 1)
                    wait(dve, acc_ready, q * NG + at.g)
                    sums = acc[:, bass.ds(blk, 1), :].rearrange("p b (h d) -> p (b h) d", h=H)
                    dve.tensor_tensor(sums, sums, factor[:, o, :].unsqueeze(2).broadcast_to([P, H, HD]), ALU.mult
                                      ).then_inc(acc_step, 1)
                    dve.wait_ge(acc_step, a0 + at.g + 1)
                    dve.wait_ge(agg_ready, q * NG + at.g + 1)
                    dve.tensor_tensor(sums, sums, agg.rearrange("p (h d) -> p h d", h=H), ALU.add
                                      ).then_inc(acc_ready, 1)

                def tick(at):
                    b, c = at.back(1), at.back(2)
                    if at.within(NG):
                        hots(at)
                    if c.within(NG):
                        blk = dve.value_load(gblk_i[0][0:1, bass.ds(c.g, 1)], min_val=0, max_val=NBLK - 1)
                        new_maximum(c, blk)
                    if b.within(NG):
                        activate(b)
                    if c.within(NG):
                        shift(c)
                    if b.within(NG):
                        scores(b)
                    if c.within(NG):
                        weigh(c)
                    if b.within(NG):
                        segment_maximum(b)
                    if c.within(NG):
                        accumulate(c, blk)
                ticks(dve, NG, 2, tick)
                dve.wait_ge(acc_ready, (q + 1) * NG)

            def attention_nodes(layer):
                sums = acc[:, :, :].rearrange("p b (h d) -> p (b h) d", h=H)
                inv = rden[:, :, :].rearrange("p b h -> p (b h)")
                chain(dve.tensor_scalar(inv, sums[:, :, D], 1e-30, None, ALU.max))
                chain(dve.reciprocal(inv, inv))
                chain(dve.tensor_tensor(h[:, :, :].rearrange("p b (h d) -> p (b h) d", h=H), sums[:, :, 0:D],
                                        inv.unsqueeze(2).broadcast_to([P, NBLK * H, D]), ALU.mult))
                chain(dve.tensor_tensor(h[:, :, :], h[:, :, :], per_block(vec(f"L1_gnn_b{layer}")), ALU.add))
                chain(dve.tensor_scalar(h[:, :, :], h[:, :, :], 0.0, None, ALU.max))
                center_rows(h[:, :, :])
                chain(dve.tensor_tensor(h[:, :, :], h[:, :, :], per_feature(stat[:, 2, :]), ALU.mult))
                chain(dve.tensor_tensor(h[:, :, :], h[:, :, :], per_block(vec(f"L1_gnn_g{layer}")), ALU.mult))
                chain(dve.tensor_tensor(h[:, :, :], h[:, :, :], per_block(vec(f"L1_gnn_be{layer}")), ALU.add))

            if STOP >= 1:
                dve.wait_ge(weights_in, 16 * NWEIGHT)
                center_rows(x[:, :, :])
                project(0, relu_scaled, both_sides)
                dve.sem_inc(table_set, 1)
                attention_pass(1, 1)
                attention_nodes(1)
                project(1, as_is, both_sides)
                dve.sem_inc(table_set, 1)
                attention_pass(2, 2)
                attention_nodes(2)
                chain(dve.tensor_tensor(x[:, :, :], x[:, :, :], h[:, :, :], ALU.add))

            def gcn_tables(psum, b):
                dve.tensor_scalar(tab[:, b, :], psum[:, 0:F], dinv[:, 0, b], None, ALU.mult)
                return dve.tensor_scalar(xr[:, b, :], psum[:, F:2 * F], dinv[:, 1, b], None, ALU.mult)

            def gcn_side(own, side):
                chain(dve.tensor_tensor(own, own, acc[:, :, 0:F], ALU.add))
                chain(dve.tensor_tensor(own, own, per_feature(dinv[:, side, :]), ALU.mult))

            def mlp_tables(psum, b):
                dve.tensor_scalar(tab[:, b, :], psum[:, 0:F], 1.0, None, ALU.mult)
                return dve.tensor_tensor(xr[:, b, :], psum[:, F:2 * F].unsqueeze(1),
                                         vec("L3_gnn_b1").unsqueeze(1), ALU.add)

            def mlp_pass(q):
                a0 = 2 * NG
                dve.wait_ge(table_out, 16 * (q + 1))
                chain(dve.memset(acc[:, :, :], 0.0))
                chain(dve.memset(attr, 0.0))
                dve.sem_inc(attr_set, 1)

                def heads(part):
                    return part.rearrange("p (n d) -> p n d", d=D)

                def per_head(col):
                    return col.unsqueeze(2).broadcast_to([P, G * H, D])

                def tiles(part):
                    return part.rearrange("p (t c) -> p t c", t=G)

                def center(at):
                    o, c = at.slot % 2, 4 * at.g
                    dve.wait_ge(rows_in[at.slot], 16 * G * (q * NU + at.turn + 1))
                    dve.wait_ge(spread, a0 + at.g + 1)
                    wait(dve, activated, at.g - 1)
                    dve.tensor_tensor(tiles(centered[:, o, :]), tiles(bank[2 + o][:, :]), rows[:, at.slot, :, 0:F],
                                      ALU.add).then_inc(sum_used, 1)
                    dve.wait_ge(sum_used, a0 + at.g + 1)
                    dve.tensor_reduce(mean[:, o, :], heads(centered[:, o, :]), AX, ALU.add).then_inc(edge_step, 1)
                    dve.wait_ge(edge_step, 3 * at.g + 1)
                    dve.tensor_scalar(mean[:, o, :], mean[:, o, :], 1.0 / D, None, ALU.mult).then_inc(edge_step, 1)
                    dve.wait_ge(edge_step, 3 * at.g + 2)
                    dve.tensor_tensor(heads(centered[:, o, :]), heads(centered[:, o, :]), per_head(mean[:, o, :]),
                                      ALU.subtract).then_inc(edge_step, 1)

                def normalise(at):
                    o, base = at.slot % 2, NORM_STEPS * at.g
                    done = [0]

                    def step(ins):
                        done[0] += 1
                        ins.then_inc(norm_step, 1)
                        dve.wait_ge(norm_step, base + done[0])

                    dve.wait_ge(squared, at.g + 1)
                    v_, y, t_ = var[:, o, :], inv[:, o, :], trial[:, o, :]
                    step(dve.tensor_reduce(v_, heads(square[:, o, :]), AX, ALU.add))
                    step(dve.tensor_scalar(v_, v_, 1.0 / D, EPS, ALU.mult, ALU.add))
                    step(dve.tensor_scalar(t_.bitcast(I32), v_.bitcast(I32), 1, None, ALU.arith_shift_right))
                    step(dve.tensor_scalar(y.bitcast(I32), t_.bitcast(I32), -1.0, float(0x5f3759df),
                                           ALU.mult, ALU.add))
                    for _ in range(3):
                        step(dve.tensor_tensor(t_, y, y, ALU.mult))
                        step(dve.scalar_tensor_tensor(out=t_, in0=t_, scalar=-0.5, in1=v_, op0=ALU.mult,
                                                      op1=ALU.mult))
                        step(dve.scalar_tensor_tensor(out=y, in0=t_, scalar=1.5, in1=y, op0=ALU.add, op1=ALU.mult))
                    z = centered[:, o, :]
                    step(dve.tensor_tensor(heads(z), heads(z), per_head(y), ALU.mult))
                    step(dve.tensor_tensor(tiles(z), tiles(z), vec("L3_gnn_gn_gamma").unsqueeze(1)
                                           .broadcast_to([P, G, F]), ALU.mult))
                    step(dve.tensor_tensor(tiles(z), tiles(z), vec("L3_gnn_gn_beta").unsqueeze(1)
                                           .broadcast_to([P, G, F]), ALU.add))
                    assert done[0] == NORM_STEPS

                def tick(at):
                    b, c, d = at.back(1), at.back(2), at.back(3)
                    if at.within(NG):
                        one_hot(q, 0, at, 1)
                    if c.within(NG):
                        normalise(c)
                    if b.within(NG):
                        center(b)
                    if d.within(NG):
                        add_sums(q, 0, d, F)
                ticks(dve, NG, 3, tick)
                dve.wait_ge(acc_ready, (q + 1) * NG)

            def sums_as_is(to, b):
                return dve.tensor_scalar(to.unsqueeze(1), acc[:, b, 0:F], 1.0, None, ALU.mult)

            def with_bias(psum, b):
                return dve.scalar_tensor_tensor(out=h[:, b, :], in0=vec("L3_gnn_b2").unsqueeze(1), scalar=deg_in[:, b],
                                                in1=psum[:, 0:F].unsqueeze(1), op0=ALU.mult, op1=ALU.add)

            if STOP >= 2:
                center_rows(x[:, :, :])
                chain(dve.tensor_scalar(dinv[:, 0, :], deg_in[:, :], 1.0, None, ALU.add))
                chain(dve.tensor_scalar(dinv[:, 1, :], deg_out[:, :], 1.0, None, ALU.add))
                dve.sem_inc(var_ready, 1)
                dve.wait_ge(sqrt_ready, centered_count[0] + 1)
                centered_count[0] += 1
                chain(dve.reciprocal(dinv[:, :, :], dinv[:, :, :]))
                project(2, relu_scaled, gcn_tables)
                dve.sem_inc(table_set, 2)
                chain(dve.memset(acc[:, :, :], 0.0))
                sum_pass(3, 0, 1)
                dve.wait_ge(acc_ready, 4 * NG)
                gcn_side(tab[:, :, :], 0)
                dve.wait_ge(table_out, 16 * 5)
                chain(dve.tensor_tensor(tab[:, :, :], tab[:, :, :], per_block(vec("L2_gnn_b_fwd")), ALU.add))
                chain(dve.memset(acc[:, :, :], 0.0))
                sum_pass(4, 1, 0)
                dve.wait_ge(acc_ready, 5 * NG)
                gcn_side(xr[:, :, :], 1)
                chain(dve.tensor_tensor(xr[:, :, :], xr[:, :, :], per_block(vec("L2_gnn_b_bwd")), ALU.add))
                chain(dve.tensor_tensor(xr[:, :, :], xr[:, :, :], tab[:, :, :], ALU.add))
                chain(dve.scalar_tensor_tensor(out=x[:, :, :], in0=xr[:, :, :], scalar=0.0, in1=x[:, :, :],
                                               op0=ALU.max, op1=ALU.add))
            if STOP >= 3:
                center_rows(x[:, :, :])
                project(3, relu_scaled, mlp_tables)
                dve.sem_inc(table_set, 1)
                mlp_pass(5)
                chain(dve.tensor_scalar(rcount[:, :], deg_in[:, :], 1.0, None, ALU.max))
                chain(dve.reciprocal(rcount[:, :], rcount[:, :]))
                project(4, sums_as_is, with_bias)
                chain(dve.tensor_tensor(h[:, :, :], h[:, :, :], per_feature(rcount[:, :]), ALU.mult))
                chain(dve.tensor_tensor(x[:, :, :], x[:, :, :], h[:, :, :], ALU.add))
            dve.sem_inc(final_set, 1)

        @block.scalar
        def _(act):
            def sqrt_rows(nth):
                act.wait_ge(var_ready, nth)
                nc.scalar.activation(stat[:, 0, :], stat[:, 1, :], ACT.Sqrt).then_inc(sqrt_ready, 1)

            def turn_rows(j):
                def tick(at):
                    act.wait_ge(turned, j * NBLK + at.g + 1)
                    wait(act, mult, j * NBLK + at.g - U + 1)
                    nc.scalar.copy(hs_t[:, at.slot, :], bank[at.slot % 2][:, 0:F]).then_inc(turned_sb, 1)
                ticks(act, NBLK, 0, tick)

            def attention_pass(q):
                a0 = (q - 1) * NG

                def hot(at):
                    o = at.slot % 2
                    act.wait_ge(turned_hot, a0 + at.g + 1)
                    wait(act, max_spread, a0 + at.g - 1)
                    nc.scalar.copy(hot_t[:, o, :], bank[o][:, :]).then_inc(turned_hot_sb, 1)

                def factors(at):
                    o = at.slot % 2
                    act.wait_ge(max_step, 6 * (a0 + at.g) + 5)
                    wait(act, acc_step, a0 + at.g - 1)
                    nc.scalar.activation(factor[:, o, :], drop[:, o, :], ACT.Exp).then_inc(factor_ready, 1)

                def weights(at):
                    o = at.slot % 2
                    act.wait_ge(shift_step, 2 * (a0 + at.g) + 2)
                    wait(act, agg_ready, q * NG + at.g - 1)
                    w = weighted[:, o, :].rearrange("p (n d) -> p n d", d=HD)
                    nc.scalar.activation(w[:, :, D], shifted[:, o, :, :].rearrange("p t h -> p (t h)"), ACT.Exp
                                         ).then_inc(weight_ready, 1)

                def score_rows(at):
                    act.wait_ge(score_turned, a0 + at.g + 1)
                    wait(act, seg_step, 3 * (a0 + at.g - 1))
                    nc.scalar.copy(turned_rows[:, at.slot % 2, :], bank[4][:, 0:2 * P]).then_inc(score_sb, 1)

                def last_rows(at):
                    act.wait_ge(seg_turned, a0 + at.g + 1)
                    wait(act, max_ready, a0 + at.g - 1)
                    nc.scalar.copy(last_t[:, at.slot % 2, :], bank[5][:, 0:P]).then_inc(seg_sb, 1)

                def tick(at):
                    b, c = at.back(1), at.back(2)
                    if at.within(NG):
                        hot(at)
                    if c.within(NG):
                        factors(c)
                        weights(c)
                    if b.within(NG):
                        score_rows(b)
                        last_rows(b)
                ticks(act, NG, 2, tick)

            def mlp_pass(q):
                a0 = 2 * NG

                def turned_in(at):
                    o = at.slot % 2
                    act.wait_ge(turned_hot, a0 + at.g + 1)
                    wait(act, spread, a0 + at.g - 1)
                    nc.scalar.copy(hot_t[:, o, :], bank[o][:, :])
                    nc.scalar.copy(attr_t[:, o, :], bank[4][:, 0:P]).then_inc(turned_hot_sb, 1)

                def squares(at):
                    o = at.slot % 2
                    act.wait_ge(edge_step, 3 * (at.g + 1))
                    wait(act, norm_step, NORM_STEPS * (at.g - 1))
                    nc.scalar.activation(square[:, o, :], centered[:, o, :], ACT.Square).then_inc(squared, 1)

                def silus(at):
                    o = at.slot % 2
                    act.wait_ge(norm_step, NORM_STEPS * (at.g + 1))
                    wait(act, agg_ready, q * NG + at.g - 1)
                    nc.scalar.activation(silu[:, o, :], centered[:, o, :], ACT.Silu).then_inc(activated, 1)

                def tick(at):
                    b, c = at.back(1), at.back(2)
                    if at.within(NG):
                        turned_in(at)
                    if c.within(NG):
                        silus(c)
                    if b.within(NG):
                        squares(b)
                ticks(act, NG, 2, tick)

            sqrt_rows(1)
            if STOP >= 1:
                sqrt_rows(2)
                turn_rows(0)
                attention_pass(1)
                sqrt_rows(3)
                turn_rows(1)
                attention_pass(2)
                sqrt_rows(4)
            if STOP >= 2:
                sqrt_rows(5)
                act.wait_ge(var_ready, 6)
                nc.scalar.activation(dinv[:, :, :], dinv[:, :, :], ACT.Sqrt).then_inc(sqrt_ready, 1)
                turn_rows(2)
            if STOP >= 3:
                sqrt_rows(7)
                turn_rows(3)
                mlp_pass(5)
                turn_rows(4)

        @block.tensor
        def _(pe):
            pe.wait_ge(consts_pool, 5)

            def prefixes(k):
                pe.wait_ge(counts_ready, k + 1)
                wait(pe, prefix_used, k)
                nc.tensor.matmul(counts_ps, ones[:, :], cnt[:, :], start=True, stop=True)
                nc.tensor.matmul(prefix_ps, tri[:, :], cnt[:, :], start=True, stop=True).then_inc(prefix_ready, 1)

            def sum_groups(q, at, width):
                turn = q * (NG // U) + at.turn
                pe.wait_ge(rows_in[at.slot], 16 * G * (turn + 1))
                pe.wait_ge(onehot_ready, q * NG + at.g + 1)
                wait(pe, acc_ready, q * NG + at.g)
                for t in range(G):
                    mm = nc.tensor.matmul(agg[:, 0:width], onehot[:, at.slot, t, :], rows[:, at.slot, t, 0:width],
                                          start=(t == 0), stop=(t == G - 1))
                mm.then_inc(agg_ready, 1)

            def histogram(turn):
                pe.wait_ge(hist_hot, 2 * turn + 2)
                for c in range(HC):
                    mm = nc.tensor.matmul(hist_ps, hist_lo[:, c, :], hist_hi[:, c, :],
                                          start=(isinstance(turn, int) and turn == 0 and c == 0),
                                          stop=(isinstance(turn, int) and turn == NG // U - 1 and c == HC - 1),
                                          skip_group_check=True)
                mm.then_inc(hist_mm, 1)

            def sum_pass(q, extra=None):
                def tick(at):
                    if at.within(NG):
                        sum_groups(q, at, F + 1)
                        if extra is not None and at.slot == 0:
                            extra(at.turn)
                ticks(pe, NG, 0, tick)

            def project(j, width):
                def tick(at):
                    if at.within(NBLK):
                        pe.wait_ge(hs_ready, j * NBLK + at.g + 1)
                        wait(pe, turned_sb, j * NBLK + at.g - 1)
                        nc.tensor.transpose(bank[at.slot % 2][:, 0:F], hs[:, at.slot, :], ident[:, :]
                                            ).then_inc(turned, 1)
                    b = at.back(1)
                    if b.within(NBLK):
                        pe.wait_ge(turned_sb, j * NBLK + b.g + 1)
                        wait(pe, mult_used, j * NBLK + b.g - 1)
                        w = w_out[:, :] if j == 4 else w_pair[:, j, :]
                        nc.tensor.matmul(bank[2 + b.slot % 2][:, 0:width], hs_t[:, b.slot, :], w,
                                         start=True, stop=True).then_inc(mult, 1)
                ticks(pe, NBLK, 1, tick)

            def attention_pass(q):
                a0 = (q - 1) * NG

                def turn_hots(at):
                    pe.wait_ge(onehot_ready, q * NG + at.g + 1)
                    wait(pe, turned_hot_sb, a0 + at.g - 1)
                    for t in range(G):
                        mm = nc.tensor.transpose(bank[at.slot % 2][:, t * P:(t + 1) * P], onehot[:, at.slot, t, :],
                                                 ident[:, :])
                    mm.then_inc(turned_hot, 1)

                def spread_maximum(at):
                    o = at.slot % 2
                    pe.wait_ge(max_step, 6 * (a0 + at.g) + 4)
                    wait(pe, shift_step, 2 * (a0 + at.g) - 1)
                    for t in range(G):
                        mm = nc.tensor.matmul(bank[6][:, t * H:(t + 1) * H], hot_t[:, o, t * P:(t + 1) * P],
                                              newmax[:, o, :], start=True, stop=True)
                    mm.then_inc(max_spread, 1)

                def spread_targets(at):
                    o = at.slot % 2
                    blk = pe.value_load(gblk_i[0][0:1, bass.ds(at.g, 1)], min_val=0, max_val=NBLK - 1)
                    pe.wait_ge(turned_hot_sb, a0 + at.g + 1)
                    wait(pe, sum_used, a0 + at.g - 1)
                    for t in range(G):
                        mm = nc.tensor.matmul(bank[2 + o][:, t * P:(t + 1) * P], hot_t[:, o, t * P:(t + 1) * P],
                                              xr[:, bass.ds(blk, 1), :], start=True, stop=True)
                    mm.then_inc(spread, 1)

                def turn_scores(at):
                    o = at.slot % 2
                    pe.wait_ge(keys_ready, a0 + at.g + 1)
                    pe.wait_ge(score_step, 3 * (a0 + at.g) + 3)
                    wait(pe, score_sb, a0 + at.g)
                    nc.tensor.transpose(bank[4][:, 0:P], steps[:, o, :], ident[:, :])
                    nc.tensor.transpose(bank[4][:, P:2 * P], score[:, o, :], ident[:, :]).then_inc(score_turned, 1)

                def sum_weighted(at):
                    pe.wait_ge(weighted_ready, a0 + at.g + 1)
                    wait(pe, acc_ready, q * NG + at.g)
                    for t in range(G):
                        mm = nc.tensor.matmul(agg, onehot[:, at.slot, t, :],
                                              weighted[:, at.slot % 2, t * H * HD:(t + 1) * H * HD],
                                              start=(t == 0), stop=(t == G - 1))
                    mm.then_inc(agg_ready, 1)

                def node_maximum(at):
                    o = at.slot % 2
                    pe.wait_ge(seg_step, 3 * (a0 + at.g) + 3)
                    wait(pe, max_step, 6 * (a0 + at.g - 1) + 2)
                    nc.tensor.transpose(bank[5][:, 0:P], at_last[:, o, :], ident[:, :]).then_inc(seg_turned, 1)
                    pe.wait_ge(seg_sb, a0 + at.g + 1)
                    for t in range(G):
                        mm = nc.tensor.matmul(bank[5][:, P + 16 * t:P + 16 * t + H + 1], onehot[:, at.slot, t, :],
                                              last_t[:, o, 32 * t:32 * t + H + 1], start=True, stop=True)
                    mm.then_inc(max_ready, 1)

                def tick(at):
                    b, c = at.back(1), at.back(2)
                    if at.within(NG):
                        turn_hots(at)
                    if c.within(NG):
                        spread_maximum(c)
                    if at.within(NG):
                        spread_targets(at)
                    if b.within(NG):
                        turn_scores(b)
                    if c.within(NG):
                        sum_weighted(c)
                    if b.within(NG):
                        node_maximum(b)
                ticks(pe, NG, 2, tick)

            def mlp_pass(q):
                a0 = 2 * NG

                def turn_hots(at):
                    pe.wait_ge(onehot_ready, q * NG + at.g + 1)
                    pe.wait_ge(attr_in[at.slot], 16 * (at.turn + 1))
                    wait(pe, turned_hot_sb, a0 + at.g)
                    nc.tensor.transpose(bank[4][:, 0:P], attr[:, at.slot, :], ident[:, :]).then_inc(attr_free, 1)
                    for t in range(G):
                        mm = nc.tensor.transpose(bank[at.slot % 2][:, t * P:(t + 1) * P], onehot[:, at.slot, t, :],
                                                 ident[:, :])
                    mm.then_inc(turned_hot, 1)

                def spread_targets(at):
                    o = at.slot % 2
                    blk = pe.value_load(gblk_i[0][0:1, bass.ds(at.g, 1)], min_val=0, max_val=NBLK - 1)
                    pe.wait_ge(turned_hot_sb, a0 + at.g + 1)
                    wait(pe, sum_used, a0 + at.g - 1)
                    for t in range(G):
                        nc.tensor.matmul(bank[2 + o][:, t * P:(t + 1) * P], hot_t[:, o, t * P:(t + 1) * P],
                                         xr[:, bass.ds(blk, 1), :], start=True, stop=False)
                        mm = nc.tensor.matmul(bank[2 + o][:, t * P:(t + 1) * P], attr_t[:, o, :], w_attr[:, t, :],
                                              start=False, stop=True)
                    mm.then_inc(spread, 1)

                def sum_activated(at):
                    pe.wait_ge(activated, at.g + 1)
                    wait(pe, acc_ready, q * NG + at.g)
                    for t in range(G):
                        mm = nc.tensor.matmul(agg[:, 0:F], onehot[:, at.slot, t, :],
                                              silu[:, at.slot % 2, t * F:(t + 1) * F],
                                              start=(t == 0), stop=(t == G - 1))
                    mm.then_inc(agg_ready, 1)

                def tick(at):
                    d = at.back(3)
                    if at.within(NG):
                        turn_hots(at)
                    if d.within(NG):
                        sum_activated(d)
                    if at.within(NG):
                        spread_targets(at)
                ticks(pe, NG, 3, tick)

            prefixes(0)
            prefixes(1)
            sum_pass(0, histogram)
            if STOP >= 1:
                pe.wait_ge(weights_in, 16 * NWEIGHT)
                project(0, 2 * F)
                attention_pass(1)
                project(1, 2 * F)
                attention_pass(2)
            if STOP >= 2:
                project(2, 2 * F)
                sum_pass(3)
                sum_pass(4)
            if STOP >= 3:
                project(3, 2 * F)
                mlp_pass(5)
                project(4, F)


INPUTS = ["x", "edge_attr_4", "L1_gnn_Wl1", "L1_gnn_Wr1", "L1_gnn_Wl2", "L1_gnn_Wr2", "L2_gnn_W_fwd", "L2_gnn_W_bwd",
          "L3_gnn_W1", "L3_gnn_W2"] + VECS


def kernel(**inputs):
    import numpy as np
    import concourse.bacc as bacc
    from concourse.bass_utils import run_bass_kernel_spmd as run

    nc = bacc.Bacc("TRN2", target_bir_lowering=False, num_devices=1)
    arrays = {"edges": np.ascontiguousarray(np.stack([inputs["src"], inputs["dst"]], axis=1))}
    arrays.update({name: np.ascontiguousarray(inputs[name]) for name in INPUTS})
    given = {name: nc.dram_tensor(f"in_{name}", array.shape, mybir.dt.from_np(array.dtype), kind="ExternalInput").ap()
             for name, array in arrays.items()}
    out = nc.dram_tensor("out", (N, F), F32, kind="ExternalOutput").ap()
    build(nc, given, out)
    result = run(nc, [{f"in_{name}": array for name, array in arrays.items()}], core_ids=[0])
    return result.results[0]["out"]
```

```python
from contextlib import ExitStack

import concourse.bass as bass
from concourse import mybir

F32 = mybir.dt.float32
I32 = mybir.dt.int32
BF16 = mybir.dt.bfloat16
ALU = mybir.AluOpType
ACT = mybir.ActivationFunctionType
AX = mybir.AxisListType.X

P = 128
N = 6250
F = 128
E = 106250
NBLK = -(-N // P)
NPAD = NBLK * P
G = 4
GE = G * P
NG = (E + NBLK * (GE - 1)) // GE
U = 8
R = 4
NCOL = 832
LASTP = E // NCOL
LASTC = E - LASTP * NCOL
NBUK = NBLK + 1
EPAD = P * NCOL + P * 5
PADT = 8191
H = 8
D = F // H
HD = D + 1
EPS = 1e-5
SLOPE = 0.2
BIG = 1e30
STEPB = float(2 ** 96)


HC = NCOL // (NG // R)
PADR = 5
VECS = ("L1_gnn_att1 L1_gnn_b1 L1_gnn_g1 L1_gnn_be1 L1_gnn_att2 L1_gnn_b2 L1_gnn_g2 L1_gnn_be2 "
        "L2_gnn_b_fwd L2_gnn_b_bwd L3_gnn_b1 L3_gnn_gn_gamma L3_gnn_gn_beta L3_gnn_b2").split()
NVEC = len(VECS)
NWEIGHT = 9 + G + NVEC
NORM_STEPS = 16
NU = NG // U
STOP = 3


class At:

    def __init__(self, turn, slot):
        self.turn, self.slot, self.g = turn, slot, turn * U + slot
        self.short = slot % R
        self.short_turn = turn * (U // R) + slot // R

    def back(self, lag):
        return At(self.turn + (self.slot - lag) // U, (self.slot - lag) % U)

    def within(self, n):
        return not isinstance(self.g, int) or 0 <= self.g < n


def ticks(eng, n, lag, tick):
    for t in range(U):
        tick(At(0, t))
    with eng.Fori(1, n // U) as turn:
        for u in range(U):
            tick(At(turn, u))
    for t in range(n // U * U, n + lag):
        tick(At(t // U, t % U))


def wait(eng, sem, value):
    if not isinstance(value, int) or value > 0:
        eng.wait_ge(sem, value)


class Chain:

    def __init__(self, eng, sem):
        self.eng, self.sem, self.done, self.turns = eng, sem, 0, None

    def __call__(self, ins):
        ins.then_inc(self.sem, 1)
        self.done += 1
        self.eng.wait_ge(self.sem, self.done if self.turns is None else self.turns + self.done)

    def enter(self, i, per):
        self.turns = i * per

    def leave(self, n, per):
        self.turns = None
        self.done += (n - 1) * per


def build(nc, a, out):
    with ExitStack() as ctx:
        def sb(name, shape, dt=F32):
            return ctx.enter_context(nc.sbuf_tensor(name, shape, dt))

        def ps(name, shape, dt=F32):
            return ctx.enter_context(nc.psum_tensor(name, shape, dt))

        def sem(name):
            return ctx.enter_context(nc.semaphore(name))

        def dram(name, shape, dt=F32):
            return nc.dram_tensor(name, shape, dt, kind="Internal").ap()

        edges_by = [dram("edges_by_dst", (EPAD, 2), I32),
                    dram("edges_by_src", (EPAD, 2), I32)]
        attr_by_dst = dram("attr_by_dst", (EPAD, 4))
        table = [dram(f"table{q}", (NPAD, F)) for q in range(6)]

        x = sb("x", [P, NBLK, F])
        h = sb("h", [P, NBLK, F])
        tab = sb("tab", [P, NBLK, F])
        xr = sb("xr", [P, NBLK, F])
        acc = sb("acc", [P, NBLK, H * HD])
        nmax = sb("nmax", [P, NBLK, H])
        rden = sb("rden", [P, NBLK, H])
        stat = sb("stat", [P, 3, NBLK])
        deg_in = sb("deg_in", [P, NBLK])
        deg_out = sb("deg_out", [P, NBLK])
        dinv = sb("dinv", [P, 2, NBLK])
        ident = sb("ident", [P, P])
        ident_b = sb("ident_b", [P, P], BF16)
        tri = sb("tri", [P, P])
        ones = sb("ones", [P, P])
        iota_n = sb("iota_n", [P, P])
        iota_g = sb("iota_g", [P, NG])
        w_pair = sb("w_pair", [P, 4, 2 * F])
        w_attr = sb("w_attr", [P, G, F])
        w_out = sb("w_out", [P, F])
        vecs = sb("vecs", [P, NVEC, F])
        edge_in = sb("edge_in", [P, NCOL, 2], I32)
        rank = sb("rank", [P, NCOL])
        spare = xr[:, :, :].rearrange("p b f -> p (b f)")
        key_i, key, lo, hot, pos, onecol = [spare[:, i * NCOL:(i + 1) * NCOL] for i in range(6)]
        key_i = key_i.bitcast(I32)
        pos_win = sb("pos_win", [P, HC], I32)
        rec_win = sb("rec_win", [P, HC, 2], I32)
        mean = sb("mean", [P, 2, G * H])
        var = sb("var", [P, 2, G * H])
        inv = sb("inv", [P, 2, G * H])
        trial = sb("trial", [P, 2, G * H])
        rcount = sb("rcount", [P, NBLK])
        cnt = sb("cnt", [P, NBUK])
        btot = sb("btot", [P, NBUK])
        bincl = sb("bincl", [P, NBUK])
        bbase = sb("bbase", [P, NG // R])
        bgrp_i = sb("bgrp_i", [P, NBUK], I32)
        bgrp = sb("bgrp", [P, NBUK])
        bend = sb("bend", [P, NBUK])
        bdelta = sb("bdelta", [P, NBUK])
        gtmp = sb("gtmp", [P, NG])
        gblk = sb("gblk", [P, NG])
        gstart = sb("gstart", [P, NG])
        gbase = [sb(f"gbase{k}", [P, NG]) for k in range(2)]
        gblk_i = [sb(f"gblk_i{k}", [P, NG], I32) for k in range(2)]
        gstart_i = [sb(f"gstart_i{k}", [P, NG], I32) for k in range(2)]
        hist_lo = sb("hist_lo", [P, HC, P], BF16)
        hist_hi = sb("hist_hi", [P, HC, NBLK], BF16)
        pad_rows = sb("pad_rows", [P, 2, PADR, 2], I32)
        pad_attr = sb("pad_attr", [P, PADR, 4])
        rec = sb("rec", [P, U, G, 2], I32)
        rows = sb("rows", [P, U, G, F + 1])
        tloc = sb("tloc", [P, U, G])
        h_flat = h[:, :, :].rearrange("p b f -> p (b f)")
        onehot = h_flat[:, 0:U * GE].rearrange("p (u t n) -> p u t n", u=U, t=G)
        onehot_b = h_flat[:, 0:U * GE // 2].bitcast(BF16).rearrange("p (u t n) -> p u t n", u=U, t=G)
        onehot_f = h_flat[:, U * GE // 2:(U // 2 + 2) * GE].rearrange("p (u t n) -> p u t n", u=2, t=G)
        xr_flat = xr[:, :, :].rearrange("p b f -> p (b f)")
        half = NBLK * F // 2
        own_parts = [part.bitcast(BF16).rearrange("p (b f) -> p b f", f=F) for part in (
            xr_flat[:, 0:half], xr_flat[:, half:], h_flat[:, (U // 2 + 2) * GE:(U // 2 + 2) * GE + half])]
        own = acc[:, :, :].rearrange("p b f -> p (b f)")[:, 0:NBLK * F].rearrange("p (b f) -> p b f", f=F)

        hs = sb("hs", [P, R, F])
        hs_t = sb("hs_t", [P, R, F])
        gmax = sb("gmax", [P, 2, H])
        gseen = sb("gseen", [P, 2, G])
        gtile = sb("gtile", [P, 2, G, H])
        newmax = sb("newmax", [P, 2, H])
        max_parts = sb("max_parts", [P, 2, 3, H], BF16)
        max_rest = sb("max_rest", [P, 2, H])
        last_parts = sb("last_parts", [P, 2, 3, G * (H + 1)], BF16)
        drop = sb("drop", [P, 2, H])
        factor = sb("factor", [P, 2, H])
        shifted = sb("shifted", [P, 2, G, H])
        bank = [ps(f"bank{k}", [P, 512]) for k in range(8)]

        (consts_pool, weights_in, x_in, edges_in, edges_set, dst_copied, pads_set, pads_out, v, counts_ready,
         prefix_ready, prefix_used, groups_ready, rank_done, hist_hot, hist_mm, pos_ready, unused_sem, scattered,
         table_set, table_out, hs_ready, turned, turned_sb, mult, mult_used, tick_mark, onehot_ready, tloc_ready, agg_ready,
         acc_ready, var_ready, sqrt_ready, final_set, stored) = [sem(n) for n in (
             "consts_pool weights_in x_in edges_in edges_set dst_copied pads_set pads_out v counts_ready "
             "prefix_ready prefix_used groups_ready rank_done hist_hot hist_mm pos_ready unused_sem scattered "
             "table_set table_out hs_ready turned turned_sb mult mult_used tick_mark onehot_ready tloc_ready agg_ready "
             "acc_ready var_ready sqrt_ready final_set stored").split()]
        (keys_ready, turned_hot, turned_hot_sb, spread, sum_used, scored, score_step, score_turned, score_sb,
         seg_step, seg_turned, seg_sb, max_ready, max_step, max_spread, shift_step, factor_ready, weight_ready,
         weighted_ready, acc_step) = [sem(n) for n in (
             "keys_ready turned_hot turned_hot_sb spread sum_used scored score_step score_turned score_sb "
             "seg_step seg_turned seg_sb max_ready max_step max_spread shift_step factor_ready weight_ready "
             "weighted_ready acc_step").split()]
        (own_rest, own_part, last_part, last_left, max_part, max_left, hot_wide, ident_ready) = [sem(n) for n in (
             "own_rest own_part last_part last_left max_part max_left hot_wide ident_ready").split()]
        (win_free, attr_set, edge_step, squared, norm_step, activated, attr_free, out_step) = [sem(n) for n in (
             "win_free attr_set edge_step squared norm_step activated attr_free out_step").split()]
        attr_in = [sem(f"attr_in{u}") for u in range(R)]
        rec_in = [sem(f"rec_in{u}") for u in range(U)]
        rows_in = [sem(f"rows_in{u}") for u in range(U)]

        block = ctx.enter_context(nc.Block())

        flat = tab[:, :, :].rearrange("p b f -> p (b f)")
        area, place = [0], [flat]

        def ring(*shape):
            size = 1
            for n in shape:
                size *= n
            part = place[0][:, area[0]:area[0] + size]
            area[0] += size
            return part.rearrange("p (u n) -> p u n", u=shape[0])

        hot_t = ring(R, GE // 2).bitcast(BF16)
        both = ring(1, GE)
        weighted = ring(2, G * H * HD)
        score = ring(R, G * 32)
        steps = ring(2, G * 32)
        turned_rows = ring(2, 2 * P)
        fence = ring(2, P + 2)
        running = ring(2, P)
        at_last = ring(2, P)
        last_rest = ring(2, G * (H + 1))
        assert area[0] <= NBLK * F
        area[0], place[0] = 0, flat
        ring(R, GE // 2)
        centered = ring(2, GE)
        square = ring(2, GE)
        silu = ring(2, GE)
        attr = ring(R, G * 32)
        attr_t = ring(2, P)
        assert area[0] <= NBLK * F
        counts_ps, prefix_ps, hist_ps = bank[0][:, 0:NBUK], bank[1][:, 0:NBUK], bank[6][:, 0:NBLK]
        bank_b = [bank[k][:, 0:GE // 2].bitcast(BF16) for k in range(2)]
        agg = bank[7][:, 0:H * HD]

        def vec(name):
            return vecs[:, VECS.index(name), :]

        def per_block(row):
            return row.unsqueeze(1).broadcast_to([P, NBLK, F])

        def per_feature(col):
            return col.unsqueeze(2).broadcast_to([P, NBLK, F])

        @block.sync
        def _(sp):
            weights = [(w_pair[:, 0, 0:F], a["L1_gnn_Wl1"]), (w_pair[:, 0, F:2 * F], a["L1_gnn_Wr1"]),
                       (w_pair[:, 1, 0:F], a["L1_gnn_Wl2"]), (w_pair[:, 1, F:2 * F], a["L1_gnn_Wr2"]),
                       (w_pair[:, 2, 0:F], a["L2_gnn_W_fwd"]), (w_pair[:, 2, F:2 * F], a["L2_gnn_W_bwd"]),
                       (w_pair[:, 3, 0:F], a["L3_gnn_W1"][F:2 * F, :]), (w_pair[:, 3, F:2 * F], a["L3_gnn_W1"][0:F, :]),
                       (w_out[:, :], a["L3_gnn_W2"])]
            weights += [(w_attr[32 * t:32 * t + 4, t, :], a["L3_gnn_W1"][2 * F:2 * F + 4, :]) for t in range(G)]
            weights += [(vecs[:, i, :], (a[name].rearrange("h d -> (h d)") if "att" in name else a[name])
                         .unsqueeze(0).broadcast_to([P, F])) for i, name in enumerate(VECS)]
            assert len(weights) == NWEIGHT
            sp.wait_ge(pads_set, 1)
            sp.dma_start(edge_in[0:LASTP, :, :], a["edges"][0:LASTP * NCOL, :].rearrange("(p c) k -> p c k", c=NCOL)
                         ).then_inc(edges_in, 16)
            sp.dma_start(edge_in[LASTP:LASTP + 1, 0:LASTC, :],
                         a["edges"][LASTP * NCOL:E, :].unsqueeze(0)).then_inc(edges_in, 16)
            sp.dma_start(x[:, 0:NBLK - 1, :], a["x"][0:(NBLK - 1) * P, :].rearrange("(b p) f -> p b f", p=P)
                         ).then_inc(x_in, 16)
            sp.dma_start(x[0:N - (NBLK - 1) * P, NBLK - 1, :], a["x"][(NBLK - 1) * P:N, :]).then_inc(x_in, 16)
            sp.dma_start(edges_by[0][0:E, :], a["edges"]).then_inc(dst_copied, 16)
            sp.dma_start(attr_by_dst[0:E, :], a["edge_attr_4"]).then_inc(dst_copied, 16)
            sp.dma_start(edges_by[0][E:E + P * PADR, :].rearrange("(p r) k -> p r k", p=P),
                         pad_rows[:, 0, :, :]).then_inc(pads_out, 16)
            sp.dma_start(edges_by[1][P * NCOL:EPAD, :].rearrange("(p r) k -> p r k", p=P),
                         pad_rows[:, 1, :, :]).then_inc(pads_out, 16)
            sp.dma_start(attr_by_dst[E:E + P * PADR, :].rearrange("(p r) k -> p r k", p=P),
                         pad_attr[:, :, :]).then_inc(pads_out, 16)
            for to, of in weights:
                sp.dma_start(to, of).then_inc(weights_in, 16)
            sp.wait_ge(dst_copied, 32)
            sp.wait_ge(pads_out, 48)

            def store_table(q, staged):
                sp.wait_ge(table_set, q + 1)
                sp.dma_start(table[q].rearrange("(b p) f -> p b f", p=P), staged).then_inc(table_out, 16)

            def edge_records(q, k, with_attr=False):
                sp.wait_ge(groups_ready, k + 1)

                def tick(at):
                    wait(sp, agg_ready, q * NG + at.g - U + 1)
                    first = sp.value_load(gstart_i[k][0:1, bass.ds(at.g, 1)], min_val=0, max_val=E)
                    sp.dma_start(rec[:, at.slot, :, :],
                                 edges_by[k][bass.ds(first, GE), :].rearrange("(p t) k -> p t k", t=G)
                                 ).then_inc(rec_in[at.slot], 16)
                    if with_attr:
                        wait(sp, attr_free, at.g - R + 1)
                        sp.dma_start(attr[:, at.short, :].rearrange("p (t c) -> p t c", t=G)[:, :, 0:4],
                                     attr_by_dst[bass.ds(first, GE), :].rearrange("(p t) k -> p t k", t=G)
                                     ).then_inc(attr_in[at.short], 16)
                ticks(sp, NG, 0, tick)

            store_table(0, tab[:, :, :])
            edge_records(0, 0)
            if STOP >= 1:
                for q in (1, 2):
                    store_table(q, tab[:, :, :])
                    edge_records(q, 0)
            if STOP >= 2:
                store_table(3, tab[:, :, :])
                store_table(4, xr[:, :, :])
                edge_records(3, 0)
                sp.wait_ge(scattered, 16 * NCOL)
                edge_records(4, 1)
            if STOP >= 3:
                store_table(5, tab[:, :, :])
                sp.wait_ge(attr_set, 1)
                edge_records(5, 0, True)
            if True:
                sp.wait_ge(final_set, 1)
                sp.dma_start(out[0:(NBLK - 1) * P, :].rearrange("(b p) f -> p b f", p=P), x[:, 0:NBLK - 1, :]
                             ).then_inc(stored, 16)
                sp.dma_start(out[(NBLK - 1) * P:N, :], x[0:N - (NBLK - 1) * P, NBLK - 1, :]).then_inc(stored, 16)
                sp.wait_ge(stored, 32)

        @block.gpsimd
        def _(pool):
            nc.gpsimd.iota(iota_n[:, :], [[1, P]], base=0, channel_multiplier=0,
                           allow_small_or_imprecise_dtypes=True).then_inc(consts_pool, 1)
            nc.gpsimd.iota(iota_g[:, :], [[1, NG]], base=0, channel_multiplier=0,
                           allow_small_or_imprecise_dtypes=True).then_inc(consts_pool, 1)
            nc.gpsimd.memset(ones[:, :], 1.0).then_inc(consts_pool, 1)
            pool.wait_ge(consts_pool, 3)
            nc.gpsimd.affine_select(out=ident[:, :], in_=ones[:, :], compare_op=ALU.is_equal, fill=0.0, base=0,
                                    pattern=[[-1, P]], channel_multiplier=1).then_inc(consts_pool, 1)
            nc.gpsimd.affine_select(out=tri[:, :], in_=ones[:, :], compare_op=ALU.is_gt, fill=0.0, base=0,
                                    pattern=[[1, P]], channel_multiplier=-1).then_inc(consts_pool, 1)

            def scatter_columns(at):
                if at.short == 0:
                    wait(pool, scattered, 16 * HC * at.short_turn)
                    if isinstance(at.short_turn, int):
                        pool.wait_ge(rank_done, 4 * (NG // R))
                    pool.sem_inc(tick_mark, 1)
                    cols = bass.ds(at.short_turn * HC, HC)
                    nc.gpsimd.tensor_copy(pos_win[:, :], rank[:, cols]).then_inc(win_free, 1)
                    nc.gpsimd.tensor_copy(rec_win[:, :, :], edge_in[:, cols, :]).then_inc(win_free, 1)
                    pool.wait_ge(win_free, 2 * at.short_turn + 2)
                    pool.sem_inc(tick_mark, 1)
                for c in range(at.short * HC // R, (at.short + 1) * HC // R):
                    pool.indirect_dma_start(edges_by[1], bass.IndirectOffsetOnAxis(pos_win[:, c:c + 1], 0),
                                            rec_win[:, c, :], None).then_inc(scattered, 16)

            def gathers(q, gathered_end, beside=None):
                pool.wait_ge(table_out, 16 * (q + 1))

                def tick(at):
                    turn = q * (NG // U) + at.turn
                    wait(pool, agg_ready, q * NG + at.g - U + 1)
                    pool.wait_ge(rec_in[at.slot], 16 * (turn + 1))
                    pool.sem_inc(tick_mark, 1)
                    for t in range(G):
                        pool.indirect_dma_start(
                            rows[:, at.slot, t, 0:F], None, table[q],
                            bass.IndirectOffsetOnAxis(rec[:, at.slot, t, gathered_end:gathered_end + 1], 0)
                        ).then_inc(rows_in[at.slot], 16)
                    if beside is not None:
                        beside(at)
                ticks(pool, NG, 0, tick)

            gathers(0, 0)
            if STOP >= 1:
                gathers(1, 0, scatter_columns)
                gathers(2, 0)
            if STOP >= 2:
                gathers(3, 0)
                gathers(4, 1)
            if STOP >= 3:
                gathers(5, 0)

        @block.vector
        def _(dve):
            chain = Chain(dve, v)
            chain(dve.memset(edge_in[96:P, :, 0], PADT))
            chain(dve.memset(edge_in[96:P, :, 1], 0))
            chain(dve.memset(pad_rows[:, :, :, :], 0))
            chain(dve.memset(pad_rows[:, 0, :, 1], PADT))
            chain(dve.memset(pad_rows[:, 1, :, 0], PADT))
            chain(dve.memset(pad_attr[:, :, :], 0.0))
            chain(dve.memset(w_attr[:, :, :], 0.0))
            chain(dve.memset(x[0:P, NBLK - 1, :], 0.0))
            dve.sem_inc(pads_set, 1)
            chain(dve.memset(rows[:, :, :, F:F + 1], 1.0))
            chain(dve.memset(onecol[:, :], 1.0))
            chain(dve.memset(bbase[:, :], 0.0))

            def count_buckets(end):
                chain(dve.tensor_scalar(key_i[:, :], edge_in[:, :, end], 7, None, ALU.arith_shift_right))
                chain(dve.tensor_copy(key[:, :], key_i[:, :]))
                chain(dve.tensor_scalar(key[:, :], key[:, :], float(NBLK), None, ALU.min))
                with dve.Fori(0, NBUK) as b:
                    chain.enter(b, 1)
                    chain(dve.tensor_scalar(hot[:, :], key[:, :], iota_n[:, bass.ds(b, 1)], 0.0,
                                            ALU.is_equal, ALU.add, accum_out=cnt[:, bass.ds(b, 1)]))
                chain.leave(NBUK, 1)
                dve.sem_inc(counts_ready, 1)

            def group_table(k):
                dve.wait_ge(prefix_ready, k + 1)
                chain(dve.tensor_copy(btot[:, :], counts_ps))
                if k == 0:
                    chain(dve.tensor_scalar(btot[:, 0:1], btot[:, 0:1], -float(P * NCOL - E), None, ALU.add))
                if k == 1:
                    chain(dve.tensor_tensor_scan(bincl[:, :], onecol[:, 0:NBUK], btot[:, :], 0.0, ALU.mult, ALU.add))
                    chain(dve.tensor_tensor(bincl[:, :], bincl[:, :], btot[:, :], ALU.subtract))
                    chain(dve.scalar_tensor_tensor(out=bbase[:, 0:NBUK], in0=bincl[:, :], scalar=-1.0, in1=prefix_ps,
                                                   op0=ALU.add, op1=ALU.add))
                dve.sem_inc(prefix_used, 1)
                chain(dve.tensor_scalar(bgrp_i[:, :], btot[:, :], float(GE - 1), None, ALU.add))
                chain(dve.tensor_scalar(bgrp_i[:, :], bgrp_i[:, :], GE.bit_length() - 1, None, ALU.arith_shift_right))
                chain(dve.tensor_copy(bgrp[:, :], bgrp_i[:, :]))
                chain(dve.tensor_tensor_scan(bend[:, :], onecol[:, 0:NBUK], bgrp[:, :], 0.0, ALU.mult, ALU.add))
                chain(dve.scalar_tensor_tensor(out=bdelta[:, :], in0=bgrp[:, :], scalar=-float(GE), in1=btot[:, :],
                                               op0=ALU.mult, op1=ALU.add))
                chain(dve.memset(gblk[:, :], 0.0))
                chain(dve.tensor_scalar(gstart[:, :], iota_g[:, :], float(GE), None, ALU.mult))
                with dve.Fori(0, NBLK) as b:
                    chain.enter(b, 3)
                    end_b, delta_b = bend[:, bass.ds(b, 1)], bdelta[:, bass.ds(b, 1)]
                    chain(dve.scalar_tensor_tensor(out=gblk[:, :], in0=iota_g[:, :], scalar=end_b, in1=gblk[:, :],
                                                   op0=ALU.is_ge, op1=ALU.add))
                    chain(dve.tensor_scalar(gtmp[:, :], iota_g[:, :], end_b, delta_b, ALU.is_ge, ALU.mult))
                    chain(dve.tensor_tensor(gstart[:, :], gstart[:, :], gtmp[:, :], ALU.add))
                chain.leave(NBLK, 3)
                chain(dve.tensor_scalar(gblk_i[k][:, :], gblk[:, :], float(NBLK - 1), None, ALU.min))
                chain(dve.tensor_scalar(gbase[k][:, :], gblk[:, :], float(NBLK - 1), float(P), ALU.min, ALU.mult))
                chain(dve.tensor_scalar(gstart_i[k][:, :], gstart[:, :], float(E), None, ALU.min))
                dve.sem_inc(groups_ready, 1)

            centered_count = [0]

            def center_rows(src):
                chain(dve.tensor_reduce(stat[:, 0, :], src, AX, ALU.add))
                chain(dve.tensor_scalar(stat[:, 1, :], stat[:, 0, :], 1.0 / F, None, ALU.mult))
                chain(dve.tensor_tensor(h[:, :, :], src, per_feature(stat[:, 1, :]), ALU.subtract))
                chain(dve.tensor_tensor(tab[:, :, :], h[:, :, :], h[:, :, :], ALU.mult))
                chain(dve.tensor_reduce(stat[:, 0, :], tab[:, :, :], AX, ALU.add))
                chain(dve.tensor_scalar(stat[:, 1, :], stat[:, 0, :], 1.0 / F, EPS, ALU.mult, ALU.add))
                dve.sem_inc(var_ready, 1)
                centered_count[0] += 1
                dve.wait_ge(sqrt_ready, centered_count[0])
                chain(dve.reciprocal(stat[:, 2, :], stat[:, 0, :]))

            def one_hot(q, k, at, end, ring_of=onehot):
                turn = q * (NG // U) + at.turn
                dve.wait_ge(rec_in[at.slot], 16 * (turn + 1))
                wait(dve, agg_ready, q * NG + at.g - U + 1)
                dve.tensor_scalar(tloc[:, at.slot, :], rec[:, at.slot, :, end], gbase[k][:, bass.ds(at.g, 1)], None,
                                  ALU.subtract).then_inc(tloc_ready, 1)
                dve.wait_ge(tloc_ready, q * NG + at.g + 1)
                dve.tensor_tensor(ring_of[:, at.slot, :, :], iota_n[:, :].unsqueeze(1).broadcast_to([P, G, P]),
                                  tloc[:, at.slot, :].unsqueeze(2).broadcast_to([P, G, P]), ALU.is_equal
                                  ).then_inc(onehot_ready, 1)

            def add_sums(q, k, at, width):
                blk = dve.value_load(gblk_i[k][0:1, bass.ds(at.g, 1)], min_val=0, max_val=NBLK - 1)
                dve.wait_ge(agg_ready, q * NG + at.g + 1)
                wait(dve, acc_ready, q * NG + at.g)
                dve.tensor_tensor(acc[:, bass.ds(blk, 1), 0:width], acc[:, bass.ds(blk, 1), 0:width],
                                  agg[:, 0:width].unsqueeze(1), ALU.add).then_inc(acc_ready, 1)

            def sum_pass(q, k, end, extra=None):
                width = F + 1

                def tick(at):
                    if at.within(NG):
                        one_hot(q, k, at, end)
                        if extra is not None and at.short == 0:
                            extra(at.short_turn)
                    if at.back(1).within(NG):
                        add_sums(q, k, at.back(1), width)
                ticks(dve, NG, 1, tick)

            dve.wait_ge(consts_pool, 5)
            chain(dve.tensor_copy(ident_b[:, :], ident[:, :]))
            dve.sem_inc(ident_ready, 1)
            dve.wait_ge(edges_in, 32)
            count_buckets(1)
            dve.wait_ge(x_in, 32)
            center_rows(x[:, :, :])
            chain(dve.scalar_tensor_tensor(out=tab[:, :, :], in0=h[:, :, :], scalar=0.0,
                                           in1=per_feature(stat[:, 2, :]), op0=ALU.max, op1=ALU.mult))
            dve.sem_inc(table_set, 1)
            group_table(0)
            count_buckets(0)
            group_table(1)
            chain(dve.memset(rank[:, :], 0.0))
            chain(dve.memset(acc[:, :, :], 0.0))
            chain(dve.tensor_scalar(key_i[:, :], edge_in[:, :, 0], P - 1, None, ALU.bitwise_and))
            chain(dve.tensor_copy(lo[:, :], key_i[:, :]))

            def sort_turn(turn):
                bucket = iota_n[:, bass.ds(turn, 1)]
                if isinstance(turn, int) and turn >= NG // R:
                    return
                done = 4 * turn
                dve.tensor_scalar(hot[:, :], key[:, :], bucket, None, ALU.is_equal).then_inc(rank_done, 1)
                dve.wait_ge(rank_done, done + 1)
                dve.tensor_tensor_scan(pos[:, :], onecol[:, :], hot[:, :], bbase[:, bass.ds(turn, 1)],
                                       ALU.mult, ALU.add).then_inc(rank_done, 1)
                dve.wait_ge(rank_done, done + 2)
                dve.tensor_tensor(hot[:, :], hot[:, :], pos[:, :], ALU.mult).then_inc(rank_done, 1)
                dve.wait_ge(rank_done, done + 3)
                dve.tensor_tensor(rank[:, :], rank[:, :], hot[:, :], ALU.add).then_inc(rank_done, 1)
                dve.wait_ge(rank_done, done + 4)
                wait(dve, hist_mm, turn)
                cols = bass.ds(turn * HC, HC)
                dve.tensor_tensor(hist_lo[:, :, :], iota_n[:, :].unsqueeze(1).broadcast_to([P, HC, P]),
                                  lo[:, cols].unsqueeze(2).broadcast_to([P, HC, P]), ALU.is_equal
                                  ).then_inc(hist_hot, 1)
                dve.tensor_tensor(hist_hi[:, :, :], iota_n[:, 0:NBLK].unsqueeze(1).broadcast_to([P, HC, NBLK]),
                                  key[:, cols].unsqueeze(2).broadcast_to([P, HC, NBLK]), ALU.is_equal
                                  ).then_inc(hist_hot, 1)

            sum_pass(0, 0, 1, sort_turn)
            dve.wait_ge(acc_ready, NG)
            chain(dve.tensor_copy(deg_in[:, :], acc[:, :, F]))
            chain(dve.tensor_tensor(x[:, :, :], x[:, :, :], acc[:, :, 0:F], ALU.add))
            dve.wait_ge(hist_mm, NG // R)
            chain(dve.tensor_copy(deg_out[:, :], hist_ps))

            def project(j, prepare, finish):
                def tick(at):
                    if at.within(NBLK):
                        wait(dve, turned, j * NBLK + at.g - R + 1)
                        prepare(hs[:, at.short, :], bass.ds(at.g, 1)).then_inc(hs_ready, 1)
                    b = at.back(2)
                    if b.within(NBLK):
                        dve.wait_ge(mult, j * NBLK + b.g + 1)
                        finish(bank[2 + b.slot % 2], bass.ds(b.g, 1)).then_inc(mult_used, 1)
                ticks(dve, NBLK, 2, tick)
                dve.wait_ge(mult_used, (j + 1) * NBLK)

            def relu_scaled(to, b):
                return dve.tensor_scalar(to, h[:, b, :], 0.0, stat[:, 2, b], ALU.max, ALU.mult)

            def as_is(to, b):
                return dve.tensor_scalar(to, h[:, b, :], 1.0, None, ALU.mult)

            def both_sides(psum, b):
                dve.tensor_scalar(tab[:, b, :], psum[:, 0:F], 1.0, None, ALU.mult)
                return dve.tensor_scalar(own[:, b, :], psum[:, F:2 * F], 1.0, None, ALU.mult)

            splits = [0]

            def split_own():
                dve.sem_inc(own_rest, 1)
                dve.wait_ge(own_part, 2 * splits[0] + 1)
                chain(dve.tensor_tensor(own, own, own_parts[0], ALU.subtract))
                dve.sem_inc(own_rest, 1)
                dve.wait_ge(own_part, 2 * splits[0] + 2)
                chain(dve.tensor_tensor(own_parts[2], own, own_parts[1], ALU.subtract))
                splits[0] += 1

            def attention_pass(q, layer):
                a0 = (q - 1) * NG
                att = vec(f"L1_gnn_att{layer}")
                split_own()
                dve.wait_ge(table_out, 16 * (q + 1))
                chain(dve.memset(acc[:, :, :], 0.0))
                chain(dve.memset(nmax[:, :, :], -BIG))
                chain(dve.memset(score, 0.0))
                chain(dve.memset(score.rearrange("p u (t c) -> p (u t) c", c=32)[:, :, H:H + 1], 1.0))
                chain(dve.memset(steps, 0.0))
                chain(dve.memset(fence, 0.0))
                chain(dve.memset(fence[:, :, P:P + 1], -1.0))

                def tiles(part):
                    return part.rearrange("p (t c) -> p t c", t=G)

                tile_max = bank[5][:, P:P + 16 * G].rearrange("p (t c) -> p t c", t=G)

                def step_keys(at):
                    wait(dve, score_turned, a0 + at.g - 1)
                    dve.tensor_scalar(tiles(steps[:, at.slot % 2, :])[:, :, 0:H + 1],
                                      tloc[:, at.slot, :].unsqueeze(2).broadcast_to([P, G, H + 1]), STEPB, None,
                                      ALU.mult).then_inc(keys_ready, 1)

                def node_max_1(at):
                    o = at.slot % 2
                    dve.wait_ge(max_ready, a0 + at.g + 1)
                    dve.tensor_scalar(gseen[:, o, :], tile_max[:, :, H], -1.0, BIG, ALU.add, ALU.mult
                                      ).then_inc(max_step, 1)

                def node_max_2(at):
                    o, c = at.slot % 2, 6 * (a0 + at.g)
                    dve.wait_ge(max_step, c + 1)
                    dve.tensor_tensor(gtile[:, o, :, :], tile_max[:, :, 0:H],
                                      gseen[:, o, :].unsqueeze(2).broadcast_to([P, G, H]), ALU.add
                                      ).then_inc(max_step, 1)

                def node_max_3(at):
                    o, c = at.slot % 2, 6 * (a0 + at.g)
                    dve.wait_ge(max_step, c + 2)
                    dve.tensor_reduce(gmax[:, o, :], gtile[:, o, :, :].rearrange("p t h -> p h t"), AX, ALU.max
                                      ).then_inc(max_step, 1)

                def node_max_4(at, blk):
                    o, c = at.slot % 2, 6 * (a0 + at.g)
                    dve.wait_ge(max_step, c + 3)
                    wait(dve, max_spread, a0 + at.g - 1)
                    dve.tensor_tensor(newmax[:, o:o + 1, :], nmax[:, bass.ds(blk, 1), :], gmax[:, o:o + 1, :], ALU.max
                                      ).then_inc(max_step, 1)

                def node_max_5(at, blk):
                    o, c = at.slot % 2, 6 * (a0 + at.g)
                    dve.wait_ge(max_step, c + 4)
                    wait(dve, factor_ready, a0 + at.g - 1)
                    dve.tensor_tensor(drop[:, o:o + 1, :], nmax[:, bass.ds(blk, 1), :], newmax[:, o:o + 1, :],
                                      ALU.subtract).then_inc(max_step, 1)

                def node_max_6(at, blk):
                    o, c = at.slot % 2, 6 * (a0 + at.g)
                    dve.wait_ge(max_step, c + 5)
                    dve.tensor_scalar(nmax[:, bass.ds(blk, 1), :], newmax[:, o:o + 1, :], 1.0, None, ALU.mult
                                      ).then_inc(max_step, 1)

                def add_rows(at):
                    o = at.slot % 2
                    dve.wait_ge(rows_in[at.slot], 16 * G * (q * NU + at.turn + 1))
                    dve.wait_ge(spread, a0 + at.g + 1)
                    dve.tensor_tensor(tiles(both[:, 0, :]), tiles(bank[2 + o][:, :]), rows[:, at.slot, :, 0:F],
                                      ALU.add).then_inc(sum_used, 1)

                def leaky(at):
                    dve.wait_ge(sum_used, a0 + at.g + 1)
                    dve.scalar_tensor_tensor(out=both[:, 0, :], in0=both[:, 0, :], scalar=SLOPE, in1=both[:, 0, :],
                                             op0=ALU.mult, op1=ALU.max).then_inc(score_step, 1)

                def times_att(at):
                    dve.wait_ge(score_step, 3 * (a0 + at.g) + 1)
                    dve.tensor_tensor(tiles(both[:, 0, :]), tiles(both[:, 0, :]),
                                      att.unsqueeze(1).broadcast_to([P, G, F]), ALU.mult).then_inc(score_step, 1)

                def head_sums(at):
                    o = at.slot % 2
                    dve.wait_ge(score_step, 3 * (a0 + at.g) + 2)
                    dve.tensor_reduce(tiles(score[:, at.short, :])[:, :, 0:H],
                                      both[:, 0, :].rearrange("p (t h d) -> p t h d", t=G, h=H), AX, ALU.add
                                      ).then_inc(score_step, 1)

                def segment_1(at):
                    o = at.slot % 2
                    dve.wait_ge(score_sb, a0 + at.g + 1)
                    dve.tensor_tensor(fence[:, o, 1:P], turned_rows[:, o, 0:P - 1], turned_rows[:, o, 1:P],
                                      ALU.subtract).then_inc(seg_step, 1)

                def segment_2(at):
                    o = at.slot % 2
                    dve.wait_ge(seg_step, 3 * (a0 + at.g) + 1)
                    dve.tensor_tensor_scan(running[:, o, :], fence[:, o, 0:P], turned_rows[:, o, P:2 * P], -BIG,
                                           ALU.add, ALU.max).then_inc(seg_step, 1)

                def segment_3(at):
                    o = at.slot % 2
                    dve.wait_ge(seg_step, 3 * (a0 + at.g) + 2)
                    wait(dve, seg_turned, a0 + at.g - 1)
                    dve.scalar_tensor_tensor(out=at_last[:, o, :], in0=fence[:, o, 1:P + 1], scalar=0.0,
                                             in1=running[:, o, :], op0=ALU.not_equal, op1=ALU.mult
                                             ).then_inc(seg_step, 1)

                last_turned = bank[5][:, 0:P].rearrange("p (t c) -> p t c", t=G)[:, :, 0:H + 1]

                def last_rest_1(at):
                    o = at.slot % 2
                    dve.wait_ge(last_part, 2 * (a0 + at.g) + 1)
                    dve.tensor_tensor(tiles(last_rest[:, o, :]), last_turned, tiles(last_parts[:, o, 0, :]),
                                      ALU.subtract).then_inc(last_left, 1)

                def last_rest_2(at):
                    o = at.slot % 2
                    dve.wait_ge(last_part, 2 * (a0 + at.g) + 2)
                    dve.tensor_tensor(last_parts[:, o, 2, :], last_rest[:, o, :], last_parts[:, o, 1, :],
                                      ALU.subtract).then_inc(last_left, 1)

                def max_rest_1(at):
                    o = at.slot % 2
                    dve.wait_ge(max_part, 2 * (a0 + at.g) + 1)
                    dve.tensor_tensor(max_rest[:, o, :], newmax[:, o, :], max_parts[:, o, 0, :], ALU.subtract
                                      ).then_inc(max_left, 1)

                def max_rest_2(at):
                    o = at.slot % 2
                    dve.wait_ge(max_part, 2 * (a0 + at.g) + 2)
                    dve.tensor_tensor(max_parts[:, o, 2, :], max_rest[:, o, :], max_parts[:, o, 1, :], ALU.subtract
                                      ).then_inc(max_left, 1)

                def shift_1(at):
                    o = at.slot % 2
                    dve.wait_ge(max_spread, a0 + at.g + 1)
                    wait(dve, weight_ready, a0 + at.g - 1)
                    dve.tensor_tensor(shifted[:, o, :, :], tiles(score[:, at.short, :])[:, :, 0:H],
                                      bank[6][:, 0:G * H].rearrange("p (t h) -> p t h", t=G), ALU.subtract
                                      ).then_inc(shift_step, 1)

                def shift_2(at):
                    o = at.slot % 2
                    dve.wait_ge(shift_step, 2 * (a0 + at.g) + 1)
                    dve.tensor_scalar(shifted[:, o, :, :], shifted[:, o, :, :], 0.0, None, ALU.min
                                      ).then_inc(shift_step, 1)

                def weigh(at):
                    o = at.slot % 2
                    dve.wait_ge(weight_ready, a0 + at.g + 1)
                    w = weighted[:, o, :].rearrange("p (t h d) -> p t h d", t=G, h=H)
                    dve.tensor_tensor(w[:, :, :, 0:D],
                                      rows[:, at.slot, :, 0:F].rearrange("p t (h d) -> p t h d", h=H),
                                      w[:, :, :, D:HD].broadcast_to([P, G, H, D]), ALU.mult
                                      ).then_inc(weighted_ready, 1)

                def rescale_sums(at, blk):
                    o = at.slot % 2
                    dve.wait_ge(factor_ready, a0 + at.g + 1)
                    wait(dve, acc_ready, q * NG + at.g)
                    sums = acc[:, bass.ds(blk, 1), :].rearrange("p b (h d) -> p (b h) d", h=H)
                    dve.tensor_tensor(sums, sums, factor[:, o, :].unsqueeze(2).broadcast_to([P, H, HD]), ALU.mult
                                      ).then_inc(acc_step, 1)

                def accumulate(at, blk):
                    sums = acc[:, bass.ds(blk, 1), :].rearrange("p b (h d) -> p (b h) d", h=H)
                    dve.wait_ge(acc_step, a0 + at.g + 1)
                    dve.wait_ge(agg_ready, q * NG + at.g + 1)
                    dve.tensor_tensor(sums, sums, agg.rearrange("p (h d) -> p h d", h=H), ALU.add
                                      ).then_inc(acc_ready, 1)

                blocks = {}

                def block_of(at):
                    return dve.value_load(gblk_i[0][0:1, bass.ds(at.g, 1)], min_val=0, max_val=NBLK - 1)

                def tick(at):
                    b, c, d, e = (at.back(lag) for lag in (1, 2, 3, 4))
                    now, one, two, three, four = (i.within(NG) for i in (at, b, c, d, e))
                    if three:
                        blk = block_of(d)
                    if four:
                        old = blocks[(at.slot - 1) % U] if at.slot else block_of(e)
                    if three:
                        blocks[at.slot] = blk
                    if now:
                        one_hot(q, 0, at, 1, onehot_b)
                    if three:
                        node_max_1(d)
                    if three:
                        node_max_2(d)
                    if four:
                        shift_1(e)
                    if one:
                        add_rows(b)
                    if three:
                        node_max_3(d)
                    if four:
                        shift_2(e)
                    if two:
                        segment_1(c)
                    if one:
                        leaky(b)
                    if three:
                        node_max_4(d, blk)
                    if two:
                        segment_2(c)
                    if four:
                        weigh(e)
                    if two:
                        segment_3(c)
                    if three:
                        node_max_5(d, blk)
                    if three:
                        max_rest_1(d)
                    if one:
                        times_att(b)
                    if two:
                        last_rest_1(c)
                    if three:
                        max_rest_2(d)
                    if now:
                        step_keys(at)
                    if three:
                        node_max_6(d, blk)
                    if one:
                        head_sums(b)
                    if two:
                        last_rest_2(c)
                    if four:
                        rescale_sums(e, old)
                    if four:
                        accumulate(e, old)
                ticks(dve, NG, 4, tick)
                dve.wait_ge(acc_ready, (q + 1) * NG)

            def attention_nodes(layer):
                sums = acc[:, :, :].rearrange("p b (h d) -> p (b h) d", h=H)
                inv = rden[:, :, :].rearrange("p b h -> p (b h)")
                chain(dve.tensor_scalar(inv, sums[:, :, D], 1e-30, None, ALU.max))
                chain(dve.reciprocal(inv, inv))
                chain(dve.tensor_tensor(h[:, :, :].rearrange("p b (h d) -> p (b h) d", h=H), sums[:, :, 0:D],
                                        inv.unsqueeze(2).broadcast_to([P, NBLK * H, D]), ALU.mult))
                chain(dve.tensor_tensor(h[:, :, :], h[:, :, :], per_block(vec(f"L1_gnn_b{layer}")), ALU.add))
                chain(dve.tensor_scalar(h[:, :, :], h[:, :, :], 0.0, None, ALU.max))
                center_rows(h[:, :, :])
                chain(dve.tensor_tensor(h[:, :, :], h[:, :, :], per_feature(stat[:, 2, :]), ALU.mult))
                chain(dve.tensor_tensor(h[:, :, :], h[:, :, :], per_block(vec(f"L1_gnn_g{layer}")), ALU.mult))
                chain(dve.tensor_tensor(h[:, :, :], h[:, :, :], per_block(vec(f"L1_gnn_be{layer}")), ALU.add))

            if STOP >= 1:
                dve.wait_ge(weights_in, 16 * NWEIGHT)
                center_rows(x[:, :, :])
                project(0, relu_scaled, both_sides)
                dve.sem_inc(table_set, 1)
                attention_pass(1, 1)
                attention_nodes(1)
                project(1, as_is, both_sides)
                dve.sem_inc(table_set, 1)
                attention_pass(2, 2)
                attention_nodes(2)
                chain(dve.tensor_tensor(x[:, :, :], x[:, :, :], h[:, :, :], ALU.add))

            def gcn_tables(psum, b):
                dve.tensor_scalar(tab[:, b, :], psum[:, 0:F], dinv[:, 0, b], None, ALU.mult)
                return dve.tensor_scalar(xr[:, b, :], psum[:, F:2 * F], dinv[:, 1, b], None, ALU.mult)

            def gcn_side(own, side):
                chain(dve.tensor_tensor(own, own, acc[:, :, 0:F], ALU.add))
                chain(dve.tensor_tensor(own, own, per_feature(dinv[:, side, :]), ALU.mult))

            def mlp_tables(psum, b):
                dve.tensor_scalar(tab[:, b, :], psum[:, 0:F], 1.0, None, ALU.mult)
                return dve.tensor_tensor(own[:, b, :], psum[:, F:2 * F].unsqueeze(1),
                                         vec("L3_gnn_b1").unsqueeze(1), ALU.add)

            def mlp_pass(q):
                a0 = 2 * NG
                split_own()
                dve.wait_ge(table_out, 16 * (q + 1))
                chain(dve.memset(acc[:, :, :], 0.0))
                chain(dve.memset(attr, 0.0))
                dve.sem_inc(attr_set, 1)

                def heads(part):
                    return part.rearrange("p (n d) -> p n d", d=D)

                def per_head(col):
                    return col.unsqueeze(2).broadcast_to([P, G * H, D])

                def tiles(part):
                    return part.rearrange("p (t c) -> p t c", t=G)

                def center(at):
                    o, c = at.slot % 2, 4 * at.g
                    dve.wait_ge(rows_in[at.slot], 16 * G * (q * NU + at.turn + 1))
                    dve.wait_ge(spread, a0 + at.g + 1)
                    wait(dve, activated, at.g - 1)
                    dve.tensor_tensor(tiles(centered[:, o, :]), tiles(bank[2 + o][:, :]), rows[:, at.slot, :, 0:F],
                                      ALU.add).then_inc(sum_used, 1)
                    dve.wait_ge(sum_used, a0 + at.g + 1)
                    dve.tensor_reduce(mean[:, o, :], heads(centered[:, o, :]), AX, ALU.add).then_inc(edge_step, 1)
                    dve.wait_ge(edge_step, 3 * at.g + 1)
                    dve.tensor_scalar(mean[:, o, :], mean[:, o, :], 1.0 / D, None, ALU.mult).then_inc(edge_step, 1)
                    dve.wait_ge(edge_step, 3 * at.g + 2)
                    dve.tensor_tensor(heads(centered[:, o, :]), heads(centered[:, o, :]), per_head(mean[:, o, :]),
                                      ALU.subtract).then_inc(edge_step, 1)

                def normalise(at):
                    o, base = at.slot % 2, NORM_STEPS * at.g
                    done = [0]

                    def step(ins):
                        done[0] += 1
                        ins.then_inc(norm_step, 1)
                        dve.wait_ge(norm_step, base + done[0])

                    dve.wait_ge(squared, at.g + 1)
                    v_, y, t_ = var[:, o, :], inv[:, o, :], trial[:, o, :]
                    step(dve.tensor_reduce(v_, heads(square[:, o, :]), AX, ALU.add))
                    step(dve.tensor_scalar(v_, v_, 1.0 / D, EPS, ALU.mult, ALU.add))
                    step(dve.tensor_scalar(t_.bitcast(I32), v_.bitcast(I32), 1, None, ALU.arith_shift_right))
                    step(dve.tensor_scalar(y.bitcast(I32), t_.bitcast(I32), -1.0, float(0x5f3759df),
                                           ALU.mult, ALU.add))
                    for _ in range(3):
                        step(dve.tensor_tensor(t_, y, y, ALU.mult))
                        step(dve.scalar_tensor_tensor(out=t_, in0=t_, scalar=-0.5, in1=v_, op0=ALU.mult,
                                                      op1=ALU.mult))
                        step(dve.scalar_tensor_tensor(out=y, in0=t_, scalar=1.5, in1=y, op0=ALU.add, op1=ALU.mult))
                    z = centered[:, o, :]
                    step(dve.tensor_tensor(heads(z), heads(z), per_head(y), ALU.mult))
                    step(dve.tensor_tensor(tiles(z), tiles(z), vec("L3_gnn_gn_gamma").unsqueeze(1)
                                           .broadcast_to([P, G, F]), ALU.mult))
                    step(dve.tensor_tensor(tiles(z), tiles(z), vec("L3_gnn_gn_beta").unsqueeze(1)
                                           .broadcast_to([P, G, F]), ALU.add))
                    assert done[0] == NORM_STEPS

                def tick(at):
                    b, c, d = at.back(1), at.back(2), at.back(3)
                    if at.within(NG):
                        one_hot(q, 0, at, 1, onehot_b)
                    if c.within(NG):
                        normalise(c)
                    if b.within(NG):
                        center(b)
                    if d.within(NG):
                        add_sums(q, 0, d, F)
                ticks(dve, NG, 3, tick)
                dve.wait_ge(acc_ready, (q + 1) * NG)

            def sums_as_is(to, b):
                return dve.tensor_scalar(to.unsqueeze(1), acc[:, b, 0:F], 1.0, None, ALU.mult)

            def with_bias(psum, b):
                return dve.scalar_tensor_tensor(out=h[:, b, :], in0=vec("L3_gnn_b2").unsqueeze(1), scalar=deg_in[:, b],
                                                in1=psum[:, 0:F].unsqueeze(1), op0=ALU.mult, op1=ALU.add)

            if STOP >= 2:
                center_rows(x[:, :, :])
                chain(dve.tensor_scalar(dinv[:, 0, :], deg_in[:, :], 1.0, None, ALU.add))
                chain(dve.tensor_scalar(dinv[:, 1, :], deg_out[:, :], 1.0, None, ALU.add))
                dve.sem_inc(var_ready, 1)
                dve.wait_ge(sqrt_ready, centered_count[0] + 1)
                centered_count[0] += 1
                chain(dve.reciprocal(dinv[:, :, :], dinv[:, :, :]))
                project(2, relu_scaled, gcn_tables)
                dve.sem_inc(table_set, 2)
                chain(dve.memset(acc[:, :, :], 0.0))
                sum_pass(3, 0, 1)
                dve.wait_ge(acc_ready, 4 * NG)
                gcn_side(tab[:, :, :], 0)
                dve.wait_ge(table_out, 16 * 5)
                chain(dve.tensor_tensor(tab[:, :, :], tab[:, :, :], per_block(vec("L2_gnn_b_fwd")), ALU.add))
                chain(dve.memset(acc[:, :, :], 0.0))
                sum_pass(4, 1, 0)
                dve.wait_ge(acc_ready, 5 * NG)
                gcn_side(xr[:, :, :], 1)
                chain(dve.tensor_tensor(xr[:, :, :], xr[:, :, :], per_block(vec("L2_gnn_b_bwd")), ALU.add))
                chain(dve.tensor_tensor(xr[:, :, :], xr[:, :, :], tab[:, :, :], ALU.add))
                chain(dve.scalar_tensor_tensor(out=x[:, :, :], in0=xr[:, :, :], scalar=0.0, in1=x[:, :, :],
                                               op0=ALU.max, op1=ALU.add))
            if STOP >= 3:
                center_rows(x[:, :, :])
                project(3, relu_scaled, mlp_tables)
                dve.sem_inc(table_set, 1)
                mlp_pass(5)
                chain(dve.tensor_scalar(rcount[:, :], deg_in[:, :], 1.0, None, ALU.max))
                chain(dve.reciprocal(rcount[:, :], rcount[:, :]))
                project(4, sums_as_is, with_bias)
                chain(dve.tensor_tensor(h[:, :, :], h[:, :, :], per_feature(rcount[:, :]), ALU.mult))
                chain(dve.tensor_tensor(x[:, :, :], x[:, :, :], h[:, :, :], ALU.add))
            dve.sem_inc(final_set, 1)

        @block.scalar
        def _(act):
            def sqrt_rows(nth):
                act.wait_ge(var_ready, nth)
                nc.scalar.activation(stat[:, 0, :], stat[:, 1, :], ACT.Sqrt).then_inc(sqrt_ready, 1)

            def turn_rows(j):
                def tick(at):
                    act.wait_ge(turned, j * NBLK + at.g + 1)
                    wait(act, mult, j * NBLK + at.g - R + 1)
                    nc.scalar.copy(hs_t[:, at.short, :], bank[at.slot % 2][:, 0:F]).then_inc(turned_sb, 1)
                ticks(act, NBLK, 0, tick)

            def split_own(nth):
                for i in range(2):
                    act.wait_ge(own_rest, 2 * nth + i + 1)
                    nc.scalar.copy(own_parts[i], own).then_inc(own_part, 1)

            def wide_hot(q, at):
                a0 = {1: 0, 2: NG, 5: 2 * NG}[q]
                wait(act, agg_ready, q * NG + at.g - 1)
                act.wait_ge(onehot_ready, q * NG + at.g + 1)
                nc.scalar.copy(onehot_f[:, at.slot % 2, :, :], onehot_b[:, at.slot, :, :]).then_inc(hot_wide, 1)

            def attention_pass(q):
                a0 = (q - 1) * NG

                def hot(at):
                    o = at.slot % 2
                    act.wait_ge(turned_hot, a0 + at.g + 1)
                    wait(act, max_spread, a0 + at.g - R + 1)
                    nc.scalar.copy(hot_t[:, at.short, :], bank_b[o]).then_inc(turned_hot_sb, 1)

                def factors(at):
                    o = at.slot % 2
                    act.wait_ge(max_step, 6 * (a0 + at.g) + 5)
                    wait(act, acc_step, a0 + at.g - 1)
                    nc.scalar.activation(factor[:, o, :], drop[:, o, :], ACT.Exp).then_inc(factor_ready, 1)

                def weights(at):
                    o = at.slot % 2
                    act.wait_ge(shift_step, 2 * (a0 + at.g) + 2)
                    wait(act, agg_ready, q * NG + at.g - 1)
                    w = weighted[:, o, :].rearrange("p (n d) -> p n d", d=HD)
                    nc.scalar.activation(w[:, :, D], shifted[:, o, :, :].rearrange("p t h -> p (t h)"), ACT.Exp
                                         ).then_inc(weight_ready, 1)

                def score_rows(at):
                    act.wait_ge(score_turned, a0 + at.g + 1)
                    wait(act, seg_step, 3 * (a0 + at.g - 1))
                    nc.scalar.copy(turned_rows[:, at.slot % 2, :], bank[4][:, 0:2 * P]).then_inc(score_sb, 1)

                def last_part_1(at):
                    act.wait_ge(seg_turned, a0 + at.g + 1)
                    wait(act, max_ready, a0 + at.g - 1)
                    nc.scalar.copy(last_parts[:, at.slot % 2, 0, :].rearrange("p (t c) -> p t c", t=G),
                                   bank[5][:, 0:P].rearrange("p (t c) -> p t c", t=G)[:, :, 0:H + 1]
                                   ).then_inc(last_part, 1)

                def last_part_2(at):
                    o = at.slot % 2
                    act.wait_ge(last_left, 2 * (a0 + at.g) + 1)
                    nc.scalar.copy(last_parts[:, o, 1, :], last_rest[:, o, :]).then_inc(last_part, 1)

                def max_part_1(at):
                    o = at.slot % 2
                    act.wait_ge(max_step, 6 * (a0 + at.g) + 4)
                    wait(act, max_spread, a0 + at.g - 1)
                    nc.scalar.copy(max_parts[:, o, 0, :], newmax[:, o, :]).then_inc(max_part, 1)

                def max_part_2(at):
                    o = at.slot % 2
                    act.wait_ge(max_left, 2 * (a0 + at.g) + 1)
                    nc.scalar.copy(max_parts[:, o, 1, :], max_rest[:, o, :]).then_inc(max_part, 1)

                def widen(at):
                    wide_hot(q, at)

                def tick(at):
                    c, d, e = at.back(2), at.back(3), at.back(4)
                    if e.within(NG):
                        widen(e)
                    if c.within(NG):
                        score_rows(c)
                    if at.within(NG):
                        hot(at)
                    if e.within(NG):
                        weights(e)
                    if d.within(NG):
                        max_part_1(d)
                    if c.within(NG):
                        last_part_1(c)
                    if d.within(NG):
                        max_part_2(d)
                    if d.within(NG):
                        factors(d)
                    if c.within(NG):
                        last_part_2(c)
                ticks(act, NG, 4, tick)

            def mlp_pass(q):
                a0 = 2 * NG

                def turned_in(at):
                    o = at.slot % 2
                    act.wait_ge(turned_hot, a0 + at.g + 1)
                    wait(act, spread, a0 + at.g - 1)
                    nc.scalar.copy(hot_t[:, at.short, :], bank_b[o])
                    nc.scalar.copy(attr_t[:, o, :], bank[4][:, 0:P]).then_inc(turned_hot_sb, 1)

                def squares(at):
                    o = at.slot % 2
                    act.wait_ge(edge_step, 3 * (at.g + 1))
                    wait(act, norm_step, NORM_STEPS * (at.g - 1))
                    nc.scalar.activation(square[:, o, :], centered[:, o, :], ACT.Square).then_inc(squared, 1)

                def silus(at):
                    o = at.slot % 2
                    act.wait_ge(norm_step, NORM_STEPS * (at.g + 1))
                    wait(act, agg_ready, q * NG + at.g - 1)
                    nc.scalar.activation(silu[:, o, :], centered[:, o, :], ACT.Silu).then_inc(activated, 1)

                def tick(at):
                    b, c, d = at.back(1), at.back(2), at.back(3)
                    if d.within(NG):
                        wide_hot(q, d)
                    if at.within(NG):
                        turned_in(at)
                    if b.within(NG):
                        squares(b)
                    if c.within(NG):
                        silus(c)
                ticks(act, NG, 3, tick)

            sqrt_rows(1)
            if STOP >= 1:
                sqrt_rows(2)
                turn_rows(0)
                split_own(0)
                attention_pass(1)
                sqrt_rows(3)
                turn_rows(1)
                split_own(1)
                attention_pass(2)
                sqrt_rows(4)
            if STOP >= 2:
                sqrt_rows(5)
                act.wait_ge(var_ready, 6)
                nc.scalar.activation(dinv[:, :, :], dinv[:, :, :], ACT.Sqrt).then_inc(sqrt_ready, 1)
                turn_rows(2)
            if STOP >= 3:
                sqrt_rows(7)
                turn_rows(3)
                split_own(2)
                mlp_pass(5)
                turn_rows(4)

        @block.tensor
        def _(pe):
            pe.wait_ge(consts_pool, 5)
            pe.wait_ge(ident_ready, 1)

            def prefixes(k):
                pe.wait_ge(counts_ready, k + 1)
                wait(pe, prefix_used, k)
                nc.tensor.matmul(counts_ps, ones[:, :], cnt[:, :], start=True, stop=True)
                nc.tensor.matmul(prefix_ps, tri[:, :], cnt[:, :], start=True, stop=True).then_inc(prefix_ready, 1)

            def sum_groups(q, at, width):
                turn = q * (NG // U) + at.turn
                pe.wait_ge(rows_in[at.slot], 16 * G * (turn + 1))
                pe.wait_ge(onehot_ready, q * NG + at.g + 1)
                wait(pe, acc_ready, q * NG + at.g)
                for t in range(G):
                    mm = nc.tensor.matmul(agg[:, 0:width], onehot[:, at.slot, t, :], rows[:, at.slot, t, 0:width],
                                          start=(t == 0), stop=(t == G - 1))
                mm.then_inc(agg_ready, 1)

            def histogram(turn):
                pe.wait_ge(hist_hot, 2 * turn + 2)
                for c in range(HC):
                    mm = nc.tensor.matmul(hist_ps, hist_lo[:, c, :], hist_hi[:, c, :],
                                          start=(isinstance(turn, int) and turn == 0 and c == 0),
                                          stop=(isinstance(turn, int) and turn == NG // R - 1 and c == HC - 1),
                                          skip_group_check=True)
                mm.then_inc(hist_mm, 1)

            def sum_pass(q, extra=None):
                def tick(at):
                    if at.within(NG):
                        sum_groups(q, at, F + 1)
                        if extra is not None and at.short == 0:
                            extra(at.short_turn)
                ticks(pe, NG, 0, tick)

            def project(j, width):
                def tick(at):
                    if at.within(NBLK):
                        pe.wait_ge(hs_ready, j * NBLK + at.g + 1)
                        wait(pe, turned_sb, j * NBLK + at.g - 1)
                        nc.tensor.transpose(bank[at.slot % 2][:, 0:F], hs[:, at.short, :], ident[:, :]
                                            ).then_inc(turned, 1)
                    b = at.back(1)
                    if b.within(NBLK):
                        pe.wait_ge(turned_sb, j * NBLK + b.g + 1)
                        wait(pe, mult_used, j * NBLK + b.g - 1)
                        w = w_out[:, :] if j == 4 else w_pair[:, j, :]
                        nc.tensor.matmul(bank[2 + b.slot % 2][:, 0:width], hs_t[:, b.short, :], w,
                                         start=True, stop=True).then_inc(mult, 1)
                ticks(pe, NBLK, 1, tick)

            def attention_pass(q):
                a0 = (q - 1) * NG

                def turn_hots(at):
                    pe.wait_ge(onehot_ready, q * NG + at.g + 1)
                    wait(pe, turned_hot_sb, a0 + at.g - 1)
                    for t in range(G):
                        mm = nc.tensor.transpose(bank_b[at.slot % 2][:, t * P:(t + 1) * P], onehot_b[:, at.slot, t, :],
                                                 ident_b[:, :])
                    mm.then_inc(turned_hot, 1)

                def spread_maximum(at):
                    o = at.slot % 2
                    pe.wait_ge(max_left, 2 * (a0 + at.g) + 2)
                    wait(pe, shift_step, 2 * (a0 + at.g) - 1)
                    for t in range(G):
                        for i in range(3):
                            mm = nc.tensor.matmul(bank[6][:, t * H:(t + 1) * H], hot_t[:, at.short, t * P:(t + 1) * P],
                                                  max_parts[:, o, i, :], start=(i == 0), stop=(i == 2))
                    mm.then_inc(max_spread, 1)

                def spread_targets(at):
                    o = at.slot % 2
                    blk = pe.value_load(gblk_i[0][0:1, bass.ds(at.g, 1)], min_val=0, max_val=NBLK - 1)
                    pe.wait_ge(turned_hot_sb, a0 + at.g + 1)
                    wait(pe, sum_used, a0 + at.g - 1)
                    for t in range(G):
                        for i in range(3):
                            mm = nc.tensor.matmul(bank[2 + o][:, t * P:(t + 1) * P],
                                                  hot_t[:, at.short, t * P:(t + 1) * P],
                                                  own_parts[i][:, bass.ds(blk, 1), :], start=(i == 0), stop=(i == 2))
                    mm.then_inc(spread, 1)

                def turn_scores(at):
                    o = at.slot % 2
                    pe.wait_ge(keys_ready, a0 + at.g + 1)
                    pe.wait_ge(score_step, 3 * (a0 + at.g) + 3)
                    wait(pe, score_sb, a0 + at.g)
                    nc.tensor.transpose(bank[4][:, 0:P], steps[:, o, :], ident[:, :])
                    nc.tensor.transpose(bank[4][:, P:2 * P], score[:, at.short, :], ident[:, :]).then_inc(score_turned, 1)

                def sum_weighted(at):
                    pe.wait_ge(weighted_ready, a0 + at.g + 1)
                    wait(pe, acc_ready, q * NG + at.g)
                    pe.wait_ge(hot_wide, a0 + at.g + 1)
                    for t in range(G):
                        mm = nc.tensor.matmul(agg, onehot_f[:, at.slot % 2, t, :],
                                              weighted[:, at.slot % 2, t * H * HD:(t + 1) * H * HD],
                                              start=(t == 0), stop=(t == G - 1))
                    mm.then_inc(agg_ready, 1)

                def turn_last(at):
                    o = at.slot % 2
                    pe.wait_ge(seg_step, 3 * (a0 + at.g) + 3)
                    wait(pe, max_step, 6 * (a0 + at.g - 1) + 2)
                    nc.tensor.transpose(bank[5][:, 0:P], at_last[:, o, :], ident[:, :]).then_inc(seg_turned, 1)

                def node_maximum(at):
                    o = at.slot % 2
                    pe.wait_ge(last_left, 2 * (a0 + at.g) + 2)
                    for t in range(G):
                        for i in range(3):
                            mm = nc.tensor.matmul(bank[5][:, P + 16 * t:P + 16 * t + H + 1], onehot_b[:, at.slot, t, :],
                                                  last_parts[:, o, i, t * (H + 1):(t + 1) * (H + 1)],
                                                  start=(i == 0), stop=(i == 2))
                    mm.then_inc(max_ready, 1)

                def tick(at):
                    c, d, e = at.back(2), at.back(3), at.back(4)
                    if c.within(NG):
                        turn_scores(c)
                    if at.within(NG):
                        turn_hots(at)
                    if at.within(NG):
                        spread_targets(at)
                    if c.within(NG):
                        turn_last(c)
                    if e.within(NG):
                        sum_weighted(e)
                    if c.within(NG):
                        node_maximum(c)
                    if d.within(NG):
                        spread_maximum(d)
                ticks(pe, NG, 4, tick)

            def mlp_pass(q):
                a0 = 2 * NG

                def turn_hots(at):
                    pe.wait_ge(onehot_ready, q * NG + at.g + 1)
                    pe.wait_ge(attr_in[at.short], 16 * (at.short_turn + 1))
                    wait(pe, turned_hot_sb, a0 + at.g)
                    nc.tensor.transpose(bank[4][:, 0:P], attr[:, at.short, :], ident[:, :]).then_inc(attr_free, 1)
                    for t in range(G):
                        mm = nc.tensor.transpose(bank_b[at.slot % 2][:, t * P:(t + 1) * P], onehot_b[:, at.slot, t, :],
                                                 ident_b[:, :])
                    mm.then_inc(turned_hot, 1)

                def spread_targets(at):
                    o = at.slot % 2
                    blk = pe.value_load(gblk_i[0][0:1, bass.ds(at.g, 1)], min_val=0, max_val=NBLK - 1)
                    pe.wait_ge(turned_hot_sb, a0 + at.g + 1)
                    wait(pe, sum_used, a0 + at.g - 1)
                    for t in range(G):
                        for i in range(3):
                            nc.tensor.matmul(bank[2 + o][:, t * P:(t + 1) * P], hot_t[:, at.short, t * P:(t + 1) * P],
                                             own_parts[i][:, bass.ds(blk, 1), :], start=(i == 0), stop=False)
                        mm = nc.tensor.matmul(bank[2 + o][:, t * P:(t + 1) * P], attr_t[:, o, :], w_attr[:, t, :],
                                              start=False, stop=True)
                    mm.then_inc(spread, 1)

                def sum_activated(at):
                    pe.wait_ge(activated, at.g + 1)
                    wait(pe, acc_ready, q * NG + at.g)
                    pe.wait_ge(hot_wide, a0 + at.g + 1)
                    for t in range(G):
                        mm = nc.tensor.matmul(agg[:, 0:F], onehot_f[:, at.slot % 2, t, :],
                                              silu[:, at.slot % 2, t * F:(t + 1) * F],
                                              start=(t == 0), stop=(t == G - 1))
                    mm.then_inc(agg_ready, 1)

                def tick(at):
                    d = at.back(3)
                    if at.within(NG):
                        turn_hots(at)
                    if d.within(NG):
                        sum_activated(d)
                    if at.within(NG):
                        spread_targets(at)
                ticks(pe, NG, 3, tick)

            prefixes(0)
            prefixes(1)
            sum_pass(0, histogram)
            if STOP >= 1:
                pe.wait_ge(weights_in, 16 * NWEIGHT)
                project(0, 2 * F)
                attention_pass(1)
                project(1, 2 * F)
                attention_pass(2)
            if STOP >= 2:
                project(2, 2 * F)
                sum_pass(3)
                sum_pass(4)
            if STOP >= 3:
                project(3, 2 * F)
                mlp_pass(5)
                project(4, F)


INPUTS = ["x", "edge_attr_4", "L1_gnn_Wl1", "L1_gnn_Wr1", "L1_gnn_Wl2", "L1_gnn_Wr2", "L2_gnn_W_fwd", "L2_gnn_W_bwd",
          "L3_gnn_W1", "L3_gnn_W2"] + VECS


def kernel(**inputs):
    import numpy as np
    import concourse.bacc as bacc
    from concourse.bass_utils import run_bass_kernel_spmd as run

    nc = bacc.Bacc("TRN2", target_bir_lowering=False, num_devices=1)
    arrays = {"edges": np.ascontiguousarray(np.stack([inputs["src"], inputs["dst"]], axis=1))}
    arrays.update({name: np.ascontiguousarray(inputs[name]) for name in INPUTS})
    given = {name: nc.dram_tensor(f"in_{name}", array.shape, mybir.dt.from_np(array.dtype), kind="ExternalInput").ap()
             for name, array in arrays.items()}
    out = nc.dram_tensor("out", (N, F), F32, kind="ExternalOutput").ap()
    build(nc, given, out)
    result = run(nc, [{f"in_{name}": array for name, array in arrays.items()}], core_ids=[0])
    return result.results[0]["out"]
```

```python
from contextlib import ExitStack

import concourse.bass as bass
from concourse import mybir

F32 = mybir.dt.float32
I32 = mybir.dt.int32
BF16 = mybir.dt.bfloat16
ALU = mybir.AluOpType
ACT = mybir.ActivationFunctionType
AX = mybir.AxisListType.X

P = 128
N = 6250
F = 128
E = 106250
NBLK = -(-N // P)
NPAD = NBLK * P
G = 4
GE = G * P
NG = (E + NBLK * (GE - 1)) // GE
U = 8
R = 4
NCOL = 832
LASTP = E // NCOL
LASTC = E - LASTP * NCOL
NBUK = NBLK + 1
EPAD = P * NCOL + P * 5
PADT = 8191
H = 8
D = F // H
HD = D + 1
EPS = 1e-5
SLOPE = 0.2
BIG = 1e30
STEPB = float(2 ** 96)


HC = NCOL // (NG // R)
PADR = 5
VECS = ("L1_gnn_att1 L1_gnn_b1 L1_gnn_g1 L1_gnn_be1 L1_gnn_att2 L1_gnn_b2 L1_gnn_g2 L1_gnn_be2 "
        "L2_gnn_b_fwd L2_gnn_b_bwd L3_gnn_b1 L3_gnn_gn_gamma L3_gnn_gn_beta L3_gnn_b2").split()
NVEC = len(VECS)
NWEIGHT = 9 + G + NVEC
NEWTON = 12
PARTS = 7
PBLK = NBLK // PARTS
NU = NG // U


class At:

    def __init__(self, turn, slot):
        self.turn, self.slot, self.g = turn, slot, turn * U + slot
        self.short = slot % R
        self.short_turn = turn * (U // R) + slot // R
        self.half = turn * (U // 2) + slot // 2

    def back(self, lag):
        return At(self.turn + (self.slot - lag) // U, (self.slot - lag) % U)

    def within(self, n):
        return not isinstance(self.g, int) or 0 <= self.g < n


def ticks(eng, n, lag, tick):
    for t in range(U):
        tick(At(0, t))
    with eng.Fori(1, n // U) as turn:
        for u in range(U):
            tick(At(turn, u))
    for t in range(n // U * U, n + lag):
        tick(At(t // U, t % U))


def wait(eng, sem, value):
    if not isinstance(value, int) or value > 0:
        eng.wait_ge(sem, value)


class Chain:

    def __init__(self, eng, sem):
        self.eng, self.sem, self.done, self.turns = eng, sem, 0, None

    def __call__(self, ins):
        ins.then_inc(self.sem, 1)
        self.done += 1
        self.eng.wait_ge(self.sem, self.done if self.turns is None else self.turns + self.done)

    def enter(self, i, per):
        self.turns = i * per

    def leave(self, n, per):
        self.turns = None
        self.done += (n - 1) * per


def build(nc, a, out):
    with ExitStack() as ctx:
        def sb(name, shape, dt=F32):
            return ctx.enter_context(nc.sbuf_tensor(name, shape, dt))

        def ps(name, shape, dt=F32):
            return ctx.enter_context(nc.psum_tensor(name, shape, dt))

        def sem(name):
            return ctx.enter_context(nc.semaphore(name))

        def dram(name, shape, dt=F32):
            return nc.dram_tensor(name, shape, dt, kind="Internal").ap()

        edges_by = [dram("edges_by_dst", (EPAD, 2), I32),
                    dram("edges_by_src", (EPAD, 2), I32)]
        attr_by_dst = dram("attr_by_dst", (EPAD, 4))
        half_sorted = [dram("half_sorted_edges", (P * NCOL, 2), I32), dram("half_sorted_attr", (P * NCOL, 4))]
        table = [dram(f"table{q}", (NPAD, F)) for q in range(6)]

        x = sb("x", [P, NBLK, F])
        h = sb("h", [P, NBLK, F])
        tab = sb("tab", [P, NBLK, F])
        xr = sb("xr", [P, NBLK, F])
        acc = sb("acc", [P, NBLK, H * HD])
        nmax = sb("nmax", [P, NBLK, H])
        rden = sb("rden", [P, NBLK, H])
        stat = sb("stat", [P, 3, NBLK])
        deg_in = sb("deg_in", [P, NBLK])
        deg_out = sb("deg_out", [P, NBLK])
        dinv = sb("dinv", [P, 2, NBLK])
        ident = sb("ident", [P, P])
        ident_b = sb("ident_b", [P, P], BF16)
        tri = sb("tri", [P, P])
        ones = sb("ones", [P, P])
        iota_n = sb("iota_n", [P, P])
        iota_g = sb("iota_g", [P, NG])
        w_pair = sb("w_pair", [P, 4, 2 * F])
        w_attr = sb("w_attr", [P, G, F])
        w_out = sb("w_out", [P, F])
        vecs = sb("vecs", [P, NVEC, F])
        edge_in = sb("edge_in", [P, NCOL, 2], I32)
        rank = sb("rank", [P, NCOL])
        spare = xr[:, :, :].rearrange("p b f -> p (b f)")
        key_i, key, lo, hot, pos, ones_row = [spare[:, i * NCOL:(i + 1) * NCOL] for i in range(6)]
        key_i = key_i.bitcast(I32)
        pos_win = sb("pos_win", [P, HC], I32)
        rec_win = sb("rec_win", [P, HC, 2], I32)
        next_first = sb("next_first", [P, 2], I32)
        disorder = sb("disorder", [P, 1])
        disorder_i = sb("disorder_i", [P, 1], I32)
        mean = sb("mean", [P, G * H])
        var = sb("var", [P, 2, G * H])
        inv = sb("inv", [P, 2, 2, G * H])
        trial = sb("trial", [P, 2, G * H])
        rcount = sb("rcount", [P, NBLK])
        cnt = sb("cnt", [P, NBUK])
        btot = sb("btot", [P, NBUK])
        bincl = sb("bincl", [P, NBUK])
        bbase = sb("bbase", [P, NG // R])
        bgrp_i = sb("bgrp_i", [P, NBUK], I32)
        bgrp = sb("bgrp", [P, NBUK])
        bend = sb("bend", [P, NBUK])
        bdelta = sb("bdelta", [P, NBUK])
        bend_t = sb("bend_t", [P, P])
        bdelta_t = sb("bdelta_t", [P, P])
        past = sb("past", [P, NG])
        gstart = sb("gstart", [P, NG])
        gbase = [sb(f"gbase{k}", [P, NG]) for k in range(2)]
        gblk_i = [sb(f"gblk_i{k}", [P, NG], I32) for k in range(2)]
        gstart_i = [sb(f"gstart_i{k}", [P, NG], I32) for k in range(2)]
        hist_lo = sb("hist_lo", [P, HC, P], BF16)
        hist_hi = sb("hist_hi", [P, HC, NBLK], BF16)
        pad_rows = sb("pad_rows", [P, 2, PADR, 2], I32)
        pad_attr = sb("pad_attr", [P, PADR, 4])
        rec = sb("rec", [P, U, G, 2], I32)
        rows = sb("rows", [P, U, G, F + 1])
        tloc = sb("tloc", [P, U, G])
        h_flat = h[:, :, :].rearrange("p b f -> p (b f)")
        onehot = h_flat[:, 0:U * GE].rearrange("p (u t n) -> p u t n", u=U, t=G)
        onehot_b = h_flat[:, 0:U * GE // 2].bitcast(BF16).rearrange("p (u t n) -> p u t n", u=U, t=G)
        onehot_f = h_flat[:, U * GE // 2:(U // 2 + 2) * GE].rearrange("p (u t n) -> p u t n", u=2, t=G)
        xr_flat = xr[:, :, :].rearrange("p b f -> p (b f)")
        half = NBLK * F // 2
        own_parts = [part.bitcast(BF16).rearrange("p (b f) -> p b f", f=F) for part in (
            xr_flat[:, 0:half], xr_flat[:, half:], h_flat[:, (U // 2 + 2) * GE:(U // 2 + 2) * GE + half])]
        own = acc[:, :, :].rearrange("p b f -> p (b f)")[:, 0:NBLK * F].rearrange("p (b f) -> p b f", f=F)

        hs = sb("hs", [P, R, F])
        hs_t = sb("hs_t", [P, R, F])
        gmax = sb("gmax", [P, 2, H])
        gseen = sb("gseen", [P, 2, G])
        gtile = sb("gtile", [P, 2, G, H])
        newmax = sb("newmax", [P, 2, H])
        max_parts = sb("max_parts", [P, 2, 3, H], BF16)
        max_rest = sb("max_rest", [P, 2, H])
        last_parts = sb("last_parts", [P, 2, 3, G * (H + 1)], BF16)
        drop = sb("drop", [P, 2, H])
        factor = sb("factor", [P, 2, H])
        shifted = sb("shifted", [P, 2, G, H])
        bank = [ps(f"bank{k}", [P, 512]) for k in range(8)]

        (consts_pool, weights_in, x_in, edges_in, edges_set, dst_copied, pads_set, pads_out, v, counts_ready,
         prefix_ready, prefix_used, group_step, group_mm, groups_ready, rank_done, hist_hot, hist_mm, scattered,
         table_set, hs_ready, turned, turned_sb, mult, mult_used, tick_mark, onehot_ready, tloc_ready, agg_ready,
         acc_ready, var_ready, sqrt_ready, final_set, stored) = [sem(n) for n in (
             "consts_pool weights_in x_in edges_in edges_set dst_copied pads_set pads_out v counts_ready "
             "prefix_ready prefix_used group_step group_mm groups_ready rank_done hist_hot hist_mm scattered "
             "table_set hs_ready turned turned_sb mult mult_used tick_mark onehot_ready tloc_ready agg_ready "
             "acc_ready var_ready sqrt_ready final_set stored").split()]
        (keys_ready, turned_hot, turned_hot_sb, spread, sum_used, score_step, score_turned, score_sb,
         seg_step, seg_turned, max_ready, max_step, max_spread, shift_step, factor_ready, weight_ready,
         weighted_ready, acc_step) = [sem(n) for n in (
             "keys_ready turned_hot turned_hot_sb spread sum_used score_step score_turned score_sb "
             "seg_step seg_turned max_ready max_step max_spread shift_step factor_ready weight_ready "
             "weighted_ready acc_step").split()]
        (own_rest, own_part, last_part, last_left, max_part, max_left, hot_wide, ident_ready) = [sem(n) for n in (
             "own_rest own_part last_part last_left max_part max_left hot_wide ident_ready").split()]
        (win_free, attr_set, w_centered, var_step, newton_step, squared, norm_step, activated, attr_free, out_step) = [sem(n) for n in (
             "win_free attr_set w_centered var_step newton_step squared norm_step activated attr_free out_step").split()]
        (bucket_counted, part_centered, part_squared, next_in, order_counted, order_summed, order_known, sort_step, sort_padded, sort_loaded, sort_counted,
         sort_prefixed, sort_ranked, sort_window, sort_edges_out, sort_attr_out) = [sem(n) for n in (
             "bucket_counted part_centered part_squared next_in order_counted order_summed order_known sort_step sort_padded sort_loaded sort_counted "
             "sort_prefixed sort_ranked sort_window sort_edges_out sort_attr_out").split()]
        table_out = [sem(f"table_out{q}") for q in range(6)]
        attr_in = [sem(f"attr_in{u}") for u in range(R)]
        rec_in = [sem(f"rec_in{u}") for u in range(U)]
        rows_in = [sem(f"rows_in{u}") for u in range(U)]

        block = ctx.enter_context(nc.Block())

        flat = tab[:, :, :].rearrange("p b f -> p (b f)")
        area, place = [0], [flat]

        def ring(*shape):
            size = 1
            for n in shape:
                size *= n
            part = place[0][:, area[0]:area[0] + size]
            area[0] += size
            return part.rearrange("p (u n) -> p u n", u=shape[0])

        hot_t = ring(R, GE // 2).bitcast(BF16)
        both = ring(1, GE)
        weighted = ring(2, G * H * HD)
        score = ring(R, G * 32)
        steps = ring(2, G * 32)
        turned_rows = ring(2, 2 * P)
        fence = ring(2, P + 2)
        running = ring(2, P)
        at_last = ring(2, P)
        last_rest = ring(2, G * (H + 1))
        assert area[0] <= NBLK * F
        area[0], place[0] = 0, flat
        ring(R, GE // 2)
        centered = ring(R, GE)
        square = ring(2, GE)
        silu = ring(2, GE)
        attr = ring(R, G * 32)
        attr_t = ring(2, P)
        assert area[0] <= NBLK * F
        acc_flat = acc[:, :, :].rearrange("p b f -> p (b f)")
        sort_edges = acc_flat[:, 0:2 * NCOL].bitcast(I32).rearrange("p (c k) -> p c k", k=2)
        sort_attr = acc_flat[:, 2 * NCOL:6 * NCOL].rearrange("p (c k) -> p c k", k=4)
        digit_cnt, digit_tot, digit_incl, digit_base = [flat[:, i * P:(i + 1) * P] for i in range(4)]
        attr_win = flat[:, 4 * P:4 * P + 4 * HC].rearrange("p (c k) -> p c k", k=4)
        counts_ps, prefix_ps, hist_ps = bank[0][:, 0:NBUK], bank[1][:, 0:NBUK], bank[6][:, 0:NBLK]
        bank_b = [bank[k][:, 0:GE // 2].bitcast(BF16) for k in range(2)]
        agg = bank[7][:, 0:H * HD]

        def vec(name):
            return vecs[:, VECS.index(name), :]

        def per_block(row):
            return row.unsqueeze(1).broadcast_to([P, NBLK, F])

        def per_feature(col):
            return col.unsqueeze(2).broadcast_to([P, NBLK, F])

        @block.sync
        def _(sp):
            weights = [(w_pair[:, 0, 0:F], a["L1_gnn_Wl1"]), (w_pair[:, 0, F:2 * F], a["L1_gnn_Wr1"]),
                       (w_pair[:, 1, 0:F], a["L1_gnn_Wl2"]), (w_pair[:, 1, F:2 * F], a["L1_gnn_Wr2"]),
                       (w_pair[:, 2, 0:F], a["L2_gnn_W_fwd"]), (w_pair[:, 2, F:2 * F], a["L2_gnn_W_bwd"]),
                       (w_pair[:, 3, 0:F], a["L3_gnn_W1"][F:2 * F, :]), (w_pair[:, 3, F:2 * F], a["L3_gnn_W1"][0:F, :]),
                       (w_out[:, :], a["L3_gnn_W2"])]
            weights += [(w_attr[32 * t:32 * t + 4, t, :], a["L3_gnn_W1"][2 * F:2 * F + 4, :]) for t in range(G)]
            weights += [(vecs[:, i, :], (a[name].rearrange("h d -> (h d)") if "att" in name else a[name])
                         .unsqueeze(0).broadcast_to([P, F])) for i, name in enumerate(VECS)]
            assert len(weights) == NWEIGHT
            sp.wait_ge(pads_set, 1)
            sp.dma_start(next_first[0:LASTP, :], a["edges"][0:LASTP * NCOL + 1, 0:2][NCOL::NCOL, :]
                         ).then_inc(next_in, 16)
            sp.dma_start(edge_in[0:LASTP, :, :], a["edges"][0:LASTP * NCOL, :].rearrange("(p c) k -> p c k", c=NCOL)
                         ).then_inc(edges_in, 16)
            sp.dma_start(edge_in[LASTP:LASTP + 1, 0:LASTC, :],
                         a["edges"][LASTP * NCOL:E, :].unsqueeze(0)).then_inc(edges_in, 16)
            sp.dma_start(x[:, 0:NBLK - 1, :], a["x"][0:(NBLK - 1) * P, :].rearrange("(b p) f -> p b f", p=P)
                         ).then_inc(x_in, 16)
            sp.dma_start(x[0:N - (NBLK - 1) * P, NBLK - 1, :], a["x"][(NBLK - 1) * P:N, :]).then_inc(x_in, 16)
            sp.dma_start(edges_by[0][E:E + P * PADR, :].rearrange("(p r) k -> p r k", p=P),
                         pad_rows[:, 0, :, :]).then_inc(pads_out, 16)
            sp.dma_start(edges_by[1][P * NCOL:EPAD, :].rearrange("(p r) k -> p r k", p=P),
                         pad_rows[:, 1, :, :]).then_inc(pads_out, 16)
            sp.dma_start(attr_by_dst[E:E + P * PADR, :].rearrange("(p r) k -> p r k", p=P),
                         pad_attr[:, :, :]).then_inc(pads_out, 16)
            for to, of in weights:
                sp.dma_start(to, of).then_inc(weights_in, 16)
            sp.wait_ge(pads_out, 48)

            def load_unsorted():
                sp.wait_ge(sort_padded, 1)
                for to, of in ((sort_edges, a["edges"]), (sort_attr, a["edge_attr_4"])):
                    sp.dma_start(to[0:LASTP, :, :], of[0:LASTP * NCOL, :].rearrange("(p c) k -> p c k", c=NCOL)
                                 ).then_inc(sort_loaded, 16)
                    sp.dma_start(to[LASTP:LASTP + 1, 0:LASTC, :], of[LASTP * NCOL:E, :].unsqueeze(0)
                                 ).then_inc(sort_loaded, 16)
                sp.wait_ge(sort_edges_out, 16 * NCOL)
                sp.wait_ge(sort_attr_out, 16 * NCOL)
                for to, of in zip((sort_edges, sort_attr), half_sorted):
                    sp.dma_start(to, of.rearrange("(p c) k -> p c k", c=NCOL)).then_inc(sort_loaded, 16)
                sp.wait_ge(sort_edges_out, 2 * 16 * NCOL)
                sp.wait_ge(sort_attr_out, 2 * 16 * NCOL)

            sp.wait_ge(order_known, 1)
            unsorted = sp.value_load(disorder_i[0:1, 0:1], min_val=0, max_val=E)
            with sp.If(unsorted > 0):
                load_unsorted()
            with sp.Else():
                sp.dma_start(edges_by[0][0:E, :], a["edges"]).then_inc(dst_copied, 16)
                sp.dma_start(attr_by_dst[0:E, :], a["edge_attr_4"]).then_inc(dst_copied, 16)
                sp.wait_ge(dst_copied, 32)

            def store_table(q, staged, projection=None):
                if projection is None:
                    sp.wait_ge(table_set, 1)
                for part in range(PARTS):
                    if projection is not None:
                        sp.wait_ge(mult_used, projection * NBLK + (part + 1) * PBLK)
                    blocks = slice(part * PBLK, (part + 1) * PBLK)
                    sp.dma_start(table[q].rearrange("(b p) f -> p b f", p=P)[:, blocks, :], staged[:, blocks, :]
                                 ).then_inc(table_out[q], 16)

            def edge_records(q, k, with_attr=False):
                sp.wait_ge(groups_ready, k + 1)

                def tick(at):
                    wait(sp, agg_ready, q * NG + at.g - U + 1)
                    first = sp.value_load(gstart_i[k][0:1, bass.ds(at.g, 1)], min_val=0, max_val=E)
                    sp.dma_start(rec[:, at.slot, :, :],
                                 edges_by[k][bass.ds(first, GE), :].rearrange("(p t) k -> p t k", t=G)
                                 ).then_inc(rec_in[at.slot], 16)
                    if with_attr:
                        wait(sp, attr_free, at.g - R + 1)
                        sp.dma_start(attr[:, at.short, :].rearrange("p (t c) -> p t c", t=G)[:, :, 0:4],
                                     attr_by_dst[bass.ds(first, GE), :].rearrange("(p t) k -> p t k", t=G)
                                     ).then_inc(attr_in[at.short], 16)
                ticks(sp, NG, 0, tick)

            store_table(0, tab)
            edge_records(0, 0)
            for q in (1, 2):
                store_table(q, tab, q - 1)
                edge_records(q, 0)
            store_table(3, tab, 2)
            store_table(4, xr, 2)
            edge_records(3, 0)
            sp.wait_ge(scattered, 16 * NCOL)
            edge_records(4, 1)
            store_table(5, tab, 3)
            sp.wait_ge(attr_set, 1)
            edge_records(5, 0, True)
            for part in range(PARTS):
                sp.wait_ge(final_set, part + 1)
                first, last = part * PBLK, min((part + 1) * PBLK, NBLK - 1)
                sp.dma_start(out[first * P:last * P, :].rearrange("(b p) f -> p b f", p=P), x[:, first:last, :]
                             ).then_inc(stored, 16)
            sp.dma_start(out[(NBLK - 1) * P:N, :], x[0:N - (NBLK - 1) * P, NBLK - 1, :]).then_inc(stored, 16)
            sp.wait_ge(stored, 16 * (PARTS + 1))

        @block.gpsimd
        def _(pool):
            nc.gpsimd.iota(iota_n[:, :], [[1, P]], base=0, channel_multiplier=0,
                           allow_small_or_imprecise_dtypes=True).then_inc(consts_pool, 1)
            nc.gpsimd.iota(iota_g[:, :], [[1, NG]], base=0, channel_multiplier=0,
                           allow_small_or_imprecise_dtypes=True).then_inc(consts_pool, 1)
            nc.gpsimd.memset(ones[:, :], 1.0).then_inc(consts_pool, 1)
            pool.wait_ge(consts_pool, 3)
            nc.gpsimd.affine_select(out=ident[:, :], in_=ones[:, :], compare_op=ALU.is_equal, fill=0.0, base=0,
                                    pattern=[[-1, P]], channel_multiplier=1).then_inc(consts_pool, 1)
            nc.gpsimd.affine_select(out=tri[:, :], in_=ones[:, :], compare_op=ALU.is_gt, fill=0.0, base=0,
                                    pattern=[[1, P]], channel_multiplier=-1).then_inc(consts_pool, 1)

            def scatter_sorted():
                for digit, (edges_to, attr_to) in enumerate((half_sorted, (edges_by[0], attr_by_dst))):
                    pool.wait_ge(sort_ranked, digit + 1)
                    with pool.Fori(0, NCOL // HC) as turn:
                        done = turn + digit * (NCOL // HC)
                        cols = bass.ds(turn * HC, HC)
                        nc.gpsimd.tensor_copy(pos_win[:, :], rank[:, cols]).then_inc(sort_window, 1)
                        nc.gpsimd.tensor_copy(rec_win[:, :, :], sort_edges[:, cols, :]).then_inc(sort_window, 1)
                        nc.gpsimd.tensor_copy(attr_win[:, :, :], sort_attr[:, cols, :]).then_inc(sort_window, 1)
                        pool.wait_ge(sort_window, 3 * done + 3)
                        pool.sem_inc(tick_mark, 1)
                        for c in range(HC):
                            place = bass.IndirectOffsetOnAxis(pos_win[:, c:c + 1], 0)
                            pool.indirect_dma_start(edges_to, place, rec_win[:, c, :], None).then_inc(sort_edges_out, 16)
                            pool.indirect_dma_start(attr_to, place, attr_win[:, c, :], None).then_inc(sort_attr_out, 16)
                        pool.wait_ge(sort_edges_out, 16 * HC * (done + 1))
                        pool.wait_ge(sort_attr_out, 16 * HC * (done + 1))
                        pool.sem_inc(tick_mark, 1)

            pool.wait_ge(order_known, 1)
            unsorted = pool.value_load(disorder_i[0:1, 0:1], min_val=0, max_val=E)
            with pool.If(unsorted > 0):
                scatter_sorted()

            def scatter_columns(q, at):
                turn = at.turn + (q - 1) * (NG // U)
                if at.slot == 0:
                    wait(pool, scattered, 16 * HC * turn)
                    if isinstance(turn, int):
                        pool.wait_ge(rank_done, 4 * (NG // R))
                    pool.sem_inc(tick_mark, 1)
                    cols = bass.ds(turn * HC, HC)
                    nc.gpsimd.tensor_copy(pos_win[:, :], rank[:, cols]).then_inc(win_free, 1)
                    nc.gpsimd.tensor_copy(rec_win[:, :, :], edge_in[:, cols, :]).then_inc(win_free, 1)
                    pool.wait_ge(win_free, 2 * turn + 2)
                    pool.sem_inc(tick_mark, 1)
                for c in range(at.slot * HC // U, (at.slot + 1) * HC // U):
                    pool.indirect_dma_start(edges_by[1], bass.IndirectOffsetOnAxis(pos_win[:, c:c + 1], 0),
                                            rec_win[:, c, :], None).then_inc(scattered, 16)

            def gathers(q, gathered_end, beside=None):
                pool.wait_ge(table_out[q], 16 * PARTS)

                def tick(at):
                    turn = q * (NG // U) + at.turn
                    wait(pool, agg_ready, q * NG + at.g - U + 1)
                    pool.wait_ge(rec_in[at.slot], 16 * (turn + 1))
                    pool.sem_inc(tick_mark, 1)
                    for t in range(G):
                        pool.indirect_dma_start(
                            rows[:, at.slot, t, 0:F], None, table[q],
                            bass.IndirectOffsetOnAxis(rec[:, at.slot, t, gathered_end:gathered_end + 1], 0)
                        ).then_inc(rows_in[at.slot], 16)
                    if beside is not None:
                        beside(q, at)
                ticks(pool, NG, 0, tick)

            gathers(0, 0)
            gathers(1, 0, scatter_columns)
            gathers(2, 0, scatter_columns)
            gathers(3, 0)
            gathers(4, 1)
            gathers(5, 0)

        @block.vector
        def _(dve):
            chain = Chain(dve, v)
            chain(dve.memset(edge_in[96:P, :, 0], PADT))
            chain(dve.memset(edge_in[96:P, :, 1], 0))
            chain(dve.memset(pad_rows[:, :, :, :], 0))
            chain(dve.memset(pad_rows[:, 0, :, 1], PADT))
            chain(dve.memset(pad_rows[:, 1, :, 0], PADT))
            chain(dve.memset(pad_attr[:, :, :], 0.0))
            chain(dve.memset(w_attr[:, :, :], 0.0))
            chain(dve.memset(x[0:P, NBLK - 1, :], 0.0))
            chain(dve.memset(next_first[:, :], PADT))
            dve.sem_inc(pads_set, 1)
            chain(dve.memset(rows[:, :, :, F:F + 1], 1.0))
            chain(dve.memset(ones_row[:, :], 1.0))
            chain(dve.memset(bbase[:, :], 0.0))

            def count_buckets(end):
                chain(dve.tensor_scalar(key_i[:, :], edge_in[:, :, end], 7, None, ALU.arith_shift_right))
                chain(dve.tensor_copy(key[:, :], key_i[:, :]))
                chain(dve.tensor_scalar(key[:, :], key[:, :], float(NBLK), None, ALU.min))
                done = (1 - end) * NBUK

                def ten_buckets(turn):
                    for i in range(10):
                        b = turn * 10 + i
                        wait(dve, bucket_counted, done + b - 1)
                        dve.tensor_scalar((hot, pos)[i % 2], key[:, :], iota_n[:, bass.ds(b, 1)], 0.0, ALU.is_equal,
                                          ALU.add, accum_out=cnt[:, bass.ds(b, 1)]).then_inc(bucket_counted, 1)
                ten_buckets(0)
                with dve.Fori(1, NBUK // 10) as turn:
                    ten_buckets(turn)
                dve.wait_ge(bucket_counted, (2 - end) * NBUK)
                dve.sem_inc(counts_ready, 1)

            def group_table(k):
                dve.wait_ge(prefix_ready, k + 1)
                chain(dve.tensor_copy(btot[:, :], counts_ps))
                if k == 0:
                    chain(dve.tensor_scalar(btot[:, 0:1], btot[:, 0:1], -float(P * NCOL - E), None, ALU.add))
                if k == 1:
                    chain(dve.tensor_tensor_scan(bincl[:, :], ones_row[:, 0:NBUK], btot[:, :], 0.0, ALU.mult, ALU.add))
                    chain(dve.tensor_tensor(bincl[:, :], bincl[:, :], btot[:, :], ALU.subtract))
                    chain(dve.scalar_tensor_tensor(out=bbase[:, 0:NBUK], in0=bincl[:, :], scalar=-1.0, in1=prefix_ps,
                                                   op0=ALU.add, op1=ALU.add))
                dve.sem_inc(prefix_used, 1)
                chain(dve.tensor_scalar(bgrp_i[:, :], btot[:, :], float(GE - 1), None, ALU.add))
                chain(dve.tensor_scalar(bgrp_i[:, :], bgrp_i[:, :], GE.bit_length() - 1, None, ALU.arith_shift_right))
                chain(dve.tensor_copy(bgrp[:, :], bgrp_i[:, :]))
                chain(dve.tensor_tensor_scan(bend[:, :], ones_row[:, 0:NBUK], bgrp[:, :], 0.0, ALU.mult, ALU.add))
                chain(dve.scalar_tensor_tensor(out=bdelta[:, :], in0=bgrp[:, :], scalar=-float(GE), in1=btot[:, :],
                                               op0=ALU.mult, op1=ALU.add))
                dve.sem_inc(group_step, 1)
                dve.wait_ge(group_mm, 2 * k + 1)
                chain(dve.tensor_copy(bend_t[0:NBUK, :], bank[2][0:NBUK, 0:P]))
                chain(dve.tensor_copy(bdelta_t[0:NBUK, :], bank[3][0:NBUK, 0:P]))
                chain(dve.tensor_scalar(past[0:NBLK, :], iota_g[0:NBLK, :], bend_t[0:NBLK, 0:1], None, ALU.is_ge))
                dve.sem_inc(group_step, 1)
                dve.wait_ge(group_mm, 2 * k + 2)
                chain(dve.tensor_scalar(gblk_i[k][:, :], bank[2][:, 0:NG], float(NBLK - 1), None, ALU.min))
                chain(dve.tensor_scalar(gbase[k][:, :], bank[2][:, 0:NG], float(NBLK - 1), float(P), ALU.min, ALU.mult))
                chain(dve.scalar_tensor_tensor(out=gstart[:, :], in0=iota_g[:, :], scalar=float(GE),
                                               in1=bank[3][:, 0:NG], op0=ALU.mult, op1=ALU.add))
                chain(dve.tensor_scalar(gstart_i[k][:, :], gstart[:, :], float(E), None, ALU.min))
                dve.sem_inc(groups_ready, 1)

            centered_count = [0]
            nth_centered = [0]

            def center_rows(src):
                chain(dve.tensor_reduce(stat[:, 0, :], src, AX, ALU.add))
                chain(dve.tensor_scalar(stat[:, 1, :], stat[:, 0, :], 1.0 / F, None, ALU.mult))
                for part in range(PARTS):
                    blocks = slice(part * PBLK, (part + 1) * PBLK)
                    dve.tensor_tensor(h[:, blocks, :], src[:, blocks, :],
                                      stat[:, 1, blocks].unsqueeze(2).broadcast_to([P, PBLK, F]), ALU.subtract
                                      ).then_inc(part_centered, 1)
                for part in range(PARTS):
                    blocks = slice(part * PBLK, (part + 1) * PBLK)
                    dve.wait_ge(part_squared, PARTS * nth_centered[0] + part + 1)
                    chain(dve.tensor_reduce(stat[:, 0, blocks], tab[:, blocks, :], AX, ALU.add))
                nth_centered[0] += 1
                chain(dve.tensor_scalar(stat[:, 1, :], stat[:, 0, :], 1.0 / F, EPS, ALU.mult, ALU.add))
                dve.sem_inc(var_ready, 1)
                centered_count[0] += 1
                dve.wait_ge(sqrt_ready, centered_count[0])
                chain(dve.reciprocal(stat[:, 2, :], stat[:, 0, :]))

            def target_place(q, k, at, end):
                turn = q * (NG // U) + at.turn
                dve.wait_ge(rec_in[at.slot], 16 * (turn + 1))
                wait(dve, agg_ready, q * NG + at.g - U + 1)
                dve.tensor_scalar(tloc[:, at.slot, :], rec[:, at.slot, :, end], gbase[k][:, bass.ds(at.g, 1)], None,
                                  ALU.subtract).then_inc(tloc_ready, 1)

            def one_hot(q, at):
                dve.wait_ge(tloc_ready, q * NG + at.g + 1)
                dve.tensor_tensor(onehot[:, at.slot, :, :], iota_n[:, :].unsqueeze(1).broadcast_to([P, G, P]),
                                  tloc[:, at.slot, :].unsqueeze(2).broadcast_to([P, G, P]), ALU.is_equal
                                  ).then_inc(onehot_ready, 1)

            def one_hot_b(q, at):
                dve.wait_ge(tloc_ready, q * NG + at.g + 1)
                dve.tensor_tensor(onehot_b[:, at.slot, :, :], iota_n[:, :].unsqueeze(1).broadcast_to([P, G, P]),
                                  tloc[:, at.slot, :].unsqueeze(2).broadcast_to([P, G, P]), ALU.is_equal
                                  ).then_inc(onehot_ready, 1)

            def add_sums(q, k, at, width):
                blk = dve.value_load(gblk_i[k][0:1, bass.ds(at.g, 1)], min_val=0, max_val=NBLK - 1)
                dve.wait_ge(agg_ready, q * NG + at.g + 1)
                wait(dve, acc_ready, q * NG + at.g)
                dve.tensor_tensor(acc[:, bass.ds(blk, 1), 0:width], acc[:, bass.ds(blk, 1), 0:width],
                                  agg[:, 0:width].unsqueeze(1), ALU.add).then_inc(acc_ready, 1)

            def sum_pass(q, k, end, extra=None):
                width = F + 1

                def tick(at):
                    if at.within(NG):
                        target_place(q, k, at, end)
                        one_hot(q, at)
                        if extra is not None and at.short == 0:
                            extra(at.short_turn)
                    if at.back(1).within(NG):
                        add_sums(q, k, at.back(1), width)
                ticks(dve, NG, 1, tick)

            dve.wait_ge(consts_pool, 5)
            chain(dve.tensor_copy(ident_b[:, :], ident[:, :]))
            dve.sem_inc(ident_ready, 1)
            dve.wait_ge(edges_in, 32)
            dve.wait_ge(next_in, 16)

            def count_disorder():
                chain(dve.tensor_scalar(key[:, :], edge_in[:, :, 0], float(PADT), float(PADT), ALU.is_equal, ALU.mult))
                chain(dve.tensor_copy(lo[:, :], edge_in[:, :, 1]))
                chain(dve.tensor_tensor(key[:, :], key[:, :], lo[:, :], ALU.max))
                chain(dve.tensor_copy(lo[:, 0:1], next_first[:, 1:2]))
                chain(dve.tensor_tensor(hot[:, 0:NCOL - 1], key[:, 0:NCOL - 1], key[:, 1:NCOL], ALU.is_gt))
                chain(dve.tensor_tensor(hot[:, NCOL - 1:NCOL], key[:, NCOL - 1:NCOL], lo[:, 0:1], ALU.is_gt))
                chain(dve.tensor_reduce(disorder[:, :], hot[:, :], AX, ALU.add))
                dve.sem_inc(order_counted, 1)
                dve.wait_ge(order_summed, 1)
                chain(dve.tensor_copy(disorder_i[:, :], bank[2][:, 0:1]))
                dve.sem_inc(order_known, 1)

            def rank_by_digits():
                step = Chain(dve, sort_step)
                step(dve.memset(sort_edges[:, :, 0], 0))
                step(dve.memset(sort_edges[:, :, 1], PADT))
                step(dve.memset(sort_attr[:, :, :], 0.0))
                dve.sem_inc(sort_padded, 1)
                for digit in range(2):
                    dve.wait_ge(sort_loaded, 16 * (4, 6)[digit])
                    step(dve.tensor_scalar(key_i[:, :], sort_edges[:, :, 1], (P - 1, 7)[digit], None,
                                           (ALU.bitwise_and, ALU.arith_shift_right)[digit]))
                    step(dve.tensor_copy(key[:, :], key_i[:, :]))
                    with dve.Fori(0, P) as b:
                        step.enter(b, 1)
                        step(dve.tensor_scalar(hot[:, :], key[:, :], iota_n[:, bass.ds(b, 1)], 0.0,
                                               ALU.is_equal, ALU.add, accum_out=digit_cnt[:, bass.ds(b, 1)]))
                    step.leave(P, 1)
                    dve.sem_inc(sort_counted, 1)
                    dve.wait_ge(sort_prefixed, digit + 1)
                    step(dve.tensor_copy(digit_tot, bank[0][:, 0:P]))
                    step(dve.tensor_tensor_scan(digit_incl, ones_row[:, 0:P], digit_tot, 0.0, ALU.mult, ALU.add))
                    step(dve.tensor_tensor(digit_incl, digit_incl, digit_tot, ALU.subtract))
                    step(dve.scalar_tensor_tensor(out=digit_base, in0=digit_incl, scalar=-1.0, in1=bank[1][:, 0:P],
                                                  op0=ALU.add, op1=ALU.add))
                    step(dve.memset(rank[:, :], 0.0))
                    with dve.Fori(0, P) as b:
                        step.enter(b, 4)
                        step(dve.tensor_scalar(hot[:, :], key[:, :], iota_n[:, bass.ds(b, 1)], None, ALU.is_equal))
                        step(dve.tensor_tensor_scan(pos[:, :], ones_row[:, :], hot[:, :], digit_base[:, bass.ds(b, 1)],
                                                    ALU.mult, ALU.add))
                        step(dve.tensor_tensor(hot[:, :], hot[:, :], pos[:, :], ALU.mult))
                        step(dve.tensor_tensor(rank[:, :], rank[:, :], hot[:, :], ALU.add))
                    step.leave(P, 4)
                    dve.sem_inc(sort_ranked, 1)
                dve.wait_ge(sort_edges_out, 2 * 16 * NCOL)
                dve.wait_ge(sort_attr_out, 2 * 16 * NCOL)

            count_disorder()
            unsorted = dve.value_load(disorder_i[0:1, 0:1], min_val=0, max_val=E)
            with dve.If(unsorted > 0):
                rank_by_digits()
            count_buckets(1)
            dve.wait_ge(x_in, 32)
            center_rows(x[:, :, :])
            chain(dve.scalar_tensor_tensor(out=tab[:, :, :], in0=h[:, :, :], scalar=0.0,
                                           in1=per_feature(stat[:, 2, :]), op0=ALU.max, op1=ALU.mult))
            dve.sem_inc(table_set, 1)
            group_table(0)
            count_buckets(0)
            group_table(1)
            chain(dve.memset(rank[:, :], 0.0))
            chain(dve.memset(acc[:, :, :], 0.0))
            chain(dve.tensor_scalar(key_i[:, :], edge_in[:, :, 0], P - 1, None, ALU.bitwise_and))
            chain(dve.tensor_copy(lo[:, :], key_i[:, :]))

            def sort_turn(turn):
                bucket = iota_n[:, bass.ds(turn, 1)]
                if isinstance(turn, int) and turn >= NG // R:
                    return
                done = 4 * turn
                dve.tensor_scalar(hot[:, :], key[:, :], bucket, None, ALU.is_equal).then_inc(rank_done, 1)
                dve.wait_ge(rank_done, done + 1)
                dve.tensor_tensor_scan(pos[:, :], ones_row[:, :], hot[:, :], bbase[:, bass.ds(turn, 1)],
                                       ALU.mult, ALU.add).then_inc(rank_done, 1)
                dve.wait_ge(rank_done, done + 2)
                dve.tensor_tensor(hot[:, :], hot[:, :], pos[:, :], ALU.mult).then_inc(rank_done, 1)
                dve.wait_ge(rank_done, done + 3)
                dve.tensor_tensor(rank[:, :], rank[:, :], hot[:, :], ALU.add).then_inc(rank_done, 1)
                dve.wait_ge(rank_done, done + 4)
                wait(dve, hist_mm, turn)
                cols = bass.ds(turn * HC, HC)
                dve.tensor_tensor(hist_lo[:, :, :], iota_n[:, :].unsqueeze(1).broadcast_to([P, HC, P]),
                                  lo[:, cols].unsqueeze(2).broadcast_to([P, HC, P]), ALU.is_equal
                                  ).then_inc(hist_hot, 1)
                dve.tensor_tensor(hist_hi[:, :, :], iota_n[:, 0:NBLK].unsqueeze(1).broadcast_to([P, HC, NBLK]),
                                  key[:, cols].unsqueeze(2).broadcast_to([P, HC, NBLK]), ALU.is_equal
                                  ).then_inc(hist_hot, 1)

            sum_pass(0, 0, 1, sort_turn)
            dve.wait_ge(acc_ready, NG)
            chain(dve.tensor_copy(deg_in[:, :], acc[:, :, F]))
            chain(dve.tensor_tensor(x[:, :, :], x[:, :, :], acc[:, :, 0:F], ALU.add))
            dve.wait_ge(hist_mm, NG // R)
            chain(dve.tensor_copy(deg_out[:, :], hist_ps))

            def project(j, prepare, finish):
                def tick(at):
                    if at.within(NBLK):
                        wait(dve, turned, j * NBLK + at.g - R + 1)
                        prepare(hs[:, at.short, :], bass.ds(at.g, 1)).then_inc(hs_ready, 1)
                    b = at.back(2)
                    if b.within(NBLK):
                        dve.wait_ge(mult, j * NBLK + b.g + 1)
                        finish(bank[2 + b.slot % 2], bass.ds(b.g, 1)).then_inc(mult_used, 1)
                ticks(dve, NBLK, 2, tick)
                dve.wait_ge(mult_used, (j + 1) * NBLK)

            def relu_scaled(to, b):
                return dve.tensor_scalar(to, h[:, b, :], 0.0, stat[:, 2, b], ALU.max, ALU.mult)

            def as_is(to, b):
                return dve.tensor_scalar(to, h[:, b, :], 1.0, None, ALU.mult)

            def both_sides(psum, b):
                dve.tensor_scalar(tab[:, b, :], psum[:, 0:F], 1.0, None, ALU.mult)
                return dve.tensor_scalar(own[:, b, :], psum[:, F:2 * F], 1.0, None, ALU.mult)

            splits = [0]

            def split_own():
                dve.sem_inc(own_rest, 1)
                done = 2 * PARTS * splits[0]
                for part in range(PARTS):
                    blocks = slice(part * PBLK, (part + 1) * PBLK)
                    dve.wait_ge(own_part, done + part + 1)
                    dve.tensor_tensor(own[:, blocks, :], own[:, blocks, :], own_parts[0][:, blocks, :], ALU.subtract
                                      ).then_inc(own_rest, 1)
                for part in range(PARTS):
                    blocks = slice(part * PBLK, (part + 1) * PBLK)
                    dve.wait_ge(own_part, done + PARTS + part + 1)
                    chain(dve.tensor_tensor(own_parts[2][:, blocks, :], own[:, blocks, :], own_parts[1][:, blocks, :],
                                            ALU.subtract))
                splits[0] += 1

            def attention_pass(q, layer):
                a0 = (q - 1) * NG
                att = vec(f"L1_gnn_att{layer}")
                split_own()
                dve.wait_ge(table_out[q], 16 * PARTS)
                chain(dve.memset(acc[:, :, :], 0.0))
                chain(dve.memset(nmax[:, :, :], -BIG))
                chain(dve.memset(score, 0.0))
                chain(dve.memset(score.rearrange("p u (t c) -> p (u t) c", c=32)[:, :, H:H + 1], 1.0))
                chain(dve.memset(steps, 0.0))
                chain(dve.memset(fence, 0.0))
                chain(dve.memset(fence[:, :, P:P + 1], -1.0))

                def tiles(part):
                    return part.rearrange("p (t c) -> p t c", t=G)

                tile_max = bank[5][:, P:P + 16 * G].rearrange("p (t c) -> p t c", t=G)

                def step_keys(at):
                    wait(dve, score_turned, a0 + at.g - 1)
                    dve.tensor_scalar(tiles(steps[:, at.slot % 2, :])[:, :, 0:H + 1],
                                      tloc[:, at.slot, :].unsqueeze(2).broadcast_to([P, G, H + 1]), STEPB, None,
                                      ALU.mult).then_inc(keys_ready, 1)

                def node_max_1(at):
                    o = at.slot % 2
                    dve.wait_ge(max_ready, a0 + at.g + 1)
                    dve.tensor_scalar(gseen[:, o, :], tile_max[:, :, H], -1.0, BIG, ALU.add, ALU.mult
                                      ).then_inc(max_step, 1)

                def node_max_2(at):
                    o, c = at.slot % 2, 6 * (a0 + at.g)
                    dve.wait_ge(max_step, c + 1)
                    dve.tensor_tensor(gtile[:, o, :, :], tile_max[:, :, 0:H],
                                      gseen[:, o, :].unsqueeze(2).broadcast_to([P, G, H]), ALU.add
                                      ).then_inc(max_step, 1)

                def node_max_3(at):
                    o, c = at.slot % 2, 6 * (a0 + at.g)
                    dve.wait_ge(max_step, c + 2)
                    dve.tensor_reduce(gmax[:, o, :], gtile[:, o, :, :].rearrange("p t h -> p h t"), AX, ALU.max
                                      ).then_inc(max_step, 1)

                def node_max_4(at, blk):
                    o, c = at.slot % 2, 6 * (a0 + at.g)
                    dve.wait_ge(max_step, c + 3)
                    wait(dve, max_spread, a0 + at.g - 1)
                    dve.tensor_tensor(newmax[:, o:o + 1, :], nmax[:, bass.ds(blk, 1), :], gmax[:, o:o + 1, :], ALU.max
                                      ).then_inc(max_step, 1)

                def node_max_5(at, blk):
                    o, c = at.slot % 2, 6 * (a0 + at.g)
                    dve.wait_ge(max_step, c + 4)
                    wait(dve, factor_ready, a0 + at.g - 1)
                    dve.tensor_tensor(drop[:, o:o + 1, :], nmax[:, bass.ds(blk, 1), :], newmax[:, o:o + 1, :],
                                      ALU.subtract).then_inc(max_step, 1)

                def node_max_6(at, blk):
                    o, c = at.slot % 2, 6 * (a0 + at.g)
                    dve.wait_ge(max_step, c + 5)
                    dve.tensor_scalar(nmax[:, bass.ds(blk, 1), :], newmax[:, o:o + 1, :], 1.0, None, ALU.mult
                                      ).then_inc(max_step, 1)

                def add_rows(at):
                    o = at.slot % 2
                    dve.wait_ge(rows_in[at.slot], 16 * G * (q * NU + at.turn + 1))
                    dve.wait_ge(spread, a0 + at.g + 1)
                    dve.tensor_tensor(tiles(both[:, 0, :]), tiles(bank[2 + o][:, :]), rows[:, at.slot, :, 0:F],
                                      ALU.add).then_inc(sum_used, 1)

                def leaky(at):
                    dve.wait_ge(sum_used, a0 + at.g + 1)
                    dve.scalar_tensor_tensor(out=both[:, 0, :], in0=both[:, 0, :], scalar=SLOPE, in1=both[:, 0, :],
                                             op0=ALU.mult, op1=ALU.max).then_inc(score_step, 1)

                def times_att(at):
                    dve.wait_ge(score_step, 3 * (a0 + at.g) + 1)
                    dve.tensor_tensor(tiles(both[:, 0, :]), tiles(both[:, 0, :]),
                                      att.unsqueeze(1).broadcast_to([P, G, F]), ALU.mult).then_inc(score_step, 1)

                def head_sums(at):
                    o = at.slot % 2
                    dve.wait_ge(score_step, 3 * (a0 + at.g) + 2)
                    dve.tensor_reduce(tiles(score[:, at.short, :])[:, :, 0:H],
                                      both[:, 0, :].rearrange("p (t h d) -> p t h d", t=G, h=H), AX, ALU.add
                                      ).then_inc(score_step, 1)

                def segment_1(at):
                    o = at.slot % 2
                    dve.wait_ge(score_sb, a0 + at.g + 1)
                    dve.tensor_tensor(fence[:, o, 1:P], turned_rows[:, o, 0:P - 1], turned_rows[:, o, 1:P],
                                      ALU.subtract).then_inc(seg_step, 1)

                def segment_2(at):
                    o = at.slot % 2
                    dve.wait_ge(seg_step, 3 * (a0 + at.g) + 1)
                    dve.tensor_tensor_scan(running[:, o, :], fence[:, o, 0:P], turned_rows[:, o, P:2 * P], -BIG,
                                           ALU.add, ALU.max).then_inc(seg_step, 1)

                def segment_3(at):
                    o = at.slot % 2
                    dve.wait_ge(seg_step, 3 * (a0 + at.g) + 2)
                    wait(dve, seg_turned, a0 + at.g - 1)
                    dve.scalar_tensor_tensor(out=at_last[:, o, :], in0=fence[:, o, 1:P + 1], scalar=0.0,
                                             in1=running[:, o, :], op0=ALU.not_equal, op1=ALU.mult
                                             ).then_inc(seg_step, 1)

                last_turned = bank[5][:, 0:P].rearrange("p (t c) -> p t c", t=G)[:, :, 0:H + 1]

                def last_rest_1(at):
                    o = at.slot % 2
                    dve.wait_ge(last_part, 2 * (a0 + at.g) + 1)
                    dve.tensor_tensor(tiles(last_rest[:, o, :]), last_turned, tiles(last_parts[:, o, 0, :]),
                                      ALU.subtract).then_inc(last_left, 1)

                def last_rest_2(at):
                    o = at.slot % 2
                    dve.wait_ge(last_part, 2 * (a0 + at.g) + 2)
                    dve.tensor_tensor(last_parts[:, o, 2, :], last_rest[:, o, :], last_parts[:, o, 1, :],
                                      ALU.subtract).then_inc(last_left, 1)

                def max_rest_1(at):
                    o = at.slot % 2
                    dve.wait_ge(max_part, 2 * (a0 + at.g) + 1)
                    dve.tensor_tensor(max_rest[:, o, :], newmax[:, o, :], max_parts[:, o, 0, :], ALU.subtract
                                      ).then_inc(max_left, 1)

                def max_rest_2(at):
                    o = at.slot % 2
                    dve.wait_ge(max_part, 2 * (a0 + at.g) + 2)
                    dve.tensor_tensor(max_parts[:, o, 2, :], max_rest[:, o, :], max_parts[:, o, 1, :], ALU.subtract
                                      ).then_inc(max_left, 1)

                def shift_1(at):
                    o = at.slot % 2
                    dve.wait_ge(max_spread, a0 + at.g + 1)
                    wait(dve, weight_ready, a0 + at.g - 1)
                    dve.tensor_tensor(shifted[:, o, :, :], tiles(score[:, at.short, :])[:, :, 0:H],
                                      bank[6][:, 0:G * H].rearrange("p (t h) -> p t h", t=G), ALU.subtract
                                      ).then_inc(shift_step, 1)

                def shift_2(at):
                    o = at.slot % 2
                    dve.wait_ge(shift_step, 2 * (a0 + at.g) + 1)
                    dve.tensor_scalar(shifted[:, o, :, :], shifted[:, o, :, :], 0.0, None, ALU.min
                                      ).then_inc(shift_step, 1)

                def weigh(at):
                    o = at.slot % 2
                    dve.wait_ge(weight_ready, a0 + at.g + 1)
                    w = weighted[:, o, :].rearrange("p (t h d) -> p t h d", t=G, h=H)
                    dve.tensor_tensor(w[:, :, :, 0:D],
                                      rows[:, at.slot, :, 0:F].rearrange("p t (h d) -> p t h d", h=H),
                                      w[:, :, :, D:HD].broadcast_to([P, G, H, D]), ALU.mult
                                      ).then_inc(weighted_ready, 1)

                def rescale_sums(at, blk):
                    o = at.slot % 2
                    dve.wait_ge(factor_ready, a0 + at.g + 1)
                    wait(dve, acc_ready, q * NG + at.g)
                    sums = acc[:, bass.ds(blk, 1), :].rearrange("p b (h d) -> p (b h) d", h=H)
                    dve.tensor_tensor(sums, sums, factor[:, o, :].unsqueeze(2).broadcast_to([P, H, HD]), ALU.mult
                                      ).then_inc(acc_step, 1)

                def accumulate(at, blk):
                    sums = acc[:, bass.ds(blk, 1), :].rearrange("p b (h d) -> p (b h) d", h=H)
                    dve.wait_ge(acc_step, a0 + at.g + 1)
                    dve.wait_ge(agg_ready, q * NG + at.g + 1)
                    dve.tensor_tensor(sums, sums, agg.rearrange("p (h d) -> p h d", h=H), ALU.add
                                      ).then_inc(acc_ready, 1)

                blocks = {}

                def load_block(at, lag):
                    g = at.back(lag)
                    if g.within(NG):
                        blocks[at.slot - lag] = dve.value_load(gblk_i[0][0:1, bass.ds(g.g, 1)], min_val=0,
                                                               max_val=NBLK - 1)

                def tick(at):
                    b, c, d, e, f = (at.back(lag) for lag in (1, 2, 3, 4, 5))
                    now, one, two, three, four, five = (i.within(NG) for i in (at, b, c, d, e, f))
                    if at.slot == 0:
                        blocks.clear()
                        for lag in (5, 4, 3):
                            load_block(at, lag)
                    blk, old, older = (blocks.get(at.slot - lag) for lag in (3, 4, 5))
                    if now:
                        target_place(q, 0, at, 1)
                    if five:
                        accumulate(f, older)
                    if now:
                        one_hot_b(q, at)
                    if three:
                        node_max_1(d)
                    if four:
                        shift_1(e)
                    if three:
                        node_max_2(d)
                    if one:
                        add_rows(b)
                    if three:
                        node_max_3(d)
                    if four:
                        shift_2(e)
                    if two:
                        segment_1(c)
                    if one:
                        leaky(b)
                    if three:
                        node_max_4(d, blk)
                    if two:
                        segment_2(c)
                    if four:
                        weigh(e)
                    if two:
                        segment_3(c)
                    if three:
                        node_max_5(d, blk)
                    if three:
                        max_rest_1(d)
                    if at.slot < U - 1:
                        load_block(at, 2)
                    if one:
                        times_att(b)
                    if three:
                        max_rest_2(d)
                    if now:
                        step_keys(at)
                    if three:
                        node_max_6(d, blk)
                    if two:
                        last_rest_1(c)
                    if one:
                        head_sums(b)
                    if two:
                        last_rest_2(c)
                    if four:
                        rescale_sums(e, old)
                ticks(dve, NG, 5, tick)
                dve.wait_ge(acc_ready, (q + 1) * NG)

            def attention_nodes(layer):
                sums = acc[:, :, :].rearrange("p b (h d) -> p (b h) d", h=H)
                inv = rden[:, :, :].rearrange("p b h -> p (b h)")
                chain(dve.tensor_scalar(inv, sums[:, :, D], 1e-30, None, ALU.max))
                chain(dve.reciprocal(inv, inv))
                chain(dve.tensor_tensor(h[:, :, :].rearrange("p b (h d) -> p (b h) d", h=H), sums[:, :, 0:D],
                                        inv.unsqueeze(2).broadcast_to([P, NBLK * H, D]), ALU.mult))
                chain(dve.tensor_tensor(h[:, :, :], h[:, :, :], per_block(vec(f"L1_gnn_b{layer}")), ALU.add))
                chain(dve.tensor_scalar(h[:, :, :], h[:, :, :], 0.0, None, ALU.max))
                center_rows(h[:, :, :])
                chain(dve.tensor_tensor(h[:, :, :], h[:, :, :], per_feature(stat[:, 2, :]), ALU.mult))
                chain(dve.tensor_tensor(h[:, :, :], h[:, :, :], per_block(vec(f"L1_gnn_g{layer}")), ALU.mult))
                chain(dve.tensor_tensor(h[:, :, :], h[:, :, :], per_block(vec(f"L1_gnn_be{layer}")), ALU.add))

            dve.wait_ge(weights_in, 16 * NWEIGHT)
            center_rows(x[:, :, :])
            project(0, relu_scaled, both_sides)
            attention_pass(1, 1)
            attention_nodes(1)
            project(1, as_is, both_sides)
            attention_pass(2, 2)
            attention_nodes(2)
            chain(dve.tensor_tensor(x[:, :, :], x[:, :, :], h[:, :, :], ALU.add))

            def gcn_tables(psum, b):
                dve.tensor_scalar(tab[:, b, :], psum[:, 0:F], dinv[:, 0, b], None, ALU.mult)
                return dve.tensor_scalar(xr[:, b, :], psum[:, F:2 * F], dinv[:, 1, b], None, ALU.mult)

            def gcn_side(own, side):
                chain(dve.tensor_tensor(own, own, acc[:, :, 0:F], ALU.add))
                chain(dve.tensor_tensor(own, own, per_feature(dinv[:, side, :]), ALU.mult))

            def mlp_tables(psum, b):
                dve.tensor_scalar(tab[:, b, :], psum[:, 0:F], 1.0, None, ALU.mult)
                return dve.tensor_tensor(own[:, b, :], psum[:, F:2 * F].unsqueeze(1),
                                         vec("L3_gnn_b1").unsqueeze(1), ALU.add)

            def mlp_pass(q):
                a0 = 2 * NG
                split_own()
                dve.wait_ge(table_out[q], 16 * PARTS)
                chain(dve.memset(acc[:, :, :], 0.0))
                chain(dve.memset(attr, 0.0))
                dve.sem_inc(attr_set, 1)

                def heads(part):
                    return part.rearrange("p (n d) -> p n d", d=D)

                def per_head(col):
                    return col.unsqueeze(2).broadcast_to([P, G * H, D])

                def tiles(part):
                    return part.rearrange("p (t c) -> p t c", t=G)

                def add_rows(at):
                    dve.wait_ge(rows_in[at.slot], 16 * G * (q * NU + at.turn + 1))
                    dve.wait_ge(spread, a0 + at.g + 1)
                    wait(dve, activated, at.g - R + 1)
                    dve.tensor_tensor(tiles(centered[:, at.short, :]), tiles(bank[2 + at.slot % 2][:, :]),
                                      rows[:, at.slot, :, 0:F], ALU.add).then_inc(sum_used, 1)

                def variances(at):
                    dve.wait_ge(squared, at.g + 1)
                    dve.tensor_reduce(var[:, at.slot % 2, :], heads(square[:, at.slot % 2, :]), AX, ALU.add
                                      ).then_inc(var_step, 1)

                def newton(at, step):
                    v_, t_, y = var[:, :, :], trial[:, :, :], inv[:, at.slot // 2 % 2, :, :]
                    if step == 0:
                        dve.wait_ge(var_step, at.g + 1)
                        ins = dve.tensor_scalar(v_, v_, 1.0 / D, EPS, ALU.mult, ALU.add)
                    else:
                        dve.wait_ge(newton_step, NEWTON * at.half + step)
                        if step == 1:
                            ins = dve.tensor_scalar(t_.bitcast(I32), v_.bitcast(I32), 1, None,
                                                    ALU.arith_shift_right)
                        elif step == 2:
                            ins = dve.tensor_scalar(y.bitcast(I32), t_.bitcast(I32), -1.0, float(0x5f3759df),
                                                    ALU.mult, ALU.add)
                        elif step % 3 == 0:
                            ins = dve.tensor_tensor(t_, y, y, ALU.mult)
                        elif step % 3 == 1:
                            ins = dve.scalar_tensor_tensor(out=t_, in0=t_, scalar=-0.5, in1=v_, op0=ALU.mult,
                                                           op1=ALU.mult)
                        else:
                            ins = dve.scalar_tensor_tensor(out=y, in0=t_, scalar=1.5, in1=y, op0=ALU.add,
                                                           op1=ALU.mult)
                    ins.then_inc(newton_step, 1)

                def scale(at):
                    z = heads(centered[:, at.short, :])
                    dve.wait_ge(newton_step, NEWTON * (at.half + 1))
                    dve.tensor_tensor(z, z, per_head(inv[:, at.slot // 2 % 2, at.slot % 2, :]), ALU.mult
                                      ).then_inc(norm_step, 1)

                def times_gamma(at):
                    z = tiles(centered[:, at.short, :])
                    dve.wait_ge(norm_step, 3 * at.g + 1)
                    dve.tensor_tensor(z, z, vec("L3_gnn_gn_gamma").unsqueeze(1).broadcast_to([P, G, F]), ALU.mult
                                      ).then_inc(norm_step, 1)

                def plus_beta(at):
                    z = tiles(centered[:, at.short, :])
                    dve.wait_ge(norm_step, 3 * at.g + 2)
                    dve.tensor_tensor(z, z, vec("L3_gnn_gn_beta").unsqueeze(1).broadcast_to([P, G, F]), ALU.add
                                      ).then_inc(norm_step, 1)

                def tick(at):
                    b, c, e, g = (at.back(lag) for lag in (1, 2, 4, 6))
                    pair = c.slot % 2 == 1 and c.within(NG)
                    if at.within(NG):
                        target_place(q, 0, at, 1)
                    if g.within(NG):
                        add_sums(q, 0, g, F)
                    if c.within(NG):
                        variances(c)
                    if e.within(NG):
                        scale(e)
                    if pair:
                        newton(c, 0)
                    if at.within(NG):
                        one_hot_b(q, at)
                    if pair:
                        newton(c, 1)
                    if e.within(NG):
                        times_gamma(e)
                    if pair:
                        newton(c, 2)
                        newton(c, 3)
                    if b.within(NG):
                        add_rows(b)
                    if pair:
                        newton(c, 4)
                        newton(c, 5)
                    if e.within(NG):
                        plus_beta(e)
                    if pair:
                        newton(c, 6)
                        newton(c, 7)
                        newton(c, 8)
                        newton(c, 9)
                        newton(c, 10)
                        newton(c, 11)
                ticks(dve, NG, 6, tick)
                dve.wait_ge(acc_ready, (q + 1) * NG)

            def sums_as_is(to, b):
                return dve.tensor_scalar(to.unsqueeze(1), acc[:, b, 0:F], 1.0, None, ALU.mult)

            def with_bias(psum, b):
                return dve.scalar_tensor_tensor(out=h[:, b, :], in0=vec("L3_gnn_b2").unsqueeze(1), scalar=deg_in[:, b],
                                                in1=psum[:, 0:F].unsqueeze(1), op0=ALU.mult, op1=ALU.add)

            center_rows(x[:, :, :])
            chain(dve.tensor_scalar(dinv[:, 0, :], deg_in[:, :], 1.0, None, ALU.add))
            chain(dve.tensor_scalar(dinv[:, 1, :], deg_out[:, :], 1.0, None, ALU.add))
            dve.sem_inc(var_ready, 1)
            dve.wait_ge(sqrt_ready, centered_count[0] + 1)
            centered_count[0] += 1
            chain(dve.reciprocal(dinv[:, :, :], dinv[:, :, :]))
            project(2, relu_scaled, gcn_tables)
            chain(dve.memset(acc[:, :, :], 0.0))
            sum_pass(3, 0, 1)
            dve.wait_ge(acc_ready, 4 * NG)
            dve.wait_ge(table_out[3], 16 * PARTS)
            gcn_side(tab[:, :, :], 0)
            dve.wait_ge(table_out[4], 16 * PARTS)
            chain(dve.tensor_tensor(tab[:, :, :], tab[:, :, :], per_block(vec("L2_gnn_b_fwd")), ALU.add))
            chain(dve.memset(acc[:, :, :], 0.0))
            sum_pass(4, 1, 0)
            dve.wait_ge(acc_ready, 5 * NG)
            gcn_side(xr[:, :, :], 1)
            chain(dve.tensor_tensor(xr[:, :, :], xr[:, :, :], per_block(vec("L2_gnn_b_bwd")), ALU.add))
            chain(dve.tensor_tensor(xr[:, :, :], xr[:, :, :], tab[:, :, :], ALU.add))
            chain(dve.scalar_tensor_tensor(out=x[:, :, :], in0=xr[:, :, :], scalar=0.0, in1=x[:, :, :],
                                           op0=ALU.max, op1=ALU.add))
            def center_weights(w, n):
                chain(dve.tensor_reduce(mean[:, 0:n], w, AX, ALU.add))
                chain(dve.tensor_scalar(mean[:, 0:n], mean[:, 0:n], 1.0 / D, None, ALU.mult))
                chain(dve.tensor_tensor(w, w, mean[:, 0:n].unsqueeze(2).broadcast_to([P, n, D]), ALU.subtract))

            center_weights(w_pair[:, 3, :].rearrange("p (n d) -> p n d", d=D), 2 * H)
            center_weights(w_attr[:, :, :].rearrange("p t (n d) -> p (t n) d", d=D), G * H)
            center_weights(vec("L3_gnn_b1").rearrange("p (n d) -> p n d", d=D), H)
            dve.sem_inc(w_centered, 1)
            center_rows(x[:, :, :])
            project(3, relu_scaled, mlp_tables)
            mlp_pass(5)
            chain(dve.tensor_scalar(rcount[:, :], deg_in[:, :], 1.0, None, ALU.max))
            chain(dve.reciprocal(rcount[:, :], rcount[:, :]))
            project(4, sums_as_is, with_bias)
            for part in range(PARTS):
                blocks = slice(part * PBLK, (part + 1) * PBLK)
                chain(dve.tensor_tensor(h[:, blocks, :], h[:, blocks, :],
                                        rcount[:, blocks].unsqueeze(2).broadcast_to([P, PBLK, F]), ALU.mult))
                chain(dve.tensor_tensor(x[:, blocks, :], x[:, blocks, :], h[:, blocks, :], ALU.add))
                dve.sem_inc(final_set, 1)

        @block.scalar
        def _(act):
            squared_rows = [0]

            def square_rows():
                for part in range(PARTS):
                    blocks = slice(part * PBLK, (part + 1) * PBLK)
                    act.wait_ge(part_centered, PARTS * squared_rows[0] + part + 1)
                    nc.scalar.activation(tab[:, blocks, :], h[:, blocks, :], ACT.Square).then_inc(part_squared, 1)
                squared_rows[0] += 1

            def sqrt_rows(nth):
                square_rows()
                act.wait_ge(var_ready, nth)
                nc.scalar.activation(stat[:, 0, :], stat[:, 1, :], ACT.Sqrt).then_inc(sqrt_ready, 1)

            def turn_rows(j):
                def tick(at):
                    act.wait_ge(turned, j * NBLK + at.g + 1)
                    wait(act, mult, j * NBLK + at.g - R + 1)
                    nc.scalar.copy(hs_t[:, at.short, :], bank[at.slot % 2][:, 0:F]).then_inc(turned_sb, 1)
                ticks(act, NBLK, 0, tick)

            def split_own(nth):
                done = (PARTS + 1) * nth
                for i in range(2):
                    for part in range(PARTS):
                        blocks = slice(part * PBLK, (part + 1) * PBLK)
                        act.wait_ge(own_rest, done + 1 + i * (part + 1))
                        nc.scalar.copy(own_parts[i][:, blocks, :], own[:, blocks, :]).then_inc(own_part, 1)

            def wide_hot(q, at):
                a0 = {1: 0, 2: NG, 5: 2 * NG}[q]
                wait(act, agg_ready, q * NG + at.g - 1)
                act.wait_ge(onehot_ready, q * NG + at.g + 1)
                nc.scalar.copy(onehot_f[:, at.slot % 2, :, :], onehot_b[:, at.slot, :, :]).then_inc(hot_wide, 1)

            def attention_pass(q):
                a0 = (q - 1) * NG

                def hot(at):
                    o = at.slot % 2
                    act.wait_ge(turned_hot, a0 + at.g + 1)
                    wait(act, max_spread, a0 + at.g - R + 1)
                    nc.scalar.copy(hot_t[:, at.short, :], bank_b[o]).then_inc(turned_hot_sb, 1)

                def factors(at):
                    o = at.slot % 2
                    act.wait_ge(max_step, 6 * (a0 + at.g) + 5)
                    wait(act, acc_step, a0 + at.g - 1)
                    nc.scalar.activation(factor[:, o, :], drop[:, o, :], ACT.Exp).then_inc(factor_ready, 1)

                def weights(at):
                    o = at.slot % 2
                    act.wait_ge(shift_step, 2 * (a0 + at.g) + 2)
                    wait(act, agg_ready, q * NG + at.g - 1)
                    w = weighted[:, o, :].rearrange("p (n d) -> p n d", d=HD)
                    nc.scalar.activation(w[:, :, D], shifted[:, o, :, :].rearrange("p t h -> p (t h)"), ACT.Exp
                                         ).then_inc(weight_ready, 1)

                def score_rows(at):
                    act.wait_ge(score_turned, a0 + at.g + 1)
                    wait(act, seg_step, 3 * (a0 + at.g - 1))
                    nc.scalar.copy(turned_rows[:, at.slot % 2, :], bank[4][:, 0:2 * P]).then_inc(score_sb, 1)

                def last_part_1(at):
                    act.wait_ge(seg_turned, a0 + at.g + 1)
                    wait(act, max_ready, a0 + at.g - 1)
                    nc.scalar.copy(last_parts[:, at.slot % 2, 0, :].rearrange("p (t c) -> p t c", t=G),
                                   bank[5][:, 0:P].rearrange("p (t c) -> p t c", t=G)[:, :, 0:H + 1]
                                   ).then_inc(last_part, 1)

                def last_part_2(at):
                    o = at.slot % 2
                    act.wait_ge(last_left, 2 * (a0 + at.g) + 1)
                    nc.scalar.copy(last_parts[:, o, 1, :], last_rest[:, o, :]).then_inc(last_part, 1)

                def max_part_1(at):
                    o = at.slot % 2
                    act.wait_ge(max_step, 6 * (a0 + at.g) + 4)
                    wait(act, max_spread, a0 + at.g - 1)
                    nc.scalar.copy(max_parts[:, o, 0, :], newmax[:, o, :]).then_inc(max_part, 1)

                def max_part_2(at):
                    o = at.slot % 2
                    act.wait_ge(max_left, 2 * (a0 + at.g) + 1)
                    nc.scalar.copy(max_parts[:, o, 1, :], max_rest[:, o, :]).then_inc(max_part, 1)

                def widen(at):
                    wide_hot(q, at)

                def tick(at):
                    c, d, e = at.back(2), at.back(3), at.back(4)
                    if e.within(NG):
                        widen(e)
                    if c.within(NG):
                        score_rows(c)
                    if at.within(NG):
                        hot(at)
                    if e.within(NG):
                        weights(e)
                    if d.within(NG):
                        max_part_1(d)
                    if d.within(NG):
                        max_part_2(d)
                    if d.within(NG):
                        factors(d)
                    if c.within(NG):
                        last_part_1(c)
                    if c.within(NG):
                        last_part_2(c)
                ticks(act, NG, 4, tick)

            def mlp_pass(q):
                a0 = 2 * NG

                def turned_in(at):
                    o = at.slot % 2
                    act.wait_ge(turned_hot, a0 + at.g + 1)
                    wait(act, spread, a0 + at.g - 1)
                    nc.scalar.copy(hot_t[:, at.short, :], bank_b[o])
                    nc.scalar.copy(attr_t[:, o, :], bank[4][:, 0:P]).then_inc(turned_hot_sb, 1)

                def squares(at):
                    o = at.slot % 2
                    act.wait_ge(sum_used, a0 + at.g + 1)
                    wait(act, var_step, at.g - 1)
                    nc.scalar.activation(square[:, o, :], centered[:, at.short, :], ACT.Square).then_inc(squared, 1)

                def silus(at):
                    o = at.slot % 2
                    act.wait_ge(norm_step, 3 * (at.g + 1))
                    wait(act, agg_ready, q * NG + at.g - 1)
                    nc.scalar.activation(silu[:, o, :], centered[:, at.short, :], ACT.Silu).then_inc(activated, 1)

                def tick(at):
                    b, e, f = at.back(1), at.back(4), at.back(5)
                    if f.within(NG):
                        wide_hot(q, f)
                    if at.within(NG):
                        turned_in(at)
                    if b.within(NG):
                        squares(b)
                    if e.within(NG):
                        silus(e)
                ticks(act, NG, 5, tick)

            sqrt_rows(1)
            sqrt_rows(2)
            turn_rows(0)
            split_own(0)
            attention_pass(1)
            sqrt_rows(3)
            turn_rows(1)
            split_own(1)
            attention_pass(2)
            sqrt_rows(4)
            sqrt_rows(5)
            act.wait_ge(var_ready, 6)
            nc.scalar.activation(dinv[:, :, :], dinv[:, :, :], ACT.Sqrt).then_inc(sqrt_ready, 1)
            turn_rows(2)
            sqrt_rows(7)
            turn_rows(3)
            split_own(2)
            mlp_pass(5)
            turn_rows(4)

        @block.tensor
        def _(pe):
            pe.wait_ge(consts_pool, 5)
            pe.wait_ge(ident_ready, 1)
            pe.wait_ge(order_counted, 1)
            nc.tensor.matmul(bank[2][:, 0:1], ones[:, :], disorder[:, :], start=True, stop=True).then_inc(order_summed, 1)
            pe.wait_ge(order_known, 1)
            unsorted = pe.value_load(disorder_i[0:1, 0:1], min_val=0, max_val=E)
            with pe.If(unsorted > 0):
                for digit in range(2):
                    pe.wait_ge(sort_counted, digit + 1)
                    nc.tensor.matmul(bank[0][:, 0:P], ones[:, :], digit_cnt, start=True, stop=True)
                    nc.tensor.matmul(bank[1][:, 0:P], tri[:, :], digit_cnt, start=True, stop=True
                                     ).then_inc(sort_prefixed, 1)

            def prefixes(k):
                pe.wait_ge(counts_ready, k + 1)
                wait(pe, prefix_used, k)
                nc.tensor.matmul(counts_ps, ones[:, :], cnt[:, :], start=True, stop=True)
                nc.tensor.matmul(prefix_ps, tri[:, :], cnt[:, :], start=True, stop=True).then_inc(prefix_ready, 1)

            def group_sums(k):
                pe.wait_ge(group_step, 2 * k + 1)
                nc.tensor.transpose(bank[2][0:NBUK, 0:P], bend[:, :], ident[:, :])
                nc.tensor.transpose(bank[3][0:NBUK, 0:P], bdelta[:, :], ident[:, :]).then_inc(group_mm, 1)
                pe.wait_ge(group_step, 2 * k + 2)
                nc.tensor.matmul(bank[2][:, 0:NG], ones[0:NBLK, :], past[0:NBLK, :], start=True, stop=True)
                nc.tensor.matmul(bank[3][:, 0:NG], bdelta_t[0:NBLK, :], past[0:NBLK, :], start=True, stop=True
                                 ).then_inc(group_mm, 1)

            def sum_groups(q, at, width):
                turn = q * (NG // U) + at.turn
                pe.wait_ge(rows_in[at.slot], 16 * G * (turn + 1))
                pe.wait_ge(onehot_ready, q * NG + at.g + 1)
                wait(pe, acc_ready, q * NG + at.g)
                for t in range(G):
                    mm = nc.tensor.matmul(agg[:, 0:width], onehot[:, at.slot, t, :], rows[:, at.slot, t, 0:width],
                                          start=(t == 0), stop=(t == G - 1))
                mm.then_inc(agg_ready, 1)

            def histogram(turn):
                pe.wait_ge(hist_hot, 2 * turn + 2)
                for c in range(HC):
                    mm = nc.tensor.matmul(hist_ps, hist_lo[:, c, :], hist_hi[:, c, :],
                                          start=(isinstance(turn, int) and turn == 0 and c == 0),
                                          stop=(isinstance(turn, int) and turn == NG // R - 1 and c == HC - 1),
                                          skip_group_check=True)
                mm.then_inc(hist_mm, 1)

            def sum_pass(q, extra=None):
                def tick(at):
                    if at.within(NG):
                        sum_groups(q, at, F + 1)
                        if extra is not None and at.short == 0:
                            extra(at.short_turn)
                ticks(pe, NG, 0, tick)

            def project(j, width):
                def tick(at):
                    if at.within(NBLK):
                        pe.wait_ge(hs_ready, j * NBLK + at.g + 1)
                        wait(pe, turned_sb, j * NBLK + at.g - 1)
                        nc.tensor.transpose(bank[at.slot % 2][:, 0:F], hs[:, at.short, :], ident[:, :]
                                            ).then_inc(turned, 1)
                    b = at.back(1)
                    if b.within(NBLK):
                        pe.wait_ge(turned_sb, j * NBLK + b.g + 1)
                        wait(pe, mult_used, j * NBLK + b.g - 1)
                        w = w_out[:, :] if j == 4 else w_pair[:, j, :]
                        nc.tensor.matmul(bank[2 + b.slot % 2][:, 0:width], hs_t[:, b.short, :], w,
                                         start=True, stop=True).then_inc(mult, 1)
                ticks(pe, NBLK, 1, tick)

            def attention_pass(q):
                a0 = (q - 1) * NG

                def turn_hots(at):
                    pe.wait_ge(onehot_ready, q * NG + at.g + 1)
                    wait(pe, turned_hot_sb, a0 + at.g - 1)
                    for t in range(G):
                        mm = nc.tensor.transpose(bank_b[at.slot % 2][:, t * P:(t + 1) * P], onehot_b[:, at.slot, t, :],
                                                 ident_b[:, :])
                    mm.then_inc(turned_hot, 1)

                def spread_maximum(at):
                    o = at.slot % 2
                    pe.wait_ge(max_left, 2 * (a0 + at.g) + 2)
                    wait(pe, shift_step, 2 * (a0 + at.g) - 1)
                    for t in range(G):
                        for i in range(3):
                            mm = nc.tensor.matmul(bank[6][:, t * H:(t + 1) * H], hot_t[:, at.short, t * P:(t + 1) * P],
                                                  max_parts[:, o, i, :], start=(i == 0), stop=(i == 2))
                    mm.then_inc(max_spread, 1)

                def spread_targets(at):
                    o = at.slot % 2
                    blk = pe.value_load(gblk_i[0][0:1, bass.ds(at.g, 1)], min_val=0, max_val=NBLK - 1)
                    pe.wait_ge(turned_hot_sb, a0 + at.g + 1)
                    wait(pe, sum_used, a0 + at.g - 1)
                    for t in range(G):
                        for i in range(3):
                            mm = nc.tensor.matmul(bank[2 + o][:, t * P:(t + 1) * P],
                                                  hot_t[:, at.short, t * P:(t + 1) * P],
                                                  own_parts[i][:, bass.ds(blk, 1), :], start=(i == 0), stop=(i == 2))
                    mm.then_inc(spread, 1)

                def turn_scores(at):
                    o = at.slot % 2
                    pe.wait_ge(keys_ready, a0 + at.g + 1)
                    pe.wait_ge(score_step, 3 * (a0 + at.g) + 3)
                    wait(pe, score_sb, a0 + at.g)
                    nc.tensor.transpose(bank[4][:, 0:P], steps[:, o, :], ident[:, :])
                    nc.tensor.transpose(bank[4][:, P:2 * P], score[:, at.short, :], ident[:, :]).then_inc(score_turned, 1)

                def sum_weighted(at):
                    pe.wait_ge(weighted_ready, a0 + at.g + 1)
                    wait(pe, acc_ready, q * NG + at.g)
                    pe.wait_ge(hot_wide, a0 + at.g + 1)
                    for t in range(G):
                        mm = nc.tensor.matmul(agg, onehot_f[:, at.slot % 2, t, :],
                                              weighted[:, at.slot % 2, t * H * HD:(t + 1) * H * HD],
                                              start=(t == 0), stop=(t == G - 1))
                    mm.then_inc(agg_ready, 1)

                def turn_last(at):
                    o = at.slot % 2
                    pe.wait_ge(seg_step, 3 * (a0 + at.g) + 3)
                    wait(pe, max_step, 6 * (a0 + at.g - 1) + 2)
                    nc.tensor.transpose(bank[5][:, 0:P], at_last[:, o, :], ident[:, :]).then_inc(seg_turned, 1)

                def node_maximum(at):
                    o = at.slot % 2
                    pe.wait_ge(last_left, 2 * (a0 + at.g) + 2)
                    for t in range(G):
                        for i in range(3):
                            mm = nc.tensor.matmul(bank[5][:, P + 16 * t:P + 16 * t + H + 1], onehot_b[:, at.slot, t, :],
                                                  last_parts[:, o, i, t * (H + 1):(t + 1) * (H + 1)],
                                                  start=(i == 0), stop=(i == 2))
                    mm.then_inc(max_ready, 1)

                def tick(at):
                    c, d, e = at.back(2), at.back(3), at.back(4)
                    if c.within(NG):
                        turn_scores(c)
                    if at.within(NG):
                        turn_hots(at)
                    if at.within(NG):
                        spread_targets(at)
                    if c.within(NG):
                        turn_last(c)
                    if e.within(NG):
                        sum_weighted(e)
                    if c.within(NG):
                        node_maximum(c)
                    if d.within(NG):
                        spread_maximum(d)
                ticks(pe, NG, 4, tick)

            def mlp_pass(q):
                a0 = 2 * NG

                def turn_hots(at):
                    pe.wait_ge(onehot_ready, q * NG + at.g + 1)
                    pe.wait_ge(attr_in[at.short], 16 * (at.short_turn + 1))
                    wait(pe, turned_hot_sb, a0 + at.g)
                    nc.tensor.transpose(bank[4][:, 0:P], attr[:, at.short, :], ident[:, :]).then_inc(attr_free, 1)
                    for t in range(G):
                        mm = nc.tensor.transpose(bank_b[at.slot % 2][:, t * P:(t + 1) * P], onehot_b[:, at.slot, t, :],
                                                 ident_b[:, :])
                    mm.then_inc(turned_hot, 1)

                def spread_targets(at):
                    o = at.slot % 2
                    blk = pe.value_load(gblk_i[0][0:1, bass.ds(at.g, 1)], min_val=0, max_val=NBLK - 1)
                    pe.wait_ge(turned_hot_sb, a0 + at.g + 1)
                    wait(pe, sum_used, a0 + at.g - 1)
                    for t in range(G):
                        for i in range(3):
                            nc.tensor.matmul(bank[2 + o][:, t * P:(t + 1) * P], hot_t[:, at.short, t * P:(t + 1) * P],
                                             own_parts[i][:, bass.ds(blk, 1), :], start=(i == 0), stop=False)
                        mm = nc.tensor.matmul(bank[2 + o][:, t * P:(t + 1) * P], attr_t[:, o, :], w_attr[:, t, :],
                                              start=False, stop=True)
                    mm.then_inc(spread, 1)

                def sum_activated(at):
                    pe.wait_ge(activated, at.g + 1)
                    wait(pe, acc_ready, q * NG + at.g)
                    pe.wait_ge(hot_wide, a0 + at.g + 1)
                    for t in range(G):
                        mm = nc.tensor.matmul(agg[:, 0:F], onehot_f[:, at.slot % 2, t, :],
                                              silu[:, at.slot % 2, t * F:(t + 1) * F],
                                              start=(t == 0), stop=(t == G - 1))
                    mm.then_inc(agg_ready, 1)

                def tick(at):
                    f = at.back(5)
                    if at.within(NG):
                        turn_hots(at)
                    if f.within(NG):
                        sum_activated(f)
                    if at.within(NG):
                        spread_targets(at)
                ticks(pe, NG, 5, tick)

            for k in range(2):
                prefixes(k)
                group_sums(k)
            sum_pass(0, histogram)
            pe.wait_ge(weights_in, 16 * NWEIGHT)
            project(0, 2 * F)
            attention_pass(1)
            project(1, 2 * F)
            attention_pass(2)
            project(2, 2 * F)
            sum_pass(3)
            sum_pass(4)
            pe.wait_ge(w_centered, 1)
            project(3, 2 * F)
            mlp_pass(5)
            project(4, F)


INPUTS = ["x", "edge_attr_4", "L1_gnn_Wl1", "L1_gnn_Wr1", "L1_gnn_Wl2", "L1_gnn_Wr2", "L2_gnn_W_fwd", "L2_gnn_W_bwd",
          "L3_gnn_W1", "L3_gnn_W2"] + VECS


def kernel(**inputs):
    import numpy as np
    import concourse.bacc as bacc
    from concourse.bass_utils import run_bass_kernel_spmd as run

    nc = bacc.Bacc("TRN2", target_bir_lowering=False, num_devices=1)
    arrays = {"edges": np.ascontiguousarray(np.stack([inputs["src"], inputs["dst"]], axis=1))}
    arrays.update({name: np.ascontiguousarray(inputs[name]) for name in INPUTS})
    given = {name: nc.dram_tensor(f"in_{name}", array.shape, mybir.dt.from_np(array.dtype), kind="ExternalInput").ap()
             for name, array in arrays.items()}
    out = nc.dram_tensor("out", (N, F), F32, kind="ExternalOutput").ap()
    build(nc, given, out)
    result = run(nc, [{f"in_{name}": array for name, array in arrays.items()}], core_ids=[0])
    return result.results[0]["out"]
```
